# Optimizing a Trainium2 kernel written in Bass

```python
import numpy as np
import jax
import jax.numpy as jnp

def _softmax(x, axis=-1):
    return jax.nn.softmax(x, axis=axis)

def _gelu(x):
    return jax.nn.gelu(x, approximate=True)

def _silu(x):
    return jax.nn.silu(x)

def _sigmoid(x):
    return jax.nn.sigmoid(x)

def _layernorm(x, axis=-1, eps=1e-05):
    m = jnp.mean(x, axis=axis, keepdims=True)
    v = jnp.var(x, axis=axis, keepdims=True)
    return (x - m) / jnp.sqrt(v + eps)

def _scatter_add(tgt, idx, src, axis=0):
    return tgt.at[idx].add(src)

def _segment_sum(src, seg, n):
    return jax.ops.segment_sum(src, seg, n)
kernel_name = 'mk_audio_tower_d1_tok_audfeat1024_r4_ae3162'

def setup_inputs(seed: int=0):
    np.random.seed(seed)
    _w = jnp.asarray

    def _rec_inputs():
        import jax
        import jax.numpy as jnp
        _rk = jax.random.key(seed)
        x = -0.000520686 + 1.00062 * jax.random.normal(jax.random.fold_in(_rk, 1), (16, 2, 4096), jnp.float32)
        return x
    x = _rec_inputs()

    def _L0_tok_setup():
        import jax, jax.numpy as jnp
        import numpy as np
        DS_RATE = 16
        key = jax.random.key(seed)
        ks = jax.random.split(key, 5)
        B, Cin, L = (64, 2, 4096)
        C_mid = 32
        embed_dim = 128
        X = jax.random.normal(ks[0], (B, Cin, L), dtype=jnp.float32)
        W_embed = jax.random.normal(ks[1], (C_mid, Cin, 7), dtype=jnp.float32) * 0.1
        b_embed = jax.random.normal(ks[2], (C_mid,), dtype=jnp.float32) * 0.1
        W_proj = jax.random.normal(ks[3], (embed_dim, C_mid * DS_RATE, 1), dtype=jnp.float32) * 0.05
        b_proj = jax.random.normal(ks[4], (embed_dim,), dtype=jnp.float32) * 0.05
        return {'X': X, 'W_embed': W_embed, 'b_embed': b_embed, 'W_proj': W_proj, 'b_proj': b_proj}
    _L0_tok_all = _L0_tok_setup()
    _L0_tok_in = {k: v for k, v in _L0_tok_all.items() if k in ('W_embed', 'b_embed', 'W_proj', 'b_proj')}
    del _L0_tok_all

    def _L0_attn_setup():
        import jax, jax.numpy as jnp
        import numpy as np
        import math
        B, T, C = (2, 512, 256)
        H, L = (16, 64)
        DH = C // H
        DHE = DH // 2
        THETA = 10000.0

        def _rope_cache(t, dim):
            inv_freq = 1.0 / THETA ** (jnp.arange(0, dim, 2, dtype=jnp.float32) / dim)
            freqs = jnp.arange(t, dtype=jnp.float32)[:, None] * inv_freq[None, :]
            emb = jnp.concatenate((freqs, freqs), axis=-1)
            return (jnp.cos(emb), jnp.sin(emb))

        def _apply_rope(x, cos, sin):
            x1 = x[..., 0::2]
            x2 = x[..., 1::2]
            rot = jnp.stack((-x2, x1), axis=-1).reshape(x.shape)
            return x * cos[None, None] + rot * sin[None, None]
        key = jax.random.key(seed)
        ks = jax.random.split(key, 10)
        s = 0.02
        return {'x': jax.random.normal(ks[0], (B, T, C), jnp.float32), 'Wq_down': jax.random.normal(ks[1], (C, H * L), jnp.float32) * s, 'Wk_down': jax.random.normal(ks[2], (C, H * L), jnp.float32) * s, 'Wv_down': jax.random.normal(ks[3], (C, H * L), jnp.float32) * s, 'Wq_up_c': jax.random.normal(ks[4], (L, DHE), jnp.float32) * s, 'Wq_up_e': jax.random.normal(ks[5], (L, DHE), jnp.float32) * s, 'Wk_up_c': jax.random.normal(ks[6], (L, DHE), jnp.float32) * s, 'Wk_up_e': jax.random.normal(ks[7], (L, DHE), jnp.float32) * s, 'Wv_up': jax.random.normal(ks[8], (L, DH), jnp.float32) * s, 'Wc': jax.random.normal(ks[9], (C, C), jnp.float32) * s}
    _L0_attn_all = _L0_attn_setup()
    _L0_attn_in = {k: v for k, v in _L0_attn_all.items() if k in ('Wq_down', 'Wk_down', 'Wv_down', 'Wq_up_c', 'Wq_up_e', 'Wk_up_c', 'Wk_up_e', 'Wv_up', 'Wc')}
    del _L0_attn_all

    def _L0_ffn_setup():
        import jax, jax.numpy as jnp
        import numpy as np
        B, S, HID, DFF, E, K = (4, 512, 256, 1024, 8, 512)
        key = jax.random.key(seed)
        ks = jax.random.split(key, 4)
        sc_h = 1.0 / np.sqrt(HID)
        sc_f = 1.0 / np.sqrt(DFF)
        return {'x': jax.random.normal(ks[0], (B, S, HID), jnp.float32), 'router_w': jax.random.normal(ks[1], (HID, E), jnp.float32) * sc_h, 'router_b': jnp.zeros((E,), jnp.float32), 'w1': jax.random.normal(ks[2], (E, HID, DFF), jnp.float32) * sc_h, 'b1': jnp.zeros((E, DFF), jnp.float32), 'w2': jax.random.normal(ks[3], (E, DFF, HID), jnp.float32) * sc_f, 'b2': jnp.zeros((E, HID), jnp.float32)}
    _L0_ffn_all = _L0_ffn_setup()
    _L0_ffn_in = {k: v for k, v in _L0_ffn_all.items() if k in ('router_w', 'router_b', 'w1', 'b1', 'w2', 'b2')}
    del _L0_ffn_all
    return {'x': x, 'L0_tok_W_embed': _L0_tok_in['W_embed'], 'L0_tok_b_embed': _L0_tok_in['b_embed'], 'L0_tok_W_proj': _L0_tok_in['W_proj'], 'L0_tok_b_proj': _L0_tok_in['b_proj'], 'L0_attn_Wq_down': _L0_attn_in['Wq_down'], 'L0_attn_Wk_down': _L0_attn_in['Wk_down'], 'L0_attn_Wv_down': _L0_attn_in['Wv_down'], 'L0_attn_Wq_up_c': _L0_attn_in['Wq_up_c'], 'L0_attn_Wq_up_e': _L0_attn_in['Wq_up_e'], 'L0_attn_Wk_up_c': _L0_attn_in['Wk_up_c'], 'L0_attn_Wk_up_e': _L0_attn_in['Wk_up_e'], 'L0_attn_Wv_up': _L0_attn_in['Wv_up'], 'L0_attn_Wc': _L0_attn_in['Wc'], 'L0_ffn_router_w': _L0_ffn_in['router_w'], 'L0_ffn_router_b': _L0_ffn_in['router_b'], 'L0_ffn_w1': _L0_ffn_in['w1'], 'L0_ffn_b1': _L0_ffn_in['b1'], 'L0_ffn_w2': _L0_ffn_in['w2'], 'L0_ffn_b2': _L0_ffn_in['b2']}

def reference(x, L0_tok_W_embed, L0_tok_b_embed, L0_tok_W_proj, L0_tok_b_proj, L0_attn_Wq_down, L0_attn_Wk_down, L0_attn_Wv_down, L0_attn_Wq_up_c, L0_attn_Wq_up_e, L0_attn_Wk_up_c, L0_attn_Wk_up_e, L0_attn_Wv_up, L0_attn_Wc, L0_ffn_router_w, L0_ffn_router_b, L0_ffn_w1, L0_ffn_b1, L0_ffn_w2, L0_ffn_b2):
    import jax
    import jax.numpy as jnp

    def _L0_tok_ref(X, W_embed, b_embed, W_proj, b_proj):
        import jax, jax.numpy as jnp
        import numpy as np
        DS_RATE = 16
        ds = DS_RATE
        h = jax.lax.conv_general_dilated(X, W_embed, window_strides=(1,), padding=((3, 3),), dimension_numbers=('NCH', 'OIH', 'NCH'))
        h = h + b_embed[None, :, None]
        B, C, L = h.shape
        Ld = L // ds
        h = h.reshape(B, C, Ld, ds).transpose(0, 3, 1, 2).reshape(B, ds * C, Ld)
        out = jnp.einsum('oc,bcl->bol', W_proj[:, :, 0], h) + b_proj[None, :, None]
        return out

    def _L0_attn_ref(x, Wq_down, Wk_down, Wv_down, Wq_up_c, Wq_up_e, Wk_up_c, Wk_up_e, Wv_up, Wc):
        import jax, jax.numpy as jnp
        import numpy as np
        import math
        B, T, C = (2, 512, 256)
        H, L = (16, 64)
        DH = C // H
        DHE = DH // 2
        THETA = 10000.0

        def _rope_cache(t, dim):
            inv_freq = 1.0 / THETA ** (jnp.arange(0, dim, 2, dtype=jnp.float32) / dim)
            freqs = jnp.arange(t, dtype=jnp.float32)[:, None] * inv_freq[None, :]
            emb = jnp.concatenate((freqs, freqs), axis=-1)
            return (jnp.cos(emb), jnp.sin(emb))

        def _apply_rope(x, cos, sin):
            x1 = x[..., 0::2]
            x2 = x[..., 1::2]
            rot = jnp.stack((-x2, x1), axis=-1).reshape(x.shape)
            return x * cos[None, None] + rot * sin[None, None]
        b, t, c = x.shape
        q_lat = (x @ Wq_down).reshape(b, t, H, L)
        k_lat = (x @ Wk_down).reshape(b, t, H, L)
        v_lat = (x @ Wv_down).reshape(b, t, H, L)
        q_c = jnp.einsum('bthl,ld->bhtd', q_lat, Wq_up_c)
        q_e = jnp.einsum('bthl,ld->bhtd', q_lat, Wq_up_e)
        k_c = jnp.einsum('bthl,ld->bhtd', k_lat, Wk_up_c)
        k_e = jnp.einsum('bthl,ld->bhtd', k_lat, Wk_up_e)
        v = jnp.einsum('bthl,ld->bhtd', v_lat, Wv_up)
        cos, sin = _rope_cache(t, DHE)
        q = jnp.concatenate([q_c, _apply_rope(q_e, cos, sin)], axis=-1)
        k = jnp.concatenate([k_c, _apply_rope(k_e, cos, sin)], axis=-1)
        scale = 1.0 / math.sqrt(DH)
        scores = jnp.einsum('bhqd,bhkd->bhqk', q, k) * scale
        causal = jnp.tril(jnp.ones((t, t), dtype=bool))
        scores = jnp.where(causal[None, None], scores, -jnp.inf)
        att = jax.nn.softmax(scores, axis=-1)
        y = jnp.einsum('bhqk,bhkd->bhqd', att, v)
        y = y.transpose(0, 2, 1, 3).reshape(b, t, c)
        return y @ Wc

    def _L0_ffn_ref(x, router_w, router_b, w1, b1, w2, b2):
        import jax, jax.numpy as jnp
        import numpy as np
        B, S, HID, DFF, E, K = (4, 512, 256, 1024, 8, 512)
        b, s, h = x.shape
        xf = x.reshape(-1, h)
        logits = xf @ router_w + router_b
        scores = jax.nn.softmax(logits, axis=-1)
        G, idx = jax.lax.top_k(scores.T, K)
        toks = xf[idx]
        h1 = jax.nn.relu(jnp.einsum('ekh,ehf->ekf', toks, w1) + b1[:, None, :])
        eo = jnp.einsum('ekf,efh->ekh', h1, w2) + b2[:, None, :]
        contrib = (eo * G[..., None]).reshape(-1, h)
        y = jnp.zeros_like(xf).at[idx.reshape(-1)].add(contrib)
        return y.reshape(b, s, h)
    h = _L0_tok_ref(x, L0_tok_W_embed, L0_tok_b_embed, L0_tok_W_proj, L0_tok_b_proj)
    h = h + _L0_attn_ref(_layernorm(h, axis=-1), L0_attn_Wq_down, L0_attn_Wk_down, L0_attn_Wv_down, L0_attn_Wq_up_c, L0_attn_Wq_up_e, L0_attn_Wk_up_c, L0_attn_Wk_up_e, L0_attn_Wv_up, L0_attn_Wc)
    h = h + _L0_ffn_ref(_layernorm(h, axis=-1), L0_ffn_router_w, L0_ffn_router_b, L0_ffn_w1, L0_ffn_b1, L0_ffn_w2, L0_ffn_b2)
    return h

_drawn_inputs = setup_inputs


def setup_inputs(seed=0):
    import zlib

    import numpy as np

    out = dict(_drawn_inputs(seed))
    spreads = {'L0_ffn_router_b': (0.0, 0.1), 'L0_ffn_b1': (0.0, 0.1), 'L0_ffn_b2': (0.0, 0.1)}
    factors = {'L0_attn_Wq_down': 8.0,
     'L0_attn_Wk_down': 8.0,
     'L0_attn_Wq_up_c': 8.0,
     'L0_attn_Wq_up_e': 8.0,
     'L0_attn_Wk_up_c': 8.0,
     'L0_attn_Wk_up_e': 8.0}
    for name, (base, spread) in spreads.items():
        noise = np.random.default_rng([zlib.crc32(name.encode()), seed]).standard_normal(out[name].shape)
        drawn = base * np.exp(spread * noise) if base else spread * noise
        out[name] = jnp.asarray(drawn.astype(out[name].dtype))
    for name, factor in factors.items():
        out[name] = (out[name] * factor).astype(out[name].dtype)
    return out
```

```python
from contextlib import ExitStack

import numpy as np

import concourse.bass as bass
from concourse import mybir

F32 = mybir.dt.float32
F16 = mybir.dt.float16
BF16 = mybir.dt.bfloat16
I32 = mybir.dt.int32
U32 = mybir.dt.uint32
ALU = mybir.AluOpType
ACT = mybir.ActivationFunctionType
AX = mybir.AxisListType

P = 128
NB, T, C = 16, 128, 256
H, L, DH = 16, 64, 16
DE = DH // 2
CIN, TAPS, DS, CMID = 2, 7, 16, 32
WIN = DS + TAPS - 1
KWIN = CIN * WIN
KX = KWIN + 2
E, FF, CAP = 8, 1024, 512
FT, CT, ST = FF // P, C // P, CAP // P
SLOT, HP = 64, H // 2
GROUP = 3
CANDS = 2 ** GROUP - 1
ROUNDS = 10
ROW = C + E
EPS = 1e-5
SEED, NEWTON = float(0x5F3759DF), 3
QUARTERS = 4
WSCALE = 64.0
MASKED = -1e30


def at(base, n):
    return max(base + n, 0) if isinstance(base, int) else base + n if n else base


def build(nc, a, out, table):
    with ExitStack() as ctx:
        def sb(name, shape, dt=F32):
            return ctx.enter_context(nc.sbuf_tensor(name, shape, dt))

        def sem(name):
            return ctx.enter_context(nc.semaphore(name))

        front = ctx.enter_context(nc.psum_tensor("front", [P, 512], F32))
        qk_ps = ctx.enter_context(nc.psum_tensor("qk_ps", [P, 512], F32))
        v_ps = ctx.enter_context(nc.psum_tensor("v_ps", [P, 512], F32))
        ring = [ctx.enter_context(nc.psum_tensor(f"ring{i}", [P, 1024], F32)) for i in range(2)]
        tail = ctx.enter_context(nc.psum_tensor("tail", [P, 512], F32))
        mT_ps = v_ps[:, 256:320].bitcast(BF16)

        ident = sb("ident", [P, P])
        ident_bf = sb("ident_bf", [P, P], BF16)
        ident_h = sb("ident_h", [P, P], F16)
        mask_qk = sb("mask_qk", [P, P], BF16)
        mask_kq = sb("mask_kq", [P, P], BF16)
        pick = sb("pick", [P, H, P], BF16)
        raw = sb("raw", [P, 3, P])
        cos_t = sb("cos_t", [P, 2 * H, DE])
        sin_t = sb("sin_t", [P, 2 * H, DE])
        lower = sb("lower", [P, P], BF16)
        ones_bf = sb("ones_bf", [P, P], BF16)
        iota_lo = sb("iota_lo", [P, P], F16)
        iota_hi = sb("iota_hi", [P, ST], F16)
        tok_id = sb("tok_id", [P, NB])
        seg = sb("seg", [P, E, NB])
        bits = sb("bits", [P, ROUNDS + 1, CANDS, E], I32)
        xwin = sb("xwin", [P, NB * C])
        band = sb("band", [P, 4, KWIN + 1])
        wpT = sb("wpT", [P, 4, P])
        weffT = sb("weffT", [64, P])
        up = sb("up", [P, 3, 2 * DH])
        stage = sb("stage", [P, 24 * C])
        wdT = stage[:, :].rearrange("p (j c) -> p j c", c=C)
        wqkv = sb("wqkv", [P, CT, 3 * C])
        wc = sb("wc", [P, CT, C])
        wr = sb("wr", [P, CT, E])
        rb = sb("rb", [P, E])
        b1 = sb("b1", [P, E, FT])
        b2 = sb("b2", [P, E, C])

        resid = sb("resid", [P, NB, C])
        scores = sb("scores", [P, E, NB])
        st6 = sb("st6", [P, NB, 6])
        mv = sb("mv", [P, NB, 2])
        var = sb("var", [P, NB])
        rstd = sb("rstd", [P, NB])
        newton = sb("newton", [P, NB])
        xhat = sb("xhat", [P, C])
        xT = sb("xT", [P, CT, P])
        qk = sb("qk", [P, 2 * H, DH])
        parts = sb("parts", [P, 2 * H, SLOT], F16)
        rot1 = sb("rot1", [P, 2 * H, DE])
        rot2 = sb("rot2", [P, 2 * H, DE])
        qT = [sb(f"qT{i}", [P, HP, P], F16) for i in range(2)]
        kT = [sb(f"kT{i}", [P, HP, 2, P], F16) for i in range(2)]
        vx = [sb(f"vx{i}", [P, H, P]) for i in range(2)]
        negmax = sb("negmax", [P, H])
        mst = sb("mst", [P, P], BF16)
        mT = sb("mT", [P, P], BF16)
        pT = sb("pT", [P, H, P])
        ysb = sb("ysb", [P, 4, P])
        rden = sb("rden", [P, H])
        yn = sb("yn", [P, H, DH])
        ynT = sb("ynT", [P, CT, P])
        x2 = [sb(f"x2_{i}", [P, C]) for i in range(2)]
        x2T = [sb(f"x2T{i}", [P, CT, P]) for i in range(2)]
        rows = sb("rows", [P, NB, ROW])
        lg = sb("lg", [P, NB, E])
        lmax = sb("lmax", [P, NB])
        lsum = sb("lsum", [P, NB])

        thr = sb("thr", [P, E], I32)
        cand = sb("cand", [P, CANDS, E], I32)
        reach = sb("reach", [P, NB, CANDS, E], BF16)
        gain = sb("gain", [P, CANDS, E])
        take = sb("take", [P, E], I32)
        above = sb("above", [P, E, NB], BF16)
        eq = sb("eq", [P, E, NB], BF16)
        cnt = sb("cnt", [P, E])
        need = sb("need", [P, E])
        incl = sb("incl", [P, E, NB])
        tot_sb = sb("tot_sb", [P, E, NB])
        rank = sb("rank", [P, E, NB])
        sel = sb("sel", [P, E, NB], BF16)
        slot = sb("slot", [P, E, NB], I32)
        slot_lo_i = sb("slot_lo_i", [P, E, NB], I32)
        slot_hi_i = sb("slot_hi_i", [P, E, NB], I32)
        slot_lo = sb("slot_lo", [P, E, NB], F16)
        slot_hi = sb("slot_hi", [P, E, NB])
        hot_hi = sb("hot_hi", [P, E * NB, ST], F16)
        hot_lo = [sb(f"hot_lo{i}", [P, NB, P], F16) for i in range(2)]
        token_of = sb("token_of", [P, E, ST], U32)

        w1s = stage[:, 0:2048].rearrange("p (k f) -> p k f", k=CT)
        w2s = stage[:, 2048:4096].rearrange("p (f c) -> p f c", f=FT)
        wh = [sb("wh0", [P, 4, 2048], F16)]
        wh.append(vx[0][:, :, :].rearrange("p h q -> p (h q)").bitcast(F16))
        wh.append(vx[1][:, :, :].rearrange("p h q -> p (h q)").bitcast(F16))
        W = [[wh[0][:, i, :] for i in range(4)],
             [wh[1][:, 0:2048], wh[1][:, 2048:4096], wh[2][:, 0:2048], wh[2][:, 2048:4096]]]
        W1 = [[w.rearrange("p (k f) -> p k f", k=CT) for w in W[i][0:2]] for i in range(2)]
        W2 = [[w.rearrange("p (f c) -> p f c", f=FT) for w in W[i][2:4]] for i in range(2)]
        hid_all = xwin[:, :].bitcast(F16).rearrange("p (i f s) -> p i f s", i=2, f=FT)
        hid = [hid_all[:, i] for i in range(2)]
        relu = pT[:, :, :].rearrange("p h q -> p (h q)").rearrange("p (i s) -> p i s", i=4)
        got = [sb(f"got{i}", [P, ST, ROW]) for i in range(2)]
        gT = [kT[0][:, 4 * i:4 * i + 4, :, :].rearrange("p i j k -> p (i j k)").rearrange("p (k s) -> p k s", k=CT)
              for i in range(2)]
        tmp = qT[0][:, :, :].rearrange("p i k -> p (i k)").bitcast(F32).rearrange("p (i c) -> p i c", i=2)
        contrib = parts[:, :, :].rearrange("p h s -> p (h s)").bitcast(F32).rearrange("p (t c) -> p t c", t=ST)
        spare_ve = sb("spare_ve", [1, 1])
        spare_sc = sb("spare_sc", [1, 1])
        b1e = [sb(f"b1e{i}", [P, FT]) for i in range(2)]

        bias_ready = sem("bias_ready")
        ld_const = sem("ld_const")
        ld_w = sem("ld_w")
        ld_x = sem("ld_x")
        ld_bias = sem("ld_bias")
        pre_mem = sem("pre_mem")
        zeroed = sem("zeroed")
        weff_ready = sem("weff_ready")
        weff_saved = sem("weff_saved")
        bp_in = sem("bp_in")
        eff_ready = sem("eff_ready")
        eff_saved = sem("eff_saved")
        bf_ready = sem("bf_ready")
        conv_ready = sem("conv_ready")
        h_saved = sem("h_saved")
        s_stats = sem("s_stats")
        s_stats2 = sem("s_stats2")
        s_root = sem("s_root")
        xhat_ready = sem("xhat_ready")
        xhatT_ready = sem("xhatT_ready")
        xhatT_saved = sem("xhatT_saved")
        qkv_ready = sem("qkv_ready")
        qkc_saved = sem("qkc_saved")
        v_saved = sem("v_saved")
        s_rot1 = sem("s_rot1")
        s_rot2 = sem("s_rot2")
        rope_done = sem("rope_done")
        q_hi = sem("q_hi")
        k_hi = sem("k_hi")
        q_lo = sem("q_lo")
        parts_ready = sem("parts_ready")
        qkT_ready = sem("qkT_ready")
        kT_even_saved = sem("kT_even_saved")
        kT_odd_saved = sem("kT_odd_saved")
        qT_saved = sem("qT_saved")
        s_mhi = sem("s_mhi")
        mst_ready = sem("mst_ready")
        mT_ready = sem("mT_ready")
        mT_saved = sem("mT_saved")
        pv_done = sem("pv_done")
        y_saved = sem("y_saved")
        ytok_ready = sem("ytok_ready")
        s_rden = sem("s_rden")
        yn_ready = sem("yn_ready")
        ynT_ready = sem("ynT_ready")
        ynT_saved = sem("ynT_saved")
        attn_ready = sem("attn_ready")
        h2_ready = sem("h2_ready")
        x2_ready = sem("x2_ready")
        x2T_ready = sem("x2T_ready")
        x2T_saved = sem("x2T_saved")
        logits_ready = sem("logits_ready")
        s_logits = sem("s_logits")
        logits_shifted = sem("logits_shifted")
        exp_logits_done = sem("exp_logits_done")
        scores_ready = sem("scores_ready")
        table_in = sem("table_in")
        resid_out = sem("resid_out")
        s_cmp = sem("s_cmp")
        s_count = sem("s_count")
        s_gain = sem("s_gain")
        s_take = sem("s_take")
        s_cand = sem("s_cand")
        s_thr = sem("s_thr")
        s_tie = sem("s_tie")
        s_tied = sem("s_tied")
        s_chosen = sem("s_chosen")
        s_prefix = sem("s_prefix")
        s_chain = sem("s_chain")
        slots_ready = sem("slots_ready")
        hot_ready = sem("hot_ready")
        list_ready = sem("list_ready")
        list_saved = sem("list_saved")
        w1_in = sem("w1_in")
        w2_in = sem("w2_in")
        wsplit_hi = sem("wsplit_hi")
        wsplit_lo = sem("wsplit_lo")
        got_in = sem("got_in")
        gT_ready = sem("gT_ready")
        gT_hi = sem("gT_hi")
        gT_lo = sem("gT_lo")
        h1_ready = sem("h1_ready")
        relu_done = sem("relu_done")
        hid_hi = sem("hid_hi")
        hid_lo = sem("hid_lo")
        eo_ready = sem("eo_ready")
        s_eo = sem("s_eo")
        contrib_ready = sem("contrib_ready")
        added = sem("added")
        S_ready = [sem("S_ready_lo"), sem("S_ready_hi")]
        T_ready = [sem("T_ready_lo"), sem("T_ready_hi")]
        row_maxed = [sem("row_maxed_lo"), sem("row_maxed_hi")]
        exp_done = [sem("exp_done_lo"), sem("exp_done_hi")]

        def take_wait(e, spare):
            e.tensor_tensor(spare, spare, spare, ALU.mult)

        out_rows = out.rearrange("b t c -> (b t) c")

        def flat(t):
            return t.rearrange("p a b -> p (a b)")

        blk = ctx.enter_context(nc.Block())

        @blk.sync
        def _(sp):
            def ld(dst, src, done):
                sp.dma_start(dst, src).then_inc(done, 16)

            ld(band[:, :, :], a["band"].rearrange("(s p) j -> p s j", p=P), ld_w)
            ld(wpT[:, :, :], a["wpT"].rearrange("(s p) o -> p s o", p=P), ld_w)
            ld(wdT, a["wdT"].rearrange("(j p) c -> p j c", p=P), ld_w)
            ld(up[:, :, :], a["up"].rearrange("j p d -> p j d"), ld_w)
            sp.wait_ge(pre_mem, 1)
            ld(xwin[0:KWIN, :], a["xwin"], ld_x)
            for dst, n in [(ident[:, :], "ident"), (raw[:, 0, :], "mask_qk"), (raw[:, 1, :], "mask_kq"),
                           (raw[:, 2, :], "lower"),
                           (flat(cos_t[:, :, :]), "cos"), (flat(sin_t[:, :, :]), "sin"),
                           (iota_lo[:, :], "iota_lo"), (iota_hi[:, :], "iota_hi"), (tok_id[:, :], "tok_id"),
                           (flat(seg[:, :, :]), "seg"), (bits[:, :, :, :].rearrange("p r j e -> p (r j e)"), "bits")]:
                ld(dst, a[n], ld_const)
            ld(wc[:, :, :], a["wc"].rearrange("(k p) c -> p k c", p=P), ld_const)
            ld(wr[:, :, :], a["wr"].rearrange("(k p) e -> p k e", p=P), ld_const)
            ld(rb[:, :], a["rb"].partition_broadcast(P), ld_const)
            ld(flat(b1[:, :, :]), a["b1"], ld_bias)
            ld(b2[:, :, :], a["b2"].partition_broadcast(P), ld_bias)
            sp.wait_ge(weff_saved, 1)
            ld(weffT[KX - 1:KX, :], a["bp"].rearrange("(a o) -> a o", a=1), bp_in)

            sp.wait_ge(eff_ready, 1)
            sp.dma_start(w1s, a["w1"][0].rearrange("(k p) f -> p k f", p=P)).then_inc(w1_in, 16)
            sp.dma_start(w2s, a["w2"][0].rearrange("(f p) c -> p f c", p=P)).then_inc(w2_in, 16)
            with sp.Fori(0, NB) as b:
                sp.wait_ge(h2_ready, at(b, 1))
                sp.dma_start(out_rows[bass.ds(b * P, P), :], resid[:, bass.ds(b, 1), :]).then_inc(resid_out, 16)
            sp.wait_ge(scores_ready, 1)
            sp.dma_start(table.rearrange("(b p) r -> p b r", p=P), rows[:, :, :]).then_inc(table_in, 16)

            def weights(e):
                sp.wait_ge(wsplit_lo, e * QUARTERS)
                sp.dma_start(w1s, a["w1"][bass.ds(e, 1)].rearrange("a (k p) f -> p (a k) f", p=P)).then_inc(w1_in, 16)
                sp.dma_start(w2s, a["w2"][bass.ds(e, 1)].rearrange("a (f p) c -> p (a f) c", p=P)).then_inc(w2_in, 16)

            with sp.Fori(1, E) as e:
                weights(e)
            sp.wait_ge(resid_out, 16 * NB)
            sp.wait_ge(table_in, 16)
            sp.wait_ge(added, 16 * ST * E)

        @blk.tensor
        def _(pe):
            mm, tr = pe.matmul, pe.transpose

            pe.wait_ge(ld_w, 64)
            for i in range(4):
                x = mm(front[0:KWIN + 1, 0:P], band[:, i, :], wpT[:, i, :], start=i == 0, stop=i == 3)
            x.then_inc(weff_ready, 1)
            for j in range(3):
                for k in range(CT):
                    g = j * CT + k
                    o = ring[g // 4][:, (g % 4) * C:(g % 4 + 1) * C]
                    for i in range(8):
                        x = mm(o[:, 32 * i:32 * i + 32], wdT[:, 8 * j + i, k * P:(k + 1) * P], up[:, j, :],
                               start=True, stop=True)
            x.then_inc(eff_ready, 1)
            pe.wait_ge(ld_const, 16 * 14)
            pe.wait_ge(bf_ready, 1)
            pe.wait_ge(ld_x, 16)
            pe.wait_ge(bp_in, 16)
            pe.wait_ge(eff_saved, 1)

            def conv(b, p):
                pe.wait_ge(h_saved, at(b, -1))
                mm((front, qk_ps)[p][:, 0:C], weffT[0:KX, :], xwin[0:KX, bass.ds(b * C, C)],
                   start=True, stop=True).then_inc(conv_ready, 1)

            def xhat_t(b):
                pe.wait_ge(xhat_ready, at(b, 1))
                pe.wait_ge(qT_saved, b)
                for k in range(CT):
                    x = tr(front[:, k * P:(k + 1) * P], xhat[:, k * P:(k + 1) * P], ident[:, :])
                x.then_inc(xhatT_ready, 1)

            def qkv(b):
                pe.wait_ge(xhatT_saved, at(b, 1))
                pe.wait_ge(kT_even_saved, b)
                pe.wait_ge(kT_odd_saved, b)
                pe.wait_ge(v_saved, b)
                for k in range(CT):
                    mm(qk_ps[:, :], xT[:, k, :], wqkv[:, k, 0:2 * C], start=k == 0, stop=k == CT - 1)
                pe.wait_ge(mT_saved, b)
                for k in range(CT):
                    x = mm(v_ps[:, 0:C], xT[:, k, :], wqkv[:, k, 2 * C:], start=k == 0, stop=k == CT - 1)
                x.then_inc(qkv_ready, 1)

            def qk_t(b):
                pe.wait_ge(parts_ready, at(b, 1))
                pe.wait_ge(q_lo, at(b, 1))
                split = flat(parts[:, :, :])
                for bank, first in ((front, 0), (qk_ps, HP)):
                    o = bank[:, :].bitcast(F16)
                    for i in range(HP):
                        x = tr(o[:, i * P:(i + 1) * P], split[:, (first + i) * P:(first + i + 1) * P], ident_h[:, :])
                x.then_inc(qkT_ready, 1)

            def scores_for_max(b, p, half):
                pe.wait_ge(exp_done[half], b)
                if not half:
                    pe.wait_ge(kT_even_saved, at(b, 1))
                    pe.wait_ge(kT_odd_saved, at(b, 1))
                    pe.wait_ge(qT_saved, at(b, 1))
                for c in range(2):
                    o = ring[half][:, c * 512:(c + 1) * 512]
                    for j in range(2):
                        i = 4 * half + 2 * c + j
                        mm(o[:, j * 2 * P:(j + 1) * 2 * P], qT[p][:, i, :], flat(kT[p][:, i, :, :]),
                           start=j == 0, stop=False, skip_group_check=True)
                    x = mm(o.rearrange("q (h k) -> q h k", h=4), ident_bf[:, :],
                           mask_qk[:, :].unsqueeze(1).to_broadcast([P, 4, P]), start=False, stop=True,
                           skip_group_check=True)
                x.then_inc(S_ready[half], 1)

            def max_t(b):
                pe.wait_ge(mst_ready, at(b, 1))
                pe.wait_ge(v_saved, at(b, 1))
                tr(mT_ps, mst[:, :], ident_bf[:, :]).then_inc(mT_ready, 1)

            def scores_t(b, p, half):
                if not half:
                    pe.wait_ge(mT_saved, at(b, 1))
                pe.wait_ge(row_maxed[half], at(b, 1))
                for c in range(2):
                    o = ring[half][:, c * 512:(c + 1) * 512]
                    for j in range(4):
                        i = 4 * half + 2 * c + j // 2
                        mm(o[:, j * P:(j + 1) * P], kT[p][:, i, j % 2, :], qT[p][:, i, :],
                           start=j == 0, stop=False, skip_group_check=True)
                    for j in range(4):
                        mm(o[:, j * P:(j + 1) * P], pick[:, 8 * half + 4 * c + j, :], mT[:, :],
                           start=False, stop=False, skip_group_check=True)
                    x = mm(o.rearrange("q (h k) -> q h k", h=4), ident_bf[:, :],
                           mask_kq[:, :].unsqueeze(1).to_broadcast([P, 4, P]), start=False, stop=True,
                           skip_group_check=True)
                x.then_inc(T_ready[half], 1)

            def values(b, p, half):
                if half:
                    pe.wait_ge(exp_done[1], at(b, 1))
                else:
                    pe.wait_ge(exp_done[0], at(b, 1))
                    pe.wait_ge(v_saved, at(b, 1))
                    pe.wait_ge(h2_ready, b)
                for g in (0, 1) if not half else (2, 3):
                    for j in range(4):
                        x = mm(tail[:, g * P:(g + 1) * P], vx[p][:, 4 * g + j, :], pT[:, 4 * g + j, :],
                               start=j == 0, stop=j == 3)
                if half:
                    x.then_inc(pv_done, 1)

            def y_tok(b):
                pe.wait_ge(y_saved, at(b, 1))
                for g in range(4):
                    x = tr(tail[:, g * P:(g + 1) * P], ysb[:, g, :], ident[:, :])
                x.then_inc(ytok_ready, 1)

            def yn_t(b):
                pe.wait_ge(yn_ready, at(b, 1))
                ynf = flat(yn[:, :, :])
                for k in range(CT):
                    x = tr(tail[:, k * P:(k + 1) * P], ynf[:, k * P:(k + 1) * P], ident[:, :])
                x.then_inc(ynT_ready, 1)

            def out_proj(b):
                pe.wait_ge(ynT_saved, at(b, 1))
                for k in range(CT):
                    x = mm(tail[:, C:2 * C], ynT[:, k, :], wc[:, k, :], start=k == 0, stop=k == CT - 1)
                x.then_inc(attn_ready, 1)

            def x2_t(b, p):
                pe.wait_ge(x2_ready, at(b, 1))
                pe.wait_ge(x2T_saved, at(b, -1))
                for k in range(CT):
                    x = tr((front, qk_ps)[p][:, k * P:(k + 1) * P], x2[p][:, k * P:(k + 1) * P], ident[:, :])
                x.then_inc(x2T_ready, 1)

            def router(b, p):
                pe.wait_ge(x2T_saved, at(b, 1))
                for k in range(CT):
                    x = mm(v_ps[:, bass.ds(b * E, E)], x2T[p][:, k, :], wr[:, k, :], start=k == 0, stop=k == CT - 1)
                x.then_inc(logits_ready, 1)

            def step(b, p, has_front=True, has_tail=True):
                n, o = at(b, 1), at(b, -1)
                scores_for_max(b, p, 0)
                if has_tail:
                    y_tok(o)
                scores_for_max(b, p, 1)
                if has_front:
                    xhat_t(n)
                if has_tail:
                    yn_t(o)
                max_t(b)
                if has_front:
                    qkv(n)
                scores_t(b, p, 0)
                if has_tail:
                    out_proj(o)
                scores_t(b, p, 1)
                values(b, p, 0)
                if has_front:
                    qk_t(n)
                values(b, p, 1)

            conv(0, 0)
            conv(1, 1)
            with pe.Fori(2, NB - 1, 2) as b:
                conv(b, 0)
                conv(b + 1, 1)
            pe.wait_ge(h_saved, NB)
            xhat_t(0)
            qkv(0)
            qk_t(0)
            step(0, 0, has_tail=False)
            step(1, 1)
            with pe.Fori(2, NB - 3, 2) as b:
                step(b, 0)
                step(b + 1, 1)
            step(NB - 2, 0)
            step(NB - 1, 1, has_front=False)
            y_tok(NB - 1)
            yn_t(NB - 1)
            out_proj(NB - 1)

            x2_t(0, 0)
            x2_t(1, 1)
            router(0, 0)
            with pe.Fori(2, NB - 1, 2) as b:
                x2_t(b, 0)
                router(b - 1, 1)
                x2_t(b + 1, 1)
                router(b, 0)
            router(NB - 1, 1)

            with pe.Fori(0, ROUNDS) as i:
                pe.wait_ge(s_cmp, at(i, 1))
                for b in range(NB):
                    x = mm(front[:, 0:CANDS * E], ones_bf[:, :], flat(reach[:, b, :, :]), start=b == 0, stop=b == NB - 1)
                x.then_inc(s_count, 1)
            pe.wait_ge(s_tie, 1)
            mm(front[:, 0:P], ones_bf[:, :], flat(above[:, :, :]), start=True, stop=True)
            mm(front[:, P:2 * P], ones_bf[:, :], flat(eq[:, :, :]), start=True, stop=True)
            mm(front[:, 2 * P:3 * P], lower[:, :], flat(eq[:, :, :]), start=True, stop=True).then_inc(s_tied, 1)
            pe.wait_ge(s_chosen, 1)
            mm(qk_ps[:, 0:P], ones_bf[:, :], flat(sel[:, :, :]), start=True, stop=True)
            mm(qk_ps[:, P:2 * P], lower[:, :], flat(sel[:, :, :]), start=True, stop=True).then_inc(s_prefix, 1)
            for e in range(E):
                pe.wait_ge(hot_ready, e + 1)
                pe.wait_ge(list_saved, at(e, -1))
                for b in range(NB):
                    x = mm((front, qk_ps)[e % 2][:, 0:ST], hot_lo[e % 2][:, b, :], hot_hi[:, e * NB + b, :],
                           start=b == 0, stop=b == NB - 1)
                x.then_inc(list_ready, 1)

            def transpose_rows(e, p):
                pe.wait_ge(got_in, at(e * 64, 64))
                for k in range(CT):
                    pe.wait_ge(gT_lo, at(e * CT, k - 1) if k else e * CT)
                    for t in range(ST):
                        x = tr((tail if k else v_ps)[:, t * P:(t + 1) * P], got[p][:, t, k * P:(k + 1) * P], ident[:, :])
                    x.then_inc(gT_ready, 1)

            def hidden(e, p, f):
                if f == 0:
                    pe.wait_ge(gT_lo, at(e * CT, CT))
                    pe.wait_ge(wsplit_lo, at(e * QUARTERS, QUARTERS))
                pe.wait_ge(hid_hi, at(e * FT, f - 3))
                o = ring[f % 4 // 2][:, (f % 2) * 512:(f % 2 + 1) * 512]
                terms = [(i, j, k) for i, j in ((0, 0), (0, 1), (1, 0)) for k in range(CT)]
                for n, (i, j, k) in enumerate(terms):
                    x = mm(o, W1[p][i][:, k, f * P:(f + 1) * P], gT[j][:, k, :], start=n == 0, stop=n == len(terms) - 1)
                x.then_inc(h1_ready, 1)

            def expert_out(e, p, t):
                if t == 0:
                    pe.wait_ge(hid_hi, at(e * FT, FT))
                    pe.wait_ge(list_saved, E)
                pe.wait_ge(s_eo, at(e * ST, t - 1))
                o = (front, qk_ps)[t % 2][:, 0:C]
                terms = [(i, j, f) for i, j in ((0, 0), (0, 1), (1, 0)) for f in range(FT)]
                for n, (i, j, f) in enumerate(terms):
                    if t == 0 and n == 2 * FT:
                        pe.wait_ge(hid_lo, at(e * FT, FT))
                    x = mm(o, hid[i][:, f, t * P:(t + 1) * P], W2[p][j][:, f, :], start=n == 0, stop=n == len(terms) - 1)
                x.then_inc(eo_ready, 1)

            def expert(e, p, last=False):
                for f in range(FT):
                    hidden(e, p, f)
                if not last:
                    transpose_rows(at(e, 1), 1 - p)
                for t in range(ST):
                    expert_out(e, p, t)

            transpose_rows(0, 0)
            expert(0, 0)
            expert(1, 1)
            with pe.Fori(2, E - 3, 2) as e:
                expert(e, 0)
                expert(e + 1, 1)
            expert(E - 2, 0)
            expert(E - 1, 1, last=True)

        @blk.vector
        def _(ve):
            tt, ts, cp = ve.tensor_tensor, ve.tensor_scalar, ve.tensor_copy
            ve.memset(xwin[:, :], 1.0).then_inc(pre_mem, 1)
            ve.memset(spare_sc[:, :], 0.0).then_inc(pre_mem, 1)
            for i in range(2):
                ve.memset(flat(vx[i][:, :, :]), 0.0)
                ve.memset(kT[i][:, :, :, :].rearrange("p i j k -> p (i j k)").bitcast(F32), 0.0)
            ve.memset(flat(parts[:, :, :]).bitcast(F32), 0.0)
            ve.memset(mst[:, :], 0.0)
            ve.memset(spare_ve[:, :], 0.0)
            ve.memset(ones_bf[:, :], 1.0).then_inc(zeroed, 1)
            ve.wait_ge(zeroed, 1)
            for i in range(2):
                for j in range(4):
                    x = ve.memset(bass.AP(vx[i], j * 160 + DH, [[H * P, P], [512, 4]]), 1.0)
            x.then_inc(zeroed, 1)
            ve.wait_ge(weff_ready, 1)
            cp(weffT[0:KWIN + 1, :], front[0:KWIN + 1, 0:P]).then_inc(weff_saved, 1)
            ve.wait_ge(eff_ready, 1)
            for j in range(3):
                for k in range(CT):
                    g = j * CT + k
                    x = ts(wqkv[:, k, j * C:(j + 1) * C], ring[g // 4][:, (g % 4) * C:(g % 4 + 1) * C],
                           DH ** -0.5 if j == 0 else 1.0, None, ALU.mult)
            x.then_inc(eff_saved, 1)
            ve.wait_ge(ld_const, 16 * 14)
            for i, dst in enumerate((mask_qk, mask_kq, lower)):
                cp(dst[:, :], raw[:, i, :])
            cp(ident_bf[:, :], ident[:, :])
            cp(ident_h[:, :], ident[:, :])
            tt(pick[:, :, :], ident[:, 0:H].unsqueeze(2).to_broadcast([P, H, P]),
               ident[:, H:2 * H].unsqueeze(2).to_broadcast([P, H, P]), ALU.add).then_inc(bf_ready, 1)

            def feat(b):
                return resid[:, bass.ds(b, 1), :].rearrange("p a c -> p (a c)")

            def stats(b, done):
                ve.wait_ge(done, b)
                take_wait(ve, spare_ve[:, :])
                ve.bn_stats(st6[:, bass.ds(b, 1), :].rearrange("p a s -> p (a s)"), feat(b)).then_inc(done, 1)

            def inverse_roots(first):
                count = [first]

                def after(x):
                    count[0] += 1
                    x.then_inc(s_root, 1)
                    ve.wait_ge(s_root, count[0])

                for b in range(NB):
                    x = ve.bn_aggr(mv[:, b, :], st6[:, b, :])
                after(x)
                after(ts(var[:, :], mv[:, :, 1], EPS, None, ALU.add))
                after(ts(rstd[:, :].bitcast(I32), var[:, :].bitcast(I32), -0.5, SEED, ALU.mult, ALU.add))
                for _ in range(NEWTON):
                    after(tt(newton[:, :], rstd[:, :], rstd[:, :], ALU.mult))
                    after(tt(newton[:, :], newton[:, :], var[:, :], ALU.mult))
                    after(ts(newton[:, :], newton[:, :], -0.5, 1.5, ALU.mult, ALU.add))
                    after(tt(rstd[:, :], rstd[:, :], newton[:, :], ALU.mult))
                return count[0]

            def normalise(b, dst):
                return ts(dst, feat(b), mv[:, bass.ds(b, 1), 0:1].rearrange("p a s -> p (a s)"),
                          rstd[:, bass.ds(b, 1)], ALU.subtract, ALU.mult)

            def norm1(b):
                ve.wait_ge(xhatT_ready, b)
                normalise(b, xhat[:, :]).then_inc(xhat_ready, 1)

            def rope(b):
                ve.wait_ge(qkc_saved, at(b, 1))
                rot = qk_ps[:, :].rearrange("p (h d) -> p h d", d=DH)[:, :, DE:]
                tt(rot1[:, :, :], rot, cos_t[:, :, :], ALU.mult).then_inc(s_rot1, 1)
                for i in range(2):
                    x = tt(rot2[:, :, i::2], rot[:, :, 1 - i::2], sin_t[:, :, i::2], ALU.mult)
                x.then_inc(s_rot2, 1)
                ve.wait_ge(s_rot1, at(b, 1))
                ve.wait_ge(s_rot2, at(b, 1))
                tt(qk[:, :, DE:], rot1[:, :, :], rot2[:, :, :], ALU.add).then_inc(rope_done, 1)

            def split_qk(b):
                ve.wait_ge(rope_done, at(b, 1))
                ve.wait_ge(qkT_ready, b)
                k = qk[:, H:, :]
                cp(parts[:, H:, 0:2 * DH].rearrange("p h (i d) -> p h i d", i=2),
                   k.unsqueeze(2).to_broadcast([P, H, 2, DH])).then_inc(k_hi, 1)
                ve.wait_ge(q_hi, at(b, 1))
                tt(parts[:, 0:H, DH:2 * DH], qk[:, 0:H, :], parts[:, 0:H, 0:DH], ALU.subtract).then_inc(q_lo, 1)
                ve.wait_ge(k_hi, at(b, 1))
                tt(parts[:, H:, 2 * DH:3 * DH], k, parts[:, H:, 0:DH], ALU.subtract).then_inc(parts_ready, 1)

            def save_kT(b, p):
                ve.wait_ge(qkT_ready, at(b, 1))
                ve.wait_ge(T_ready[1], at(b, -1))
                cp(kT[p][64:P, :, 1, :], qk_ps[64:P, :].bitcast(F16).rearrange("p (i k) -> p i k", i=HP))\
                    .then_inc(kT_odd_saved, 1)

            def row_max(b, half):
                ve.wait_ge(S_ready[half], at(b, 1))
                if not half:
                    ve.wait_ge(mst_ready, b)
                ve.tensor_reduce(negmax[:, 8 * half:8 * half + 8],
                                 ring[half][:, :].rearrange("q (h k) -> q h k", h=8), AX.X, ALU.max,
                                 negate=True).then_inc(row_maxed[half], 1)

            def split_max(b):
                ve.wait_ge(row_maxed[0], at(b, 1))
                ve.wait_ge(row_maxed[1], at(b, 1))
                ve.wait_ge(mT_ready, b)
                cp(mst[:, 0:H], negmax[:, :]).then_inc(s_mhi, 1)
                ve.wait_ge(s_mhi, at(b, 1))
                tt(mst[:, H:2 * H], negmax[:, :], mst[:, 0:H], ALU.subtract).then_inc(mst_ready, 1)

            def divide(b):
                ve.wait_ge(ytok_ready, at(b, 1))
                y = tail[:, :].rearrange("q (h d) -> q h d", h=H)
                ve.reciprocal(rden[:, :], y[:, :, DH]).then_inc(s_rden, 1)
                ve.wait_ge(s_rden, at(b, 1))
                ve.wait_ge(ynT_ready, b)
                tt(yn[:, :, :], y[:, :, 0:DH], rden[:, :].unsqueeze(2).to_broadcast([P, H, DH]),
                   ALU.mult).then_inc(yn_ready, 1)

            def add_attention(b):
                ve.wait_ge(attn_ready, at(b, 1))
                tt(feat(b), tail[:, C:2 * C], feat(b), ALU.add).then_inc(h2_ready, 1)
                ve.wait_ge(h2_ready, at(b, 1))
                stats(b, s_stats2)

            def step(b, p, has_front=True, has_tail=True):
                n, o = at(b, 1), at(b, -1)
                if has_front:
                    norm1(n)
                row_max(b, 0)
                if has_tail:
                    divide(o)
                row_max(b, 1)
                split_max(b)
                if has_front:
                    rope(n)
                if has_front:
                    split_qk(n)
                if has_tail:
                    add_attention(o)
                if has_front:
                    save_kT(n, 1 - p)

            ve.wait_ge(h_saved, 1)
            stats(0, s_stats)
            with ve.Fori(1, NB) as b:
                ve.wait_ge(h_saved, at(b, 1))
                stats(b, s_stats)
            ve.wait_ge(s_stats, NB)
            roots = inverse_roots(0)
            norm1(0)
            rope(0)
            split_qk(0)
            save_kT(0, 0)
            step(0, 0, has_tail=False)
            step(1, 1)
            with ve.Fori(2, NB - 3, 2) as b:
                step(b, 0)
                step(b + 1, 1)
            step(NB - 2, 0)
            step(NB - 1, 1, has_front=False)
            divide(NB - 1)
            add_attention(NB - 1)

            def split_quarter(e, p, i):
                part, side = divmod(i, 2)
                src = stage[:, 2048 * part + 1024 * side:2048 * part + 1024 * (side + 1)]
                hi, lo = (W[p][2 * part + n][:, 1024 * side:1024 * (side + 1)] for n in range(2))
                if i == 0:
                    ve.wait_ge(w1_in, at(e * 16, 16))
                    ve.wait_ge(w2_in, at(e * 16, 16))
                    ve.wait_ge(eo_ready, at(e * ST, -ST))
                ts(hi, src, WSCALE, None, ALU.mult).then_inc(wsplit_hi, 1)
                ve.wait_ge(wsplit_hi, at(e * QUARTERS, i + 1))
                x = ve.scalar_tensor_tensor(lo, src, WSCALE, hi, ALU.mult, ALU.subtract)
                x.then_inc(wsplit_lo, 1)
                if i == QUARTERS - 1:
                    ts(b1e[p][:, :], b1[:, bass.ds(e, 1), :].rearrange("p a f -> p (a f)"), 1.0, None,
                       ALU.mult).then_inc(bias_ready, 1)

            ve.wait_ge(s_stats2, NB)
            inverse_roots(roots)

            def norm2(b, p):
                ve.wait_ge(x2T_ready, at(b, -1))
                normalise(b, x2[p][:, :]).then_inc(x2_ready, 1)
                normalise(b, rows[:, bass.ds(b, 1), 0:C].rearrange("p a c -> p (a c)"))

            norm2(0, 0)
            norm2(1, 1)
            with ve.Fori(2, NB - 1, 2) as b:
                norm2(b, 0)
                norm2(b + 1, 1)
            order = [0]

            def chain(x):
                order[0] += 1
                x.then_inc(s_chain, 1)
                ve.wait_ge(s_chain, order[0])

            ve.wait_ge(ld_bias, 32)
            for i in range(QUARTERS):
                split_quarter(0, 0, i)
            ve.wait_ge(logits_ready, NB)
            lgs = v_ps[:, 0:NB * E].rearrange("p (b e) -> p b e", e=E)
            chain(tt(lg[:, :, :], lgs, rb[:, :].unsqueeze(1).to_broadcast([P, NB, E]), ALU.add))
            chain(ve.tensor_reduce(lmax[:, :], lg[:, :, :], AX.X, ALU.max))
            tt(lg[:, :, :], lg[:, :, :], lmax[:, :].unsqueeze(2).to_broadcast([P, NB, E]),
               ALU.subtract).then_inc(logits_shifted, 1)
            ve.wait_ge(exp_logits_done, 1)
            chain(ve.tensor_reduce(lsum[:, :], lg[:, :, :], AX.X, ALU.add))
            chain(ve.reciprocal(lsum[:, :], lsum[:, :]))
            chain(tt(scores[:, :, :].rearrange("p e b -> p b e"), lg[:, :, :],
                     lsum[:, :].unsqueeze(2).to_broadcast([P, NB, E]), ALU.mult))
            cp(rows[:, :, C:], scores[:, :, :].rearrange("p e b -> p b e")).then_inc(scores_ready, 1)

            ve.memset(thr[:, :], 0).then_inc(s_thr, 1)
            cp(cand[:, :, :], bits[:, 0, :, :]).then_inc(s_cand, 1)
            all_scores = scores[:, :, :].rearrange("p e b -> p b e").unsqueeze(2).to_broadcast([P, NB, CANDS, E])

            with ve.Fori(0, ROUNDS) as i:
                bit = bits[:, bass.ds(i, 1), 0, :].to_broadcast([P, CANDS, E])
                nxt = bits[:, bass.ds(i + 1, 1), :, :].rearrange("p a j e -> p (a j) e")
                ve.wait_ge(s_cand, at(i, 1))
                tt(reach[:, :, :, :], all_scores,
                   cand[:, :, :].bitcast(F32).unsqueeze(1).to_broadcast([P, NB, CANDS, E]), ALU.is_ge).then_inc(s_cmp, 1)
                ve.wait_ge(s_count, at(i, 1))
                ve.scalar_tensor_tensor(gain[:, :, :], front[:, 0:CANDS * E].rearrange("p (j e) -> p j e", e=E),
                                        float(CAP), bit, ALU.is_ge, ALU.mult).then_inc(s_gain, 1)
                ve.wait_ge(s_gain, at(i, 1))
                with nc.allow_low_precision(reason="GROUP bits of an integer, which float32 holds"):
                    ve.tensor_reduce(take[:, :], gain[:, :, :].rearrange("p j e -> p e j"), AX.X,
                                     ALU.add).then_inc(s_take, 1)
                ve.wait_ge(s_take, at(i, 1))
                tt(thr[:, :], thr[:, :], take[:, :], ALU.bitwise_or).then_inc(s_thr, 1)
                ve.wait_ge(s_thr, at(i, 2))
                tt(cand[:, :, :], thr[:, :].unsqueeze(1).to_broadcast([P, CANDS, E]), nxt,
                   ALU.bitwise_or).then_inc(s_cand, 1)

            def against(dst, op):
                return tt(dst, scores[:, :, :], thr[:, :].bitcast(F32).unsqueeze(2).to_broadcast([P, E, NB]), op)

            against(above[:, :, :], ALU.is_gt)
            against(eq[:, :, :], ALU.is_equal).then_inc(s_tie, 1)
            ve.wait_ge(s_tied, 1)
            def running(total, within):
                chain(cp(tot_sb[:, :, :], total))
                chain(ve.tensor_tensor_scan(flat(incl[:, :, :]), flat(seg[:, :, :]), flat(tot_sb[:, :, :]), 0.0,
                                            ALU.mult, ALU.add))
                chain(tt(incl[:, :, :], incl[:, :, :], tot_sb[:, :, :], ALU.subtract))
                chain(tt(rank[:, :, :], incl[:, :, :], within, ALU.add))

            def grid(t, i):
                return t[:, i * P:(i + 1) * P].rearrange("p (e b) -> p e b", e=E)

            chain(ve.tensor_reduce(cnt[:, :], grid(front, 0), AX.X, ALU.add))
            chain(ts(need[:, :], cnt[:, :], -1.0, float(CAP), ALU.mult, ALU.add))
            running(grid(front, 1), grid(front, 2))
            chain(tt(rank[:, :, :], rank[:, :, :], need[:, :].unsqueeze(2).to_broadcast([P, E, NB]), ALU.is_lt))
            chain(tt(rank[:, :, :], rank[:, :, :], eq[:, :, :], ALU.mult))
            tt(sel[:, :, :], rank[:, :, :], above[:, :, :], ALU.add).then_inc(s_chosen, 1)
            ve.wait_ge(s_chosen, 1)
            ve.wait_ge(s_prefix, 1)
            running(grid(qk_ps, 0), grid(qk_ps, 1))
            chain(tt(rank[:, :, :], rank[:, :, :], sel[:, :, :], ALU.mult))
            chain(ts(incl[:, :, :], sel[:, :, :], -1023.0, 1023.0, ALU.mult, ALU.add))
            chain(tt(slot[:, :, :], rank[:, :, :], incl[:, :, :], ALU.add))
            chain(ts(slot_lo_i[:, :, :], slot[:, :, :], P - 1, None, ALU.bitwise_and))
            chain(ts(slot_hi_i[:, :, :], slot[:, :, :], 7, None, ALU.logical_shift_right))
            chain(cp(slot_lo[:, :, :], slot_lo_i[:, :, :]))
            chain(cp(slot_hi[:, :, :], slot_hi_i[:, :, :]))
            chain(tt(hot_hi[:, :, :], flat(slot_hi[:, :, :]).unsqueeze(2).to_broadcast([P, E * NB, ST]),
                     iota_hi[:, :].unsqueeze(1).to_broadcast([P, E * NB, ST]), ALU.is_equal))
            for e in range(E):
                o = hot_hi[:, e * NB:(e + 1) * NB, :]
                x = tt(o, o, tok_id[:, :].unsqueeze(2).to_broadcast([P, NB, ST]), ALU.mult)
            x.then_inc(slots_ready, 1)
            ve.wait_ge(slots_ready, 1)

            def save_list(e):
                ve.wait_ge(list_ready, e + 1)
                cp(token_of[:, e, :], (front, qk_ps)[e % 2][:, 0:ST]).then_inc(list_saved, 1)

            for e in range(E):
                ve.wait_ge(list_ready, at(e, -1))
                tt(hot_lo[e % 2][:, :, :], slot_lo[:, e, :].unsqueeze(2).to_broadcast([P, NB, P]),
                   iota_lo[:, :].unsqueeze(1).to_broadcast([P, NB, P]), ALU.is_equal).then_inc(hot_ready, 1)
                if e:
                    save_list(e - 1)
            save_list(E - 1)

            def split_rows(e):
                for k in range(CT):
                    src = (tail if k else v_ps)[:, :]
                    ve.wait_ge(gT_ready, at(e * CT, k + 1))
                    ve.wait_ge(h1_ready, e * FT)
                    cp(gT[0][:, k, :], src).then_inc(gT_hi, 1)
                    ve.wait_ge(gT_hi, at(e * CT, k + 1))
                    tt(gT[1][:, k, :], src, gT[0][:, k, :], ALU.subtract).then_inc(gT_lo, 1)

            def split_hidden(e, f):
                ve.wait_ge(hid_hi, at(e * FT, f + 1))
                ve.wait_ge(relu_done, at(e * FT, f + 1))
                tt(hid[1][:, f, :], relu[:, f % 4, :], hid[0][:, f, :], ALU.subtract).then_inc(hid_lo, 1)

            def combine(e, p, t):
                ve.wait_ge(eo_ready, at(e * ST, t + 1))
                b2e = b2[:, bass.ds(e, 1), :].rearrange("p a c -> p (a c)")
                ve.wait_ge(contrib_ready, at(e * ST, t))
                ve.scalar_tensor_tensor(tmp[:, t % 2, :], (front, qk_ps)[t % 2][:, 0:C], 1.0 / WSCALE, b2e,
                                        ALU.mult, ALU.add).then_inc(s_eo, 1)
                ve.wait_ge(s_eo, at(e * ST, t + 1))
                ve.wait_ge(added, at(e * 64, 0))
                gate = got[p][:, t, C:].rearrange("p (a e) -> p a e", a=1)[:, 0, bass.ds(e, 1)]
                ts(contrib[:, t, :], tmp[:, t % 2, :], gate, None, ALU.mult).then_inc(contrib_ready, 1)

            def expert(e, p, last=False):
                for f in range(FT):
                    split_hidden(e, f)
                    if f in (1, 3, 5) and not last:
                        split_quarter(at(e, 1), 1 - p, f // 2)
                if not last:
                    split_rows(at(e, 1))
                    split_quarter(at(e, 1), 1 - p, QUARTERS - 1)
                for t in range(ST):
                    combine(e, p, t)

            split_rows(0)
            expert(0, 0)
            expert(1, 1)
            with ve.Fori(2, E - 3, 2) as e:
                expert(e, 0)
                expert(e + 1, 1)
            expert(E - 2, 0)
            expert(E - 1, 1, last=True)

        @blk.scalar
        def _(sc):
            def copy(dst, src):
                return sc.activation(dst, src, ACT.Copy)

            def save_h(b, p):
                sc.wait_ge(conv_ready, at(b, 1))
                if not isinstance(b, int):
                    sc.wait_ge(h_saved, b)
                    copy(spare_sc[:, :], spare_sc[:, :])
                copy(resid[:, bass.ds(b, 1), :].rearrange("p a c -> p (a c)"), (front, qk_ps)[p][:, 0:C]).then_inc(h_saved, 1)

            def save_xT(b):
                sc.wait_ge(xhatT_ready, at(b, 1))
                sc.wait_ge(qkv_ready, b)
                copy(flat(xT[:, :, :]), front[:, 0:C]).then_inc(xhatT_saved, 1)

            def save_qkv(b, p):
                sc.wait_ge(qkv_ready, at(b, 1))
                sc.wait_ge(parts_ready, b)
                sc.wait_ge(q_lo, b)
                copy(qk[:, :, 0:DE], qk_ps[:, :].rearrange("p (h d) -> p h d", d=DH)[:, :, 0:DE]).then_inc(qkc_saved, 1)
                sc.wait_ge(pv_done, at(b, -1))
                copy(bass.AP(vx[p], 0, [[H * P, P], [512, 4], [160, 4], [1, DH]]),
                     v_ps[:, 0:C].rearrange("p (g j d) -> p g j d", g=4, j=4)).then_inc(v_saved, 1)

            def high_q(b):
                sc.wait_ge(rope_done, at(b, 1))
                sc.wait_ge(qkT_ready, b)
                copy(parts[:, 0:H, :].rearrange("p h (i d) -> p h i d", d=DH)[:, :, 0:3:2, :],
                     qk[:, 0:H, :].unsqueeze(2).to_broadcast([P, H, 2, DH])).then_inc(q_hi, 1)

            def save_qkT(b, p):
                sc.wait_ge(qkT_ready, at(b, 1))
                sc.wait_ge(T_ready[1], at(b, -1))
                copy(flat(qT[p][:, :, :]), front[:, :].bitcast(F16)).then_inc(qT_saved, 1)
                copy(kT[p][0:64, :, 0, :], qk_ps[0:64, :].bitcast(F16).rearrange("p (i k) -> p i k", i=HP))\
                    .then_inc(kT_even_saved, 1)

            def save_mT(b):
                sc.wait_ge(mT_ready, at(b, 1))
                sc.wait_ge(T_ready[1], b)
                copy(mT[:, :], mT_ps).then_inc(mT_saved, 1)

            def exps(b, half):
                sc.wait_ge(T_ready[half], at(b, 1))
                sc.wait_ge(pv_done, b)
                sc.activation(flat(pT[:, 8 * half:8 * half + 8, :]), ring[half][:, :], ACT.Exp).then_inc(exp_done[half], 1)

            def save_y(b):
                sc.wait_ge(pv_done, at(b, 1))
                sc.wait_ge(ytok_ready, b)
                copy(flat(ysb[:, :, :]), tail[:, :]).then_inc(y_saved, 1)

            def save_ynT(b):
                sc.wait_ge(ynT_ready, at(b, 1))
                sc.wait_ge(attn_ready, b)
                copy(flat(ynT[:, :, :]), tail[:, 0:C]).then_inc(ynT_saved, 1)

            def save_x2T(b, p):
                sc.wait_ge(x2T_ready, at(b, 1))
                sc.wait_ge(logits_ready, at(b, -1))
                copy(flat(x2T[p][:, :, :]), (front, qk_ps)[p][:, 0:C]).then_inc(x2T_saved, 1)

            def step(b, p, has_front=True, has_tail=True):
                n, o = at(b, 1), at(b, -1)
                if has_tail:
                    save_y(o)
                if has_front:
                    save_xT(n)
                if has_tail:
                    save_ynT(o)
                save_mT(b)
                if has_front:
                    save_qkv(n, 1 - p)
                exps(b, 0)
                if has_front:
                    high_q(n)
                exps(b, 1)
                if has_front:
                    save_qkT(n, 1 - p)

            sc.wait_ge(pre_mem, 2)
            save_h(0, 0)
            save_h(1, 1)
            with sc.Fori(2, NB - 1, 2) as b:
                save_h(b, 0)
                save_h(b + 1, 1)
            save_xT(0)
            sc.wait_ge(zeroed, 2)
            save_qkv(0, 0)
            high_q(0)
            save_qkT(0, 0)
            step(0, 0, has_tail=False)
            step(1, 1)
            with sc.Fori(2, NB - 3, 2) as b:
                step(b, 0)
                step(b + 1, 1)
            step(NB - 2, 0)
            step(NB - 1, 1, has_front=False)
            save_y(NB - 1)
            save_ynT(NB - 1)
            save_x2T(0, 0)
            save_x2T(1, 1)
            with sc.Fori(2, NB - 1, 2) as b:
                save_x2T(b, 0)
                save_x2T(b + 1, 1)
            sc.wait_ge(logits_shifted, 1)
            sc.activation(flat(lg[:, :, :]), flat(lg[:, :, :]), ACT.Exp).then_inc(exp_logits_done, 1)

            def rectify(e, p, f):
                if f == 0:
                    sc.wait_ge(bias_ready, at(e, 1))
                sc.wait_ge(h1_ready, at(e * FT, f + 1))
                if f >= 4:
                    sc.wait_ge(hid_lo, at(e * FT, f - 3))
                else:
                    sc.wait_ge(hid_lo, e * FT)
                bias = b1e[p][:, f:f + 1]
                sc.activation(relu[:, f % 4, :], ring[f % 4 // 2][:, (f % 2) * 512:(f % 2 + 1) * 512], ACT.Relu,
                              bias=bias, scale=1.0 / WSCALE).then_inc(relu_done, 1)
                sc.wait_ge(eo_ready, at(e * ST, 0))
                sc.activation(hid[0][:, f, :], ring[f % 4 // 2][:, (f % 2) * 512:(f % 2 + 1) * 512], ACT.Relu,
                              bias=bias, scale=1.0 / WSCALE).then_inc(hid_hi, 1)

            def expert(e, p):
                for f in range(FT):
                    rectify(e, p, f)

            expert(0, 0)
            expert(1, 1)
            with sc.Fori(2, E - 1, 2) as e:
                expert(e, 0)
                expert(e + 1, 1)

        @blk.gpsimd
        def _(gp):
            def gather(e, p):
                gp.wait_ge(list_saved, e + 1)
                gp.wait_ge(got_in, e * 64)
                gp.wait_ge(contrib_ready, at(e * ST, -ST))
                gp.wait_ge(gT_ready, at(e * CT, -CT))
                for t in range(ST):
                    gp.indirect_dma_start(got[p][:, t, :], None, table,
                                          bass.IndirectOffsetOnAxis(ap=token_of[:, e, t:t + 1], axis=0)).then_inc(got_in, 16)

            def add(e, p, t):
                gp.wait_ge(contrib_ready, at(e * ST, t + 1))
                if t == 0:
                    gp.wait_ge(added, e * 64)
                gp.indirect_dma_start(out_rows, bass.IndirectOffsetOnAxis(ap=token_of[:, e, t:t + 1], axis=0),
                                      contrib[:, t, :], None, compute_op=ALU.add).then_inc(added, 16)

            def expert(e, p, last=False):
                if not last:
                    gather(at(e, 1), 1 - p)
                for t in range(ST):
                    add(e, p, t)

            gp.wait_ge(table_in, 16)
            gather(0, 0)
            gp.wait_ge(resid_out, 16 * NB)
            for e in range(E):
                expert(e, e % 2, last=e == E - 1)


def constants():
    i = np.arange(P)
    eye = np.eye(P, dtype=np.float32)
    later = i[None, :] > i[:, None]
    inv = (np.float32(1.0) / np.float32(10000.0) ** (np.arange(0, DE, 2, dtype=np.float32) / np.float32(DE))).astype(np.float32)
    ang = np.arange(T, dtype=np.float32)[:, None] * np.concatenate([inv, inv])[None, :]
    cos, sin = np.cos(ang).astype(np.float32), np.sin(ang).astype(np.float32)
    sin[:, 0::2] *= -1.0
    seg = np.ones((P, E, NB), np.float32)
    seg[:, :, 0] = 0.0
    bits = np.zeros((P, ROUNDS + 1, CANDS, E), np.int32)
    for r in range(ROUNDS):
        for j in range(CANDS):
            bits[:, r, j, :] = (j + 1) << (GROUP * (ROUNDS - 1 - r))
    return {
        "ident": eye,
        "mask_qk": np.where(later, np.float32(MASKED), np.float32(0)),
        "mask_kq": np.where(later.T, np.float32(MASKED), np.float32(0)),
        "cos": np.tile(cos, (1, 2 * H)), "sin": np.tile(sin, (1, 2 * H)),
        "lower": later.astype(np.float32),
        "iota_lo": np.tile(i.astype(np.float16), (P, 1)),
        "iota_hi": np.tile(np.arange(ST, dtype=np.float16), (P, 1)),
        "tok_id": (np.arange(NB)[None, :] * P + i[:, None]).astype(np.float32),
        "seg": seg.reshape(P, -1), "bits": bits.reshape(P, -1),
    }


def kernel(**inputs):
    import concourse.bacc as _bacc
    from concourse.bass_utils import run_bass_kernel_spmd as _run

    g = {k: np.ascontiguousarray(v) for k, v in inputs.items()}
    x, we, be = g["x"], g["L0_tok_W_embed"], g["L0_tok_b_embed"]
    xp = np.zeros((NB, CIN, x.shape[2] + TAPS - 1), x.dtype)
    xp[:, :, TAPS // 2:TAPS // 2 + x.shape[2]] = x
    xwin = np.stack([xp[:, c, j:j + DS * C:DS] for c in range(CIN) for j in range(WIN)])
    band = np.zeros((DS * CMID, KWIN + 1), we.dtype)
    for i in range(DS):
        for c in range(CIN):
            band[i * CMID:(i + 1) * CMID, c * WIN + i:c * WIN + i + TAPS] = we[:, c, :]
        band[i * CMID:(i + 1) * CMID, KWIN] = be
    up = np.zeros((3, P, 2 * DH), np.float32)
    ups = [np.concatenate([g["L0_attn_Wq_up_c"], g["L0_attn_Wq_up_e"]], 1),
           np.concatenate([g["L0_attn_Wk_up_c"], g["L0_attn_Wk_up_e"]], 1), g["L0_attn_Wv_up"]]
    for j in range(3):
        for i in range(2):
            up[j, i * L:(i + 1) * L, i * DH:(i + 1) * DH] = ups[j]
    arrays = {
        "xwin": xwin.reshape(KWIN, NB * C), "band": band,
        "wpT": np.ascontiguousarray(g["L0_tok_W_proj"][:, :, 0].T), "bp": g["L0_tok_b_proj"],
        "wdT": np.concatenate([g["L0_attn_Wq_down"].T, g["L0_attn_Wk_down"].T, g["L0_attn_Wv_down"].T]),
        "up": up, "wc": g["L0_attn_Wc"], "wr": g["L0_ffn_router_w"], "rb": g["L0_ffn_router_b"],
        "w1": g["L0_ffn_w1"], "b1": g["L0_ffn_b1"].reshape(E, FT, P).transpose(2, 0, 1).reshape(P, E * FT), "w2": g["L0_ffn_w2"], "b2": g["L0_ffn_b2"],
        **constants(),
    }
    arrays = {k: np.ascontiguousarray(v) for k, v in arrays.items()}
    nc = _bacc.Bacc("TRN2", target_bir_lowering=False, num_devices=1)
    a = {k: nc.dram_tensor(f"in_{k}", v.shape, mybir.dt.from_np(v.dtype), kind="ExternalInput").ap()
         for k, v in arrays.items()}
    out = nc.dram_tensor("out_0", (NB, T, C), F32, kind="ExternalOutput").ap()
    table = nc.dram_tensor("token_rows", (NB * T, ROW), F32, kind="Internal").ap()
    build(nc, a, out, table)
    r = _run(nc, [{f"in_{k}": v for k, v in arrays.items()}], core_ids=[0])
    return r.results[0]["out_0"]
```

```python
from contextlib import ExitStack

import numpy as np

import concourse.bass as bass
from concourse import mybir

F32 = mybir.dt.float32
F16 = mybir.dt.float16
BF16 = mybir.dt.bfloat16
I32 = mybir.dt.int32
U32 = mybir.dt.uint32
ALU = mybir.AluOpType
ACT = mybir.ActivationFunctionType
AX = mybir.AxisListType

P = 128
NB, T, C = 16, 128, 256
H, L, DH = 16, 64, 16
DE = DH // 2
CIN, TAPS, DS, CMID = 2, 7, 16, 32
WIN = DS + TAPS - 1
KWIN = CIN * WIN
KX = KWIN + 2
E, FF, CAP = 8, 1024, 512
FT, CT, ST = FF // P, C // P, CAP // P
SLOT, HP = 64, H // 2
GROUP = 3
CANDS = 2 ** GROUP - 1
ROUNDS = 10
ROW = C + E
EPS = 1e-5
SEED, NEWTON = float(0x5F3759DF), 3
QUARTERS = 4
VSCALE = 64.0
LIFT = 7.0
WSCALE = 64.0
MASKED = -1e30


def at(base, n):
    return max(base + n, 0) if isinstance(base, int) else base + n if n else base


def build(nc, a, out, table):
    with ExitStack() as ctx:
        def sb(name, shape, dt=F32):
            return ctx.enter_context(nc.sbuf_tensor(name, shape, dt))

        def sem(name):
            return ctx.enter_context(nc.semaphore(name))

        front = ctx.enter_context(nc.psum_tensor("front", [P, 512], F32))
        qk_ps = ctx.enter_context(nc.psum_tensor("qk_ps", [P, 512], F32))
        v_ps = ctx.enter_context(nc.psum_tensor("v_ps", [P, 512], F32))
        ring = [ctx.enter_context(nc.psum_tensor(f"ring{i}", [P, 1024], F32)) for i in range(2)]
        tail = ctx.enter_context(nc.psum_tensor("tail", [P, 512], F32))
        out_bank = [front, qk_ps, ring[1][:, 512:1024], ring[1][:, 0:512]]
        mT_ps = v_ps[:, 256:320].bitcast(BF16)

        ident = sb("ident", [P, P])
        ident_bf = sb("ident_bf", [P, P], BF16)
        ident_h = sb("ident_h", [P, P], F16)
        mask_qk = sb("mask_qk", [P, P], BF16)
        mask_kq = sb("mask_kq", [P, P], BF16)
        pick = sb("pick", [P, H, P], BF16)
        raw = sb("raw", [P, 3, P])
        cos_t = sb("cos_t", [P, 2 * H, DE])
        sin_t = sb("sin_t", [P, 2 * H, DE])
        lower = sb("lower", [P, P], BF16)
        ones_bf = sb("ones_bf", [P, P], BF16)
        iota_lo = sb("iota_lo", [P, P], F16)
        iota_hi = sb("iota_hi", [P, ST], F16)
        tok_id = sb("tok_id", [P, NB])
        seg = sb("seg", [P, E, NB])
        bits = sb("bits", [P, ROUNDS + 1, CANDS, E], I32)
        xwin = sb("xwin", [P, NB * C])
        band = sb("band", [P, 4, KWIN + 1])
        wpT = sb("wpT", [P, 4, P])
        weffT = sb("weffT", [64, P])
        stage = sb("stage", [P, 24 * C])
        wdT = stage[:, :].rearrange("p (j c) -> p j c", c=C)
        wqkv = sb("wqkv", [P, CT, 3 * C])
        wc = sb("wc", [P, CT, C])
        wr = sb("wr", [P, CT, E])
        rb = sb("rb", [P, E])
        b1 = sb("b1", [P, E, FT])
        b2 = sb("b2", [P, E, C])

        resid = sb("resid", [P, NB, C])
        scores = sb("scores", [P, E, NB])
        st6 = sb("st6", [P, NB, 6])
        mv = sb("mv", [P, NB, 2])
        var = sb("var", [P, NB])
        rstd = sb("rstd", [P, NB])
        newton = sb("newton", [P, NB])
        xhat = sb("xhat", [P, C])
        xT = sb("xT", [P, CT, P])
        qk = sb("qk", [P, 2 * H, DH])
        parts = sb("parts", [P, 2 * H, SLOT], F16)
        rot1 = sb("rot1", [P, 2 * H, DE])
        rot2 = sb("rot2", [P, 2 * H, DE])
        qT = [sb(f"qT{i}", [P, HP, P], F16) for i in range(2)]
        kT = [sb(f"kT{i}", [P, HP, 2, P], F16) for i in range(2)]
        vv = [sb(f"vv{i}", [P, 2, H, DH + 1], F16) for i in range(2)]
        negmax = sb("negmax", [P, H])
        mst = sb("mst", [P, P], BF16)
        mT = sb("mT", [P, P], BF16)
        pT = sb("pT", [P, H, P])
        ph = sb("ph", [P, 2, H, P], F16)
        lift = sb("lift", [P, 1])
        rden = sb("rden", [P, H])
        yn = sb("yn", [P, H, DH])
        ynT = sb("ynT", [P, CT, P])
        x2 = [sb(f"x2_{i}", [P, C]) for i in range(2)]
        x2T = [sb(f"x2T{i}", [P, CT, P]) for i in range(2)]
        rows = sb("rows", [P, NB, ROW])
        lg = sb("lg", [P, NB, E])
        lmax = sb("lmax", [P, NB])
        lsum = sb("lsum", [P, NB])

        thr = sb("thr", [P, E], I32)
        cand = sb("cand", [P, CANDS, E], I32)
        reach = sb("reach", [P, NB, CANDS, E], BF16)
        gain = sb("gain", [P, CANDS, E])
        take = sb("take", [P, E], I32)
        above = sb("above", [P, E, NB], BF16)
        eq = sb("eq", [P, E, NB], BF16)
        cnt = sb("cnt", [P, E])
        need = sb("need", [P, E])
        incl = sb("incl", [P, E, NB])
        tot_sb = sb("tot_sb", [P, E, NB])
        rank = sb("rank", [P, E, NB])
        sel = sb("sel", [P, E, NB], BF16)
        slot = sb("slot", [P, E, NB], I32)
        slot_lo_i = sb("slot_lo_i", [P, E, NB], I32)
        slot_hi_i = sb("slot_hi_i", [P, E, NB], I32)
        slot_lo = sb("slot_lo", [P, E, NB], F16)
        slot_hi = sb("slot_hi", [P, E, NB])
        hot_hi = sb("hot_hi", [P, E * NB, ST], F16)
        hot_lo = [ph[:, i] for i in range(2)]
        token_of = sb("token_of", [P, E, ST], U32)

        w1s = stage[:, 0:2048].rearrange("p (k f) -> p k f", k=CT)
        w2s = stage[:, 2048:4096].rearrange("p (f c) -> p f c", f=FT)
        wh = [sb(f"wh{i}", [P, 4, 2048], F16) for i in range(2)]
        W = [[wh[i][:, j, :] for j in range(4)] for i in range(2)]
        W1 = [[w.rearrange("p (k f) -> p k f", k=CT) for w in W[i][0:2]] for i in range(2)]
        W2 = [[w.rearrange("p (f c) -> p f c", f=FT) for w in W[i][2:4]] for i in range(2)]
        hid_all = xwin[:, :].bitcast(F16).rearrange("p (i f s) -> p i f s", i=2, f=FT)
        hid = [hid_all[:, i] for i in range(2)]
        relu = pT[:, :, :].rearrange("p h q -> p (h q)").rearrange("p (i s) -> p i s", i=4)
        got = [sb(f"got{i}", [P, ST, ROW]) for i in range(2)]
        gT = [kT[0][:, 4 * i:4 * i + 4, :, :].rearrange("p i j k -> p (i j k)").rearrange("p (k s) -> p k s", k=CT)
              for i in range(2)]
        tmp = qT[0][:, :, :].rearrange("p i k -> p (i k)").bitcast(F32).rearrange("p (i c) -> p i c", i=2)
        contrib = parts[:, :, :].rearrange("p h s -> p (h s)").bitcast(F32).rearrange("p (t c) -> p t c", t=ST)
        spare_ve = sb("spare_ve", [1, 1])
        b1e = [sb(f"b1e{i}", [P, FT]) for i in range(2)]

        up = pT[:, 0:12, :].rearrange("p (j i) m -> p j i m", j=3)
        weT = wh[1][:, :, :].rearrange("p i w -> p (i w)").bitcast(F32)[:, 0:3 * 2 * C]\
            .rearrange("p (j i c) -> p j i c", j=3, i=2)
        weT_bank = [ring[0][:, 0:512], ring[0][:, 512:1024], ring[1][:, 0:512]]
        eff_bank = [v_ps, tail, ring[1][:, 512:1024]]

        bias_ready = sem("bias_ready")
        ld_const = sem("ld_const")
        ld_w = sem("ld_w")
        ld_x = sem("ld_x")
        ld_bias = sem("ld_bias")
        ld_up = sem("ld_up")
        ld_down = [sem(f"ld_down_{i}") for i in "qkv"]
        zeroed = sem("zeroed")
        weff_ready = sem("weff_ready")
        weff_saved = sem("weff_saved")
        bp_in = sem("bp_in")
        weT_ready = sem("weT_ready")
        weT_saved = sem("weT_saved")
        eff_ready = sem("eff_ready")
        eff_saved = sem("eff_saved")
        bf_ready = sem("bf_ready")
        conv_ready = sem("conv_ready")
        h_saved = sem("h_saved")
        s_stats = sem("s_stats")
        s_stats2 = sem("s_stats2")
        s_root = sem("s_root")
        xhat_ready = sem("xhat_ready")
        xhatT_ready = sem("xhatT_ready")
        xhatT_saved = sem("xhatT_saved")
        qk_ready = sem("qk_ready")
        v_ready = sem("v_ready")
        qkc_saved = sem("qkc_saved")
        v_hi = sem("v_hi")
        v_lo = sem("v_lo")
        s_rot1 = sem("s_rot1")
        s_rot2 = sem("s_rot2")
        rope_done = sem("rope_done")
        q_hi = sem("q_hi")
        k_hi = sem("k_hi")
        q_lo = sem("q_lo")
        parts_ready = sem("parts_ready")
        qkT_ready = sem("qkT_ready")
        kT_even_saved = sem("kT_even_saved")
        kT_odd_saved = sem("kT_odd_saved")
        qT_saved = sem("qT_saved")
        s_mhi = sem("s_mhi")
        mst_ready = sem("mst_ready")
        mT_ready = sem("mT_ready")
        mT_saved = sem("mT_saved")
        pv_done = sem("pv_done")
        s_rden = sem("s_rden")
        yn_ready = sem("yn_ready")
        ynT_ready = sem("ynT_ready")
        ynT_saved = sem("ynT_saved")
        attn_ready = sem("attn_ready")
        h2_ready = sem("h2_ready")
        x2_ready = sem("x2_ready")
        x2T_ready = sem("x2T_ready")
        x2T_saved = sem("x2T_saved")
        logits_ready = sem("logits_ready")
        logits_shifted = sem("logits_shifted")
        exp_logits_done = sem("exp_logits_done")
        scores_ready = sem("scores_ready")
        table_in = sem("table_in")
        resid_out = sem("resid_out")
        s_cmp = sem("s_cmp")
        s_count = sem("s_count")
        s_gain = sem("s_gain")
        s_take = sem("s_take")
        s_cand = sem("s_cand")
        s_thr = sem("s_thr")
        s_tie = sem("s_tie")
        s_tied = sem("s_tied")
        s_chosen = sem("s_chosen")
        s_prefix = sem("s_prefix")
        s_chain = sem("s_chain")
        slots_ready = sem("slots_ready")
        hot_ready = sem("hot_ready")
        list_ready = sem("list_ready")
        list_saved = sem("list_saved")
        w1_in = sem("w1_in")
        w2_in = sem("w2_in")
        wsplit_hi = sem("wsplit_hi")
        wsplit_lo = sem("wsplit_lo")
        got_in = sem("got_in")
        gT_ready = sem("gT_ready")
        gT_hi = sem("gT_hi")
        gT_lo = sem("gT_lo")
        h1_ready = sem("h1_ready")
        relu_done = sem("relu_done")
        hid_hi = sem("hid_hi")
        hid_lo = sem("hid_lo")
        eo_ready = sem("eo_ready")
        s_eo = sem("s_eo")
        contrib_ready = sem("contrib_ready")
        added = sem("added")
        S_ready = [sem("S_ready_lo"), sem("S_ready_hi")]
        T_ready = [sem("T_ready_lo"), sem("T_ready_hi")]
        row_maxed = [sem("row_maxed_lo"), sem("row_maxed_hi")]
        p_hi = [sem("p_hi_lo"), sem("p_hi_hi")]
        p_lo = [sem("p_lo_lo"), sem("p_lo_hi")]
        exp_done = [sem("exp_done_lo"), sem("exp_done_hi")]

        def take_wait(e, spare):
            e.tensor_tensor(spare, spare, spare, ALU.mult)

        out_rows = out.rearrange("b t c -> (b t) c")

        def flat(t):
            return t.rearrange("p a b -> p (a b)")

        blk = ctx.enter_context(nc.Block())

        @blk.sync
        def _(sp):
            def ld(dst, src, done):
                sp.dma_start(dst, src).then_inc(done, 16)

            ld(band[:, :, :], a["band"].rearrange("(s p) j -> p s j", p=P), ld_w)
            ld(wpT[:, :, :], a["wpT"].rearrange("(s p) o -> p s o", p=P), ld_w)
            ld(weffT[KX - 1:KX, :], a["bp"].rearrange("(a o) -> a o", a=1), bp_in)
            ld(xwin[0:KX, :], a["xwin"], ld_x)
            ld(pT[:, 0:12, :].rearrange("p i m -> p (i m)"), a["up"], ld_up)
            for j in range(3):
                ld(wdT[:, 8 * j:8 * j + 8, :], a["wdT"][j * 8 * P:(j + 1) * 8 * P].rearrange("(j p) c -> p j c", p=P),
                   ld_down[j])
            for dst, n in [(ident[:, :], "ident"), (raw[:, 0, :], "mask_qk"), (raw[:, 1, :], "mask_kq"),
                           (raw[:, 2, :], "lower"),
                           (flat(cos_t[:, :, :]), "cos"), (flat(sin_t[:, :, :]), "sin"),
                           (iota_lo[:, :], "iota_lo"), (iota_hi[:, :], "iota_hi"), (tok_id[:, :], "tok_id"),
                           (flat(seg[:, :, :]), "seg"), (bits[:, :, :, :].rearrange("p r j e -> p (r j e)"), "bits")]:
                ld(dst, a[n], ld_const)
            ld(wc[:, :, :], a["wc"].rearrange("(k p) c -> p k c", p=P), ld_const)
            ld(wr[:, :, :], a["wr"].rearrange("(k p) e -> p k e", p=P), ld_const)
            ld(rb[:, :], a["rb"].partition_broadcast(P), ld_const)
            ld(flat(b1[:, :, :]), a["b1"], ld_bias)
            ld(b2[:, :, :], a["b2"].partition_broadcast(P), ld_bias)
            sp.wait_ge(weT_ready, 3)
            sp.dma_start(w1s, a["w1"][0].rearrange("(k p) f -> p k f", p=P)).then_inc(w1_in, 16)
            sp.dma_start(w2s, a["w2"][0].rearrange("(f p) c -> p f c", p=P)).then_inc(w2_in, 16)
            with sp.Fori(0, NB) as b:
                sp.wait_ge(h2_ready, at(b, 1))
                sp.dma_start(out_rows[bass.ds(b * P, P), :], resid[:, bass.ds(b, 1), :]).then_inc(resid_out, 16)
            sp.wait_ge(scores_ready, 1)
            sp.dma_start(table.rearrange("(b p) r -> p b r", p=P), rows[:, :, :]).then_inc(table_in, 16)

            def weights(e):
                sp.wait_ge(wsplit_lo, e * QUARTERS)
                sp.dma_start(w1s, a["w1"][bass.ds(e, 1)].rearrange("a (k p) f -> p (a k) f", p=P)).then_inc(w1_in, 16)
                sp.dma_start(w2s, a["w2"][bass.ds(e, 1)].rearrange("a (f p) c -> p (a f) c", p=P)).then_inc(w2_in, 16)

            with sp.Fori(1, E) as e:
                weights(e)
            sp.wait_ge(resid_out, 16 * NB)
            sp.wait_ge(table_in, 16)
            sp.wait_ge(added, 16 * ST * E)

        @blk.tensor
        def _(pe):
            mm, tr = pe.matmul, pe.transpose

            pe.wait_ge(ld_w, 32)
            for i in range(4):
                x = mm(front[0:KWIN + 1, 0:P], band[:, i, :], wpT[:, i, :], start=i == 0, stop=i == 3)
            x.then_inc(weff_ready, 1)
            pe.wait_ge(weff_saved, 1)
            pe.wait_ge(ld_x, 16)
            pe.wait_ge(bp_in, 16)
            for b in range(NB):
                pe.wait_ge(h_saved, at(b, -1))
                mm((front, qk_ps)[b % 2][:, 0:C], weffT[0:KX, :], xwin[0:KX, b * C:(b + 1) * C],
                   start=True, stop=True).then_inc(conv_ready, 1)
            pe.wait_ge(ld_up, 16)
            for j in range(3):
                pe.wait_ge(ld_down[j], 16)
                for half in range(2):
                    for i in range(4):
                        x = mm(weT_bank[j][:, half * C:(half + 1) * C], up[:, j, i, :], wdT[:, 8 * j + 4 * half + i, :],
                               start=i == 0, stop=i == 3)
                x.then_inc(weT_ready, 1)
            pe.wait_ge(ld_const, 16 * 14)
            for j in range(3):
                pe.wait_ge(weT_saved, j + 1)
                for k in range(CT):
                    for half in range(2):
                        x = tr(eff_bank[j][:, k * C + half * P:k * C + (half + 1) * P],
                               weT[:, j, half, k * P:(k + 1) * P], ident[:, :])
                x.then_inc(eff_ready, 1)
            pe.wait_ge(eff_saved, 3)
            pe.wait_ge(bf_ready, 1)
            pe.wait_ge(h_saved, NB)

            def xhat_t(b):
                pe.wait_ge(xhat_ready, at(b, 1))
                pe.wait_ge(qT_saved, b)
                for k in range(CT):
                    x = tr(front[:, k * P:(k + 1) * P], xhat[:, k * P:(k + 1) * P], ident[:, :])
                x.then_inc(xhatT_ready, 1)

            def qk(b):
                pe.wait_ge(xhatT_saved, at(b, 1))
                pe.wait_ge(kT_even_saved, b)
                pe.wait_ge(kT_odd_saved, b)
                for k in range(CT):
                    x = mm(qk_ps[:, :], xT[:, k, :], wqkv[:, k, 0:2 * C], start=k == 0, stop=k == CT - 1)
                x.then_inc(qk_ready, 1)

            def v(b):
                pe.wait_ge(v_lo, b)
                pe.wait_ge(mT_saved, b)
                for k in range(CT):
                    x = mm(v_ps[:, 0:C], xT[:, k, :], wqkv[:, k, 2 * C:], start=k == 0, stop=k == CT - 1)
                x.then_inc(v_ready, 1)

            def qk_t(b):
                pe.wait_ge(parts_ready, at(b, 1))
                pe.wait_ge(q_lo, at(b, 1))
                split = flat(parts[:, :, :])
                for bank, first in ((front, 0), (qk_ps, HP)):
                    o = bank[:, :].bitcast(F16)
                    for i in range(HP):
                        x = tr(o[:, i * P:(i + 1) * P], split[:, (first + i) * P:(first + i + 1) * P], ident_h[:, :])
                x.then_inc(qkT_ready, 1)

            def scores_for_max(b, p, half):
                pe.wait_ge(exp_done[half], b)
                if not half:
                    pe.wait_ge(kT_even_saved, at(b, 1))
                    pe.wait_ge(kT_odd_saved, at(b, 1))
                    pe.wait_ge(qT_saved, at(b, 1))
                for c in range(2):
                    o = ring[half][:, c * 512:(c + 1) * 512]
                    for j in range(2):
                        i = 4 * half + 2 * c + j
                        mm(o[:, j * 2 * P:(j + 1) * 2 * P], qT[p][:, i, :], flat(kT[p][:, i, :, :]),
                           start=j == 0, stop=False, skip_group_check=True)
                    x = mm(o.rearrange("q (h k) -> q h k", h=4), ident_bf[:, :],
                           mask_qk[:, :].unsqueeze(1).to_broadcast([P, 4, P]), start=False, stop=True,
                           skip_group_check=True)
                x.then_inc(S_ready[half], 1)

            def max_t(b):
                pe.wait_ge(mst_ready, at(b, 1))
                pe.wait_ge(v_lo, at(b, 1))
                tr(mT_ps, mst[:, :], ident_bf[:, :]).then_inc(mT_ready, 1)

            def scores_t(b, p, half):
                if not half:
                    pe.wait_ge(mT_saved, at(b, 1))
                pe.wait_ge(row_maxed[half], at(b, 1))
                for c in range(2):
                    o = ring[half][:, c * 512:(c + 1) * 512]
                    for j in range(4):
                        i = 4 * half + 2 * c + j // 2
                        mm(o[:, j * P:(j + 1) * P], kT[p][:, i, j % 2, :], qT[p][:, i, :],
                           start=j == 0, stop=False, skip_group_check=True)
                    for j in range(4):
                        mm(o[:, j * P:(j + 1) * P], pick[:, 8 * half + 4 * c + j, :], mT[:, :],
                           start=False, stop=False, skip_group_check=True)
                    x = mm(o.rearrange("q (h k) -> q h k", h=4), ident_bf[:, :],
                           mask_kq[:, :].unsqueeze(1).to_broadcast([P, 4, P]), start=False, stop=True,
                           skip_group_check=True)
                x.then_inc(T_ready[half], 1)

            def values(b, p, half):
                pe.wait_ge(p_lo[half], at(b, 1))
                pe.wait_ge(v_lo, at(b, 1))
                pe.wait_ge(h2_ready, b)
                for h in range(8 * half, 8 * half + 8):
                    o = tail[:, 32 * h:32 * h + DH + 1]
                    mm(o, ph[:, 0, h, :], vv[p][:, 0, h, :], start=True, stop=False)
                    mm(o, ph[:, 0, h, :], vv[p][:, 1, h, :], start=False, stop=False)
                    x = mm(o, ph[:, 1, h, :], vv[p][:, 0, h, :], start=False, stop=True)
                if half:
                    x.then_inc(pv_done, 1)

            def yn_t(b):
                pe.wait_ge(yn_ready, at(b, 1))
                ynf = flat(yn[:, :, :])
                for k in range(CT):
                    x = tr(tail[:, k * P:(k + 1) * P], ynf[:, k * P:(k + 1) * P], ident[:, :])
                x.then_inc(ynT_ready, 1)

            def out_proj(b):
                pe.wait_ge(ynT_saved, at(b, 1))
                for k in range(CT):
                    x = mm(tail[:, C:2 * C], ynT[:, k, :], wc[:, k, :], start=k == 0, stop=k == CT - 1)
                x.then_inc(attn_ready, 1)

            def x2_t(b, p):
                pe.wait_ge(x2_ready, at(b, 1))
                pe.wait_ge(x2T_saved, at(b, -1))
                for k in range(CT):
                    x = tr((front, qk_ps)[p][:, k * P:(k + 1) * P], x2[p][:, k * P:(k + 1) * P], ident[:, :])
                x.then_inc(x2T_ready, 1)

            def router(b, p):
                pe.wait_ge(x2T_saved, at(b, 1))
                for k in range(CT):
                    x = mm(v_ps[:, bass.ds(b * E, E)], x2T[p][:, k, :], wr[:, k, :], start=k == 0, stop=k == CT - 1)
                x.then_inc(logits_ready, 1)

            def step(b, p, has_front=True, has_tail=True):
                n, o = at(b, 1), at(b, -1)
                scores_for_max(b, p, 0)
                if has_tail:
                    values(o, 1 - p, 0)
                scores_for_max(b, p, 1)
                if has_tail:
                    values(o, 1 - p, 1)
                if has_front:
                    xhat_t(n)
                    qk(n)
                max_t(b)
                if has_front:
                    v(n)
                scores_t(b, p, 0)
                if has_tail:
                    yn_t(o)
                scores_t(b, p, 1)
                if has_front:
                    qk_t(n)
                if has_tail:
                    out_proj(o)

            xhat_t(0)
            qk(0)
            v(0)
            qk_t(0)
            step(0, 0, has_tail=False)
            step(1, 1)
            with pe.Fori(2, NB - 3, 2) as b:
                step(b, 0)
                step(b + 1, 1)
            step(NB - 2, 0)
            step(NB - 1, 1, has_front=False)
            values(NB - 1, 1, 0)
            values(NB - 1, 1, 1)
            yn_t(NB - 1)
            out_proj(NB - 1)

            x2_t(0, 0)
            x2_t(1, 1)
            router(0, 0)
            with pe.Fori(2, NB - 1, 2) as b:
                x2_t(b, 0)
                router(b - 1, 1)
                x2_t(b + 1, 1)
                router(b, 0)
            router(NB - 1, 1)

            with pe.Fori(0, ROUNDS) as i:
                for b in range(NB):
                    if b in (0, NB // 2):
                        pe.wait_ge(s_cmp, at(i * 2, 1 if b == 0 else 2))
                    x = mm(front[:, 0:CANDS * E], ones_bf[:, :], flat(reach[:, b, :, :]), start=b == 0, stop=b == NB - 1)
                x.then_inc(s_count, 1)
            pe.wait_ge(s_tie, 1)
            mm(front[:, 0:P], ones_bf[:, :], flat(above[:, :, :]), start=True, stop=True)
            mm(front[:, P:2 * P], ones_bf[:, :], flat(eq[:, :, :]), start=True, stop=True)
            mm(front[:, 2 * P:3 * P], lower[:, :], flat(eq[:, :, :]), start=True, stop=True).then_inc(s_tied, 1)
            pe.wait_ge(s_chosen, 1)
            mm(qk_ps[:, 0:P], ones_bf[:, :], flat(sel[:, :, :]), start=True, stop=True)
            mm(qk_ps[:, P:2 * P], lower[:, :], flat(sel[:, :, :]), start=True, stop=True).then_inc(s_prefix, 1)
            for e in range(E):
                pe.wait_ge(hot_ready, e + 1)
                pe.wait_ge(list_saved, at(e, -1))
                for b in range(NB):
                    x = mm((front, qk_ps)[e % 2][:, 0:ST], hot_lo[e % 2][:, b, :], hot_hi[:, e * NB + b, :],
                           start=b == 0, stop=b == NB - 1)
                x.then_inc(list_ready, 1)

            def transpose_rows(e, p):
                pe.wait_ge(got_in, at(e * 64, 64))
                for k in range(CT):
                    pe.wait_ge(gT_lo, at(e * CT, k - 1) if k else e * CT)
                    for t in range(ST):
                        x = tr((tail if k else v_ps)[:, t * P:(t + 1) * P], got[p][:, t, k * P:(k + 1) * P], ident[:, :])
                    x.then_inc(gT_ready, 1)

            def hidden(e, p, f):
                if f == 0:
                    pe.wait_ge(gT_lo, at(e * CT, CT))
                    pe.wait_ge(wsplit_lo, at(e * QUARTERS, QUARTERS))
                pe.wait_ge(relu_done, at(e * FT, f - 3))
                if f in (2, 3):
                    pe.wait_ge(s_eo, e * ST)
                o = ring[f % 4 // 2][:, (f % 2) * 512:(f % 2 + 1) * 512]
                terms = [(i, j, k) for i, j in ((0, 0), (0, 1), (1, 0)) for k in range(CT)]
                for n, (i, j, k) in enumerate(terms):
                    x = mm(o, W1[p][i][:, k, f * P:(f + 1) * P], gT[j][:, k, :], start=n == 0, stop=n == len(terms) - 1)
                x.then_inc(h1_ready, 1)

            def expert_out(e, p, t):
                if t == 0:
                    pe.wait_ge(hid_hi, at(e * FT, FT - 1))
                    pe.wait_ge(list_saved, E)
                    pe.wait_ge(s_eo, e * ST)
                if t == 2:
                    pe.wait_ge(relu_done, at(e * FT, FT))
                o = out_bank[t][:, 0:C]
                terms = [(i, j, f) for i, j in ((0, 0), (0, 1), (1, 0)) for f in range(FT)]
                for n, (i, j, f) in enumerate(terms):
                    if t == 0 and n == FT - 1:
                        pe.wait_ge(hid_hi, at(e * FT, FT))
                    if t == 0 and n == 2 * FT:
                        pe.wait_ge(hid_lo, at(e * FT, FT))
                    x = mm(o, hid[i][:, f, t * P:(t + 1) * P], W2[p][j][:, f, :], start=n == 0, stop=n == len(terms) - 1)
                x.then_inc(eo_ready, 1)

            def expert(e, p, last=False):
                for f in range(FT):
                    hidden(e, p, f)
                if not last:
                    transpose_rows(at(e, 1), 1 - p)
                for t in range(ST):
                    expert_out(e, p, t)

            transpose_rows(0, 0)
            expert(0, 0)
            expert(1, 1)
            with pe.Fori(2, E - 3, 2) as e:
                expert(e, 0)
                expert(e + 1, 1)
            expert(E - 2, 0)
            expert(E - 1, 1, last=True)

        @blk.vector
        def _(ve):
            tt, ts, cp = ve.tensor_tensor, ve.tensor_scalar, ve.tensor_copy
            ve.wait_ge(weff_ready, 1)
            cp(weffT[0:KWIN + 1, :], front[0:KWIN + 1, 0:P]).then_inc(weff_saved, 1)

            def feat(b):
                return resid[:, bass.ds(b, 1), :].rearrange("p a c -> p (a c)")

            def stats(b, done):
                ve.wait_ge(done, b)
                take_wait(ve, spare_ve[:, :])
                ve.bn_stats(st6[:, bass.ds(b, 1), :].rearrange("p a s -> p (a s)"), feat(b)).then_inc(done, 1)

            def inverse_roots(first):
                count = [first]

                def after(x):
                    count[0] += 1
                    x.then_inc(s_root, 1)
                    ve.wait_ge(s_root, count[0])

                for b in range(NB):
                    x = ve.bn_aggr(mv[:, b, :], st6[:, b, :])
                after(x)
                after(ts(var[:, :], mv[:, :, 1], EPS, None, ALU.add))
                after(ts(rstd[:, :].bitcast(I32), var[:, :].bitcast(I32), -0.5, SEED, ALU.mult, ALU.add))
                for _ in range(NEWTON):
                    after(tt(newton[:, :], rstd[:, :], rstd[:, :], ALU.mult))
                    after(tt(newton[:, :], newton[:, :], var[:, :], ALU.mult))
                    after(ts(newton[:, :], newton[:, :], -0.5, 1.5, ALU.mult, ALU.add))
                    after(tt(rstd[:, :], rstd[:, :], newton[:, :], ALU.mult))
                return count[0]

            def save_eff(j, scale):
                ve.wait_ge(eff_ready, j + 1)
                ts(wqkv[:, :, j * C:(j + 1) * C], eff_bank[j][:, :].rearrange("p (k c) -> p k c", k=CT),
                   scale, None, ALU.mult).then_inc(eff_saved, 1)

            def normalise(b, dst):
                return ts(dst, feat(b), mv[:, bass.ds(b, 1), 0:1].rearrange("p a s -> p (a s)"),
                          rstd[:, bass.ds(b, 1)], ALU.subtract, ALU.mult)

            def norm1(b):
                ve.wait_ge(xhatT_ready, b)
                normalise(b, xhat[:, :]).then_inc(xhat_ready, 1)

            def rope(b):
                ve.wait_ge(qkc_saved, at(b, 1))
                rot = qk_ps[:, :].rearrange("p (h d) -> p h d", d=DH)[:, :, DE:]
                tt(rot1[:, :, :], rot, cos_t[:, :, :], ALU.mult).then_inc(s_rot1, 1)
                for i in range(2):
                    x = tt(rot2[:, :, i::2], rot[:, :, 1 - i::2], sin_t[:, :, i::2], ALU.mult)
                x.then_inc(s_rot2, 1)
                ve.wait_ge(s_rot1, at(b, 1))
                ve.wait_ge(s_rot2, at(b, 1))
                tt(qk[:, :, DE:], rot1[:, :, :], rot2[:, :, :], ALU.add).then_inc(rope_done, 1)

            def split_qk(b):
                ve.wait_ge(rope_done, at(b, 1))
                ve.wait_ge(qkT_ready, b)
                k = qk[:, H:, :]
                cp(parts[:, H:, 0:2 * DH].rearrange("p h (i d) -> p h i d", i=2),
                   k.unsqueeze(2).to_broadcast([P, H, 2, DH])).then_inc(k_hi, 1)
                ve.wait_ge(q_hi, at(b, 1))
                tt(parts[:, 0:H, DH:2 * DH], qk[:, 0:H, :], parts[:, 0:H, 0:DH], ALU.subtract).then_inc(q_lo, 1)
                ve.wait_ge(k_hi, at(b, 1))
                tt(parts[:, H:, 2 * DH:3 * DH], k, parts[:, H:, 0:DH], ALU.subtract).then_inc(parts_ready, 1)

            def low_v(b, p):
                ve.wait_ge(v_hi, at(b, 1))
                tt(vv[p][:, 1, :, 0:DH], v_ps[:, 0:C].rearrange("p (h d) -> p h d", d=DH), vv[p][:, 0, :, 0:DH],
                   ALU.subtract).then_inc(v_lo, 1)

            def save_qkT(b, p):
                ve.wait_ge(qkT_ready, at(b, 1))
                ve.wait_ge(T_ready[1], at(b, -1))
                cp(kT[p][64:P, :, 1, :], qk_ps[64:P, :].bitcast(F16).rearrange("p (i k) -> p i k", i=HP))\
                    .then_inc(kT_odd_saved, 1)
                cp(flat(qT[p][:, :, :]), front[:, :].bitcast(F16)).then_inc(qT_saved, 1)

            def low_p(b, half):
                ve.wait_ge(p_hi[half], at(b, 1))
                ve.wait_ge(exp_done[half], at(b, 1))
                h = slice(8 * half, 8 * half + 8)
                tt(ph[:, 1, h, :], pT[:, h, :], ph[:, 0, h, :], ALU.subtract).then_inc(p_lo[half], 1)

            def row_max(b, half):
                ve.wait_ge(S_ready[half], at(b, 1))
                if not half:
                    ve.wait_ge(mst_ready, b)
                ve.tensor_reduce(negmax[:, 8 * half:8 * half + 8],
                                 ring[half][:, :].rearrange("q (h k) -> q h k", h=8), AX.X, ALU.max,
                                 negate=True).then_inc(row_maxed[half], 1)

            def split_max(b):
                ve.wait_ge(row_maxed[0], at(b, 1))
                ve.wait_ge(row_maxed[1], at(b, 1))
                ve.wait_ge(mT_ready, b)
                cp(mst[:, 0:H], negmax[:, :]).then_inc(s_mhi, 1)
                ve.wait_ge(s_mhi, at(b, 1))
                tt(mst[:, H:2 * H], negmax[:, :], mst[:, 0:H], ALU.subtract).then_inc(mst_ready, 1)

            def divide(b):
                ve.wait_ge(pv_done, at(b, 1))
                y = tail[:, :].rearrange("q (h d) -> q h d", h=H)
                ve.reciprocal(rden[:, :], y[:, :, DH]).then_inc(s_rden, 1)
                ve.wait_ge(s_rden, at(b, 1))
                ve.wait_ge(ynT_ready, b)
                tt(yn[:, :, :], y[:, :, 0:DH], rden[:, :].unsqueeze(2).to_broadcast([P, H, DH]),
                   ALU.mult).then_inc(yn_ready, 1)

            def add_attention(b):
                ve.wait_ge(attn_ready, at(b, 1))
                tt(feat(b), tail[:, C:2 * C], feat(b), ALU.add).then_inc(h2_ready, 1)
                ve.wait_ge(h2_ready, at(b, 1))
                stats(b, s_stats2)

            def step(b, p, has_front=True, has_tail=True, has_next=True):
                n, o = at(b, 1), at(b, -1)
                row_max(b, 0)
                row_max(b, 1)
                split_max(b)
                if has_tail:
                    divide(o)
                if has_front:
                    rope(n)
                    split_qk(n)
                    low_v(n, 1 - p)
                low_p(b, 0)
                if has_front:
                    save_qkT(n, 1 - p)
                if has_tail:
                    add_attention(o)
                low_p(b, 1)
                if has_next:
                    norm1(at(b, 2))

            def split_quarter(e, p, i):
                part, side = divmod(i, 2)
                src = stage[:, 2048 * part + 1024 * side:2048 * part + 1024 * (side + 1)]
                hi, lo = (W[p][2 * part + n][:, 1024 * side:1024 * (side + 1)] for n in range(2))
                if i == 0:
                    ve.wait_ge(w1_in, at(e * 16, 16))
                    ve.wait_ge(w2_in, at(e * 16, 16))
                    ve.wait_ge(eo_ready, at(e * ST, -ST))
                ts(hi, src, WSCALE, None, ALU.mult).then_inc(wsplit_hi, 1)
                ve.wait_ge(wsplit_hi, at(e * QUARTERS, i + 1))
                x = ve.scalar_tensor_tensor(lo, src, WSCALE, hi, ALU.mult, ALU.subtract)
                x.then_inc(wsplit_lo, 1)
                if i == QUARTERS - 1:
                    ts(b1e[p][:, :], b1[:, bass.ds(e, 1), :].rearrange("p a f -> p (a f)"), 1.0, None,
                       ALU.mult).then_inc(bias_ready, 1)

            for b in range(NB):
                ve.wait_ge(h_saved, b + 1)
                ve.bn_stats(st6[:, b, :], resid[:, b, :]).then_inc(s_stats, 1)
            ve.wait_ge(s_stats, NB)
            roots = inverse_roots(0)
            norm1(0)
            save_eff(0, DH ** -0.5)
            save_eff(1, 1.0)
            save_eff(2, VSCALE)
            ve.wait_ge(ld_const, 16 * 14)
            ve.wait_ge(zeroed, 2)
            ve.wait_ge(bf_ready, 1)
            rope(0)
            split_qk(0)
            low_v(0, 0)
            save_qkT(0, 0)
            norm1(1)
            ve.wait_ge(ld_bias, 32)
            split_quarter(0, 0, 0)
            step(0, 0, has_tail=False)
            for i in range(1, QUARTERS - 1):
                split_quarter(0, 0, i)
            step(1, 1)
            split_quarter(0, 0, QUARTERS - 1)
            with ve.Fori(2, NB - 3, 2) as b:
                step(b, 0)
                step(b + 1, 1)
            step(NB - 2, 0, has_next=False)
            step(NB - 1, 1, has_front=False, has_next=False)
            divide(NB - 1)
            add_attention(NB - 1)

            ve.wait_ge(s_stats2, NB)
            inverse_roots(roots)

            def norm2(b, p):
                ve.wait_ge(x2T_ready, at(b, -1))
                normalise(b, x2[p][:, :]).then_inc(x2_ready, 1)
                normalise(b, rows[:, bass.ds(b, 1), 0:C].rearrange("p a c -> p (a c)"))

            norm2(0, 0)
            norm2(1, 1)
            with ve.Fori(2, NB - 1, 2) as b:
                norm2(b, 0)
                norm2(b + 1, 1)
            order = [0]

            def chain(x):
                order[0] += 1
                x.then_inc(s_chain, 1)
                ve.wait_ge(s_chain, order[0])

            ve.wait_ge(logits_ready, NB)
            lgs = v_ps[:, 0:NB * E].rearrange("p (b e) -> p b e", e=E)
            chain(tt(lg[:, :, :], lgs, rb[:, :].unsqueeze(1).to_broadcast([P, NB, E]), ALU.add))
            chain(ve.tensor_reduce(lmax[:, :], lg[:, :, :], AX.X, ALU.max))
            tt(lg[:, :, :], lg[:, :, :], lmax[:, :].unsqueeze(2).to_broadcast([P, NB, E]),
               ALU.subtract).then_inc(logits_shifted, 1)
            ve.wait_ge(exp_logits_done, 1)
            chain(ve.tensor_reduce(lsum[:, :], lg[:, :, :], AX.X, ALU.add))
            chain(ve.reciprocal(lsum[:, :], lsum[:, :]))
            chain(tt(scores[:, :, :].rearrange("p e b -> p b e"), lg[:, :, :],
                     lsum[:, :].unsqueeze(2).to_broadcast([P, NB, E]), ALU.mult))
            cp(rows[:, :, C:], scores[:, :, :].rearrange("p e b -> p b e")).then_inc(scores_ready, 1)

            ve.memset(thr[:, :], 0).then_inc(s_thr, 1)
            cp(cand[:, :, :], bits[:, 0, :, :]).then_inc(s_cand, 1)
            all_scores = scores[:, :, :].rearrange("p e b -> p b e").unsqueeze(2).to_broadcast([P, NB, CANDS, E])

            with ve.Fori(0, ROUNDS) as i:
                bit = bits[:, bass.ds(i, 1), 0, :].to_broadcast([P, CANDS, E])
                nxt = bits[:, bass.ds(i + 1, 1), :, :].rearrange("p a j e -> p (a j) e")
                ve.wait_ge(s_cand, at(i, 1))
                for half in (0, NB // 2), (NB // 2, NB):
                    tt(reach[:, half[0]:half[1], :, :], all_scores[:, half[0]:half[1], :, :],
                       cand[:, :, :].bitcast(F32).unsqueeze(1).to_broadcast([P, NB // 2, CANDS, E]),
                       ALU.is_ge).then_inc(s_cmp, 1)
                ve.wait_ge(s_count, at(i, 1))
                ve.scalar_tensor_tensor(gain[:, :, :], front[:, 0:CANDS * E].rearrange("p (j e) -> p j e", e=E),
                                        float(CAP), bit, ALU.is_ge, ALU.mult).then_inc(s_gain, 1)
                ve.wait_ge(s_gain, at(i, 1))
                with nc.allow_low_precision(reason="GROUP bits of an integer, which float32 holds"):
                    ve.tensor_reduce(take[:, :], gain[:, :, :].rearrange("p j e -> p e j"), AX.X,
                                     ALU.add).then_inc(s_take, 1)
                ve.wait_ge(s_take, at(i, 1))
                tt(thr[:, :], thr[:, :], take[:, :], ALU.bitwise_or).then_inc(s_thr, 1)
                ve.wait_ge(s_thr, at(i, 2))
                tt(cand[:, :, :], thr[:, :].unsqueeze(1).to_broadcast([P, CANDS, E]), nxt,
                   ALU.bitwise_or).then_inc(s_cand, 1)

            def against(dst, op):
                return tt(dst, scores[:, :, :], thr[:, :].bitcast(F32).unsqueeze(2).to_broadcast([P, E, NB]), op)

            against(above[:, :, :], ALU.is_gt)
            against(eq[:, :, :], ALU.is_equal).then_inc(s_tie, 1)
            ve.wait_ge(s_tied, 1)
            def running(total, within):
                chain(cp(tot_sb[:, :, :], total))
                chain(ve.tensor_tensor_scan(flat(incl[:, :, :]), flat(seg[:, :, :]), flat(tot_sb[:, :, :]), 0.0,
                                            ALU.mult, ALU.add))
                chain(tt(incl[:, :, :], incl[:, :, :], tot_sb[:, :, :], ALU.subtract))
                chain(tt(rank[:, :, :], incl[:, :, :], within, ALU.add))

            def grid(t, i):
                return t[:, i * P:(i + 1) * P].rearrange("p (e b) -> p e b", e=E)

            chain(ve.tensor_reduce(cnt[:, :], grid(front, 0), AX.X, ALU.add))
            chain(ts(need[:, :], cnt[:, :], -1.0, float(CAP), ALU.mult, ALU.add))
            running(grid(front, 1), grid(front, 2))
            chain(tt(rank[:, :, :], rank[:, :, :], need[:, :].unsqueeze(2).to_broadcast([P, E, NB]), ALU.is_lt))
            chain(tt(rank[:, :, :], rank[:, :, :], eq[:, :, :], ALU.mult))
            tt(sel[:, :, :], rank[:, :, :], above[:, :, :], ALU.add).then_inc(s_chosen, 1)
            ve.wait_ge(s_chosen, 1)
            ve.wait_ge(s_prefix, 1)
            running(grid(qk_ps, 0), grid(qk_ps, 1))
            chain(tt(rank[:, :, :], rank[:, :, :], sel[:, :, :], ALU.mult))
            chain(ts(incl[:, :, :], sel[:, :, :], -1023.0, 1023.0, ALU.mult, ALU.add))
            chain(tt(slot[:, :, :], rank[:, :, :], incl[:, :, :], ALU.add))
            chain(ts(slot_lo_i[:, :, :], slot[:, :, :], P - 1, None, ALU.bitwise_and))
            chain(ts(slot_hi_i[:, :, :], slot[:, :, :], 7, None, ALU.logical_shift_right))
            chain(cp(slot_lo[:, :, :], slot_lo_i[:, :, :]))
            chain(cp(slot_hi[:, :, :], slot_hi_i[:, :, :]))
            chain(tt(hot_hi[:, :, :], flat(slot_hi[:, :, :]).unsqueeze(2).to_broadcast([P, E * NB, ST]),
                     iota_hi[:, :].unsqueeze(1).to_broadcast([P, E * NB, ST]), ALU.is_equal))
            for e in range(E):
                o = hot_hi[:, e * NB:(e + 1) * NB, :]
                x = tt(o, o, tok_id[:, :].unsqueeze(2).to_broadcast([P, NB, ST]), ALU.mult)
            x.then_inc(slots_ready, 1)
            ve.wait_ge(slots_ready, 1)

            def save_list(e):
                ve.wait_ge(list_ready, e + 1)
                cp(token_of[:, e, :], (front, qk_ps)[e % 2][:, 0:ST]).then_inc(list_saved, 1)

            for e in range(E):
                ve.wait_ge(list_ready, at(e, -1))
                tt(hot_lo[e % 2][:, :, :], slot_lo[:, e, :].unsqueeze(2).to_broadcast([P, NB, P]),
                   iota_lo[:, :].unsqueeze(1).to_broadcast([P, NB, P]), ALU.is_equal).then_inc(hot_ready, 1)
                if e:
                    save_list(e - 1)
            save_list(E - 1)

            def split_rows(e):
                for k in range(CT):
                    src = (tail if k else v_ps)[:, :]
                    ve.wait_ge(gT_ready, at(e * CT, k + 1))
                    ve.wait_ge(h1_ready, e * FT)
                    cp(gT[0][:, k, :], src).then_inc(gT_hi, 1)
                    ve.wait_ge(gT_hi, at(e * CT, k + 1))
                    tt(gT[1][:, k, :], src, gT[0][:, k, :], ALU.subtract).then_inc(gT_lo, 1)

            def split_hidden(e, f):
                ve.wait_ge(hid_hi, at(e * FT, f + 1))
                ve.wait_ge(relu_done, at(e * FT, f + 1))
                tt(hid[1][:, f, :], relu[:, f % 4, :], hid[0][:, f, :], ALU.subtract).then_inc(hid_lo, 1)

            def combine(e, p, t):
                ve.wait_ge(eo_ready, at(e * ST, t + 1))
                b2e = b2[:, bass.ds(e, 1), :].rearrange("p a c -> p (a c)")
                ve.wait_ge(contrib_ready, at(e * ST, t))
                ve.scalar_tensor_tensor(tmp[:, t % 2, :], out_bank[t][:, 0:C], 1.0 / WSCALE, b2e,
                                        ALU.mult, ALU.add).then_inc(s_eo, 1)
                ve.wait_ge(s_eo, at(e * ST, t + 1))
                ve.wait_ge(added, at(e * 64, 0))
                gate = got[p][:, t, C:].rearrange("p (a e) -> p a e", a=1)[:, 0, bass.ds(e, 1)]
                ts(contrib[:, t, :], tmp[:, t % 2, :], gate, None, ALU.mult).then_inc(contrib_ready, 1)

            def expert(e, p, last=False):
                for f in range(FT):
                    split_hidden(e, f)
                    if f in (1, 3) and not last:
                        split_quarter(at(e, 1), 1 - p, f // 2)
                if not last:
                    split_rows(at(e, 1))
                    split_quarter(at(e, 1), 1 - p, QUARTERS - 2)
                combine(e, p, 0)
                if not last:
                    split_quarter(at(e, 1), 1 - p, QUARTERS - 1)
                for t in range(1, ST):
                    combine(e, p, t)

            split_rows(0)
            expert(0, 0)
            expert(1, 1)
            with ve.Fori(2, E - 3, 2) as e:
                expert(e, 0)
                expert(e + 1, 1)
            expert(E - 2, 0)
            expert(E - 1, 1, last=True)

        @blk.scalar
        def _(sc):
            def copy(dst, src):
                return sc.activation(dst, src, ACT.Copy)

            def save_xT(b):
                sc.wait_ge(xhatT_ready, at(b, 1))
                sc.wait_ge(v_ready, b)
                copy(flat(xT[:, :, :]), front[:, 0:C]).then_inc(xhatT_saved, 1)

            def save_qk(b):
                sc.wait_ge(qk_ready, at(b, 1))
                sc.wait_ge(parts_ready, b)
                sc.wait_ge(q_lo, b)
                copy(qk[:, :, 0:DE], qk_ps[:, :].rearrange("p (h d) -> p h d", d=DH)[:, :, 0:DE]).then_inc(qkc_saved, 1)

            def high_v(b, p):
                sc.wait_ge(v_ready, at(b, 1))
                sc.wait_ge(pv_done, at(b, -1))
                copy(vv[p][:, 0, :, 0:DH], v_ps[:, 0:C].rearrange("p (h d) -> p h d", d=DH)).then_inc(v_hi, 1)

            def high_q(b):
                sc.wait_ge(rope_done, at(b, 1))
                sc.wait_ge(qkT_ready, b)
                copy(parts[:, 0:H, :].rearrange("p h (i d) -> p h i d", d=DH)[:, :, 0:3:2, :],
                     qk[:, 0:H, :].unsqueeze(2).to_broadcast([P, H, 2, DH])).then_inc(q_hi, 1)

            def save_kT(b, p):
                sc.wait_ge(qkT_ready, at(b, 1))
                sc.wait_ge(T_ready[1], at(b, -1))
                copy(kT[p][0:64, :, 0, :], qk_ps[0:64, :].bitcast(F16).rearrange("p (i k) -> p i k", i=HP))\
                    .then_inc(kT_even_saved, 1)

            def save_mT(b):
                sc.wait_ge(mT_ready, at(b, 1))
                sc.wait_ge(T_ready[1], b)
                copy(mT[:, :], mT_ps).then_inc(mT_saved, 1)

            def exp_high(b, half):
                sc.wait_ge(T_ready[half], at(b, 1))
                sc.wait_ge(pv_done, b)
                sc.activation(flat(ph[:, 0, 8 * half:8 * half + 8, :]), ring[half][:, :], ACT.Exp,
                              bias=lift[:, :]).then_inc(p_hi[half], 1)

            def exp(b, half):
                sc.wait_ge(T_ready[half], at(b, 1))
                sc.wait_ge(p_lo[half], b)
                sc.activation(flat(pT[:, 8 * half:8 * half + 8, :]), ring[half][:, :], ACT.Exp,
                              bias=lift[:, :]).then_inc(exp_done[half], 1)

            def save_ynT(b):
                sc.wait_ge(ynT_ready, at(b, 1))
                sc.wait_ge(attn_ready, b)
                copy(flat(ynT[:, :, :]), tail[:, 0:C]).then_inc(ynT_saved, 1)

            def save_x2T(b, p):
                sc.wait_ge(x2T_ready, at(b, 1))
                sc.wait_ge(logits_ready, at(b, -1))
                copy(flat(x2T[p][:, :, :]), (front, qk_ps)[p][:, 0:C]).then_inc(x2T_saved, 1)

            def step(b, p, has_front=True, has_tail=True):
                n, o = at(b, 1), at(b, -1)
                if has_front:
                    save_xT(n)
                save_mT(b)
                if has_front:
                    save_qk(n)
                    high_v(n, 1 - p)
                    high_q(n)
                exp_high(b, 0)
                exp(b, 0)
                if has_tail:
                    save_ynT(o)
                exp_high(b, 1)
                if has_front:
                    save_kT(n, 1 - p)
                exp(b, 1)

            for b in range(NB):
                sc.wait_ge(conv_ready, b + 1)
                copy(resid[:, b, :], (front, qk_ps)[b % 2][:, 0:C]).then_inc(h_saved, 1)
            for j in range(3):
                sc.wait_ge(weT_ready, j + 1)
                copy(weT[:, j, :, :].rearrange("p i c -> p (i c)"), weT_bank[j]).then_inc(weT_saved, 1)
            save_xT(0)
            sc.wait_ge(zeroed, 2)
            save_qk(0)
            high_v(0, 0)
            high_q(0)
            save_kT(0, 0)
            step(0, 0, has_tail=False)
            step(1, 1)
            with sc.Fori(2, NB - 3, 2) as b:
                step(b, 0)
                step(b + 1, 1)
            step(NB - 2, 0)
            step(NB - 1, 1, has_front=False)
            save_ynT(NB - 1)
            save_x2T(0, 0)
            save_x2T(1, 1)
            with sc.Fori(2, NB - 1, 2) as b:
                save_x2T(b, 0)
                save_x2T(b + 1, 1)
            sc.wait_ge(logits_shifted, 1)
            sc.activation(flat(lg[:, :, :]), flat(lg[:, :, :]), ACT.Exp).then_inc(exp_logits_done, 1)

            def rectify(e, p, f):
                if f == 0:
                    sc.wait_ge(bias_ready, at(e, 1))
                sc.wait_ge(h1_ready, at(e * FT, f + 1))
                h1, bias = ring[f % 4 // 2][:, (f % 2) * 512:(f % 2 + 1) * 512], b1e[p][:, f:f + 1]
                sc.wait_ge(eo_ready, at(e * ST, 0))
                sc.activation(hid[0][:, f, :], h1, ACT.Relu, bias=bias, scale=1.0 / WSCALE).then_inc(hid_hi, 1)
                if f >= 4:
                    sc.wait_ge(hid_lo, at(e * FT, f - 3))
                else:
                    sc.wait_ge(hid_lo, e * FT)
                sc.activation(relu[:, f % 4, :], h1, ACT.Relu, bias=bias, scale=1.0 / WSCALE).then_inc(relu_done, 1)

            def expert(e, p):
                for f in range(FT):
                    rectify(e, p, f)

            expert(0, 0)
            expert(1, 1)
            with sc.Fori(2, E - 1, 2) as e:
                expert(e, 0)
                expert(e + 1, 1)

        @blk.gpsimd
        def _(gp):
            def gather(e, p):
                gp.wait_ge(list_saved, e + 1)
                gp.wait_ge(got_in, e * 64)
                gp.wait_ge(contrib_ready, at(e * ST, -ST))
                gp.wait_ge(gT_ready, at(e * CT, -CT))
                for t in range(ST):
                    gp.indirect_dma_start(got[p][:, t, :], None, table,
                                          bass.IndirectOffsetOnAxis(ap=token_of[:, e, t:t + 1], axis=0)).then_inc(got_in, 16)

            def add(e, p, t):
                gp.wait_ge(contrib_ready, at(e * ST, t + 1))
                if t == 0:
                    gp.wait_ge(added, e * 64)
                gp.indirect_dma_start(out_rows, bass.IndirectOffsetOnAxis(ap=token_of[:, e, t:t + 1], axis=0),
                                      contrib[:, t, :], None, compute_op=ALU.add).then_inc(added, 16)

            def expert(e, p, last=False):
                if not last:
                    gather(at(e, 1), 1 - p)
                for t in range(ST):
                    add(e, p, t)

            for i in range(2):
                gp.memset(vv[i][:, :, :, :], 0.0)
            gp.memset(flat(parts[:, :, :]).bitcast(F32), 0.0)
            for i in range(2):
                gp.memset(kT[i][:, :, :, :].rearrange("p i j k -> p (i j k)").bitcast(F32), 0.0)
            gp.memset(mst[:, :], 0.0)
            gp.memset(spare_ve[:, :], 0.0)
            gp.memset(lift[:, :], LIFT)
            gp.memset(ones_bf[:, :], 1.0).then_inc(zeroed, 1)
            gp.wait_ge(zeroed, 1)
            for i in range(2):
                x = gp.memset(vv[i][:, 0, :, DH], VSCALE)
            x.then_inc(zeroed, 1)
            gp.wait_ge(ld_const, 16 * 14)
            gp.tensor_copy(ident_h[:, :], ident[:, :])
            gp.tensor_copy(ident_bf[:, :], ident[:, :])
            for i, dst in enumerate((mask_qk, mask_kq, lower)):
                gp.tensor_copy(dst[:, :], raw[:, i, :])
            gp.tensor_tensor(pick[:, :, :], ident[:, 0:H].unsqueeze(2).to_broadcast([P, H, P]),
                             ident[:, H:2 * H].unsqueeze(2).to_broadcast([P, H, P]), ALU.add).then_inc(bf_ready, 1)

            gp.wait_ge(table_in, 16)
            gather(0, 0)
            gp.wait_ge(resid_out, 16 * NB)
            for e in range(E):
                expert(e, e % 2, last=e == E - 1)


def constants():
    i = np.arange(P)
    eye = np.eye(P, dtype=np.float32)
    later = i[None, :] > i[:, None]
    inv = (np.float32(1.0) / np.float32(10000.0) ** (np.arange(0, DE, 2, dtype=np.float32) / np.float32(DE))).astype(np.float32)
    ang = np.arange(T, dtype=np.float32)[:, None] * np.concatenate([inv, inv])[None, :]
    cos, sin = np.cos(ang).astype(np.float32), np.sin(ang).astype(np.float32)
    sin[:, 0::2] *= -1.0
    seg = np.ones((P, E, NB), np.float32)
    seg[:, :, 0] = 0.0
    bits = np.zeros((P, ROUNDS + 1, CANDS, E), np.int32)
    for r in range(ROUNDS):
        for j in range(CANDS):
            bits[:, r, j, :] = (j + 1) << (GROUP * (ROUNDS - 1 - r))
    return {
        "ident": eye,
        "mask_qk": np.where(later, np.float32(MASKED), np.float32(0)),
        "mask_kq": np.where(later.T, np.float32(MASKED), np.float32(0)),
        "cos": np.tile(cos, (1, 2 * H)), "sin": np.tile(sin, (1, 2 * H)),
        "lower": later.astype(np.float32),
        "iota_lo": np.tile(i.astype(np.float16), (P, 1)),
        "iota_hi": np.tile(np.arange(ST, dtype=np.float16), (P, 1)),
        "tok_id": (np.arange(NB)[None, :] * P + i[:, None]).astype(np.float32),
        "seg": seg.reshape(P, -1), "bits": bits.reshape(P, -1),
    }


def kernel(**inputs):
    import concourse.bacc as _bacc
    from concourse.bass_utils import run_bass_kernel_spmd as _run

    g = {k: np.ascontiguousarray(v) for k, v in inputs.items()}
    x, we, be = g["x"], g["L0_tok_W_embed"], g["L0_tok_b_embed"]
    xp = np.zeros((NB, CIN, x.shape[2] + TAPS - 1), x.dtype)
    xp[:, :, TAPS // 2:TAPS // 2 + x.shape[2]] = x
    xwin = np.stack([xp[:, c, j:j + DS * C:DS] for c in range(CIN) for j in range(WIN)]
                    + [np.ones((NB, C), x.dtype)] * 2)
    band = np.zeros((DS * CMID, KWIN + 1), we.dtype)
    for i in range(DS):
        for c in range(CIN):
            band[i * CMID:(i + 1) * CMID, c * WIN + i:c * WIN + i + TAPS] = we[:, c, :]
        band[i * CMID:(i + 1) * CMID, KWIN] = be
    up = np.zeros((P, 3, 4, P), np.float32)
    ups = [np.concatenate([g["L0_attn_Wq_up_c"], g["L0_attn_Wq_up_e"]], 1),
           np.concatenate([g["L0_attn_Wk_up_c"], g["L0_attn_Wk_up_e"]], 1), g["L0_attn_Wv_up"]]
    for j in range(3):
        for pair in range(4):
            for i in range(2):
                up[i * L:(i + 1) * L, j, pair, (2 * pair + i) * DH:(2 * pair + i + 1) * DH] = ups[j]
    arrays = {
        "xwin": xwin.reshape(KX, NB * C), "band": band,
        "wpT": np.ascontiguousarray(g["L0_tok_W_proj"][:, :, 0].T), "bp": g["L0_tok_b_proj"],
        "wdT": np.concatenate([g["L0_attn_Wq_down"].T, g["L0_attn_Wk_down"].T, g["L0_attn_Wv_down"].T]),
        "up": up.reshape(P, -1), "wc": g["L0_attn_Wc"], "wr": g["L0_ffn_router_w"], "rb": g["L0_ffn_router_b"],
        "w1": g["L0_ffn_w1"], "b1": g["L0_ffn_b1"].reshape(E, FT, P).transpose(2, 0, 1).reshape(P, E * FT), "w2": g["L0_ffn_w2"], "b2": g["L0_ffn_b2"],
        **constants(),
    }
    arrays = {k: np.ascontiguousarray(v) for k, v in arrays.items()}
    nc = _bacc.Bacc("TRN2", target_bir_lowering=False, num_devices=1)
    a = {k: nc.dram_tensor(f"in_{k}", v.shape, mybir.dt.from_np(v.dtype), kind="ExternalInput").ap()
         for k, v in arrays.items()}
    out = nc.dram_tensor("out_0", (NB, T, C), F32, kind="ExternalOutput").ap()
    table = nc.dram_tensor("token_rows", (NB * T, ROW), F32, kind="Internal").ap()
    build(nc, a, out, table)
    r = _run(nc, [{f"in_{k}": v for k, v in arrays.items()}], core_ids=[0])
    return r.results[0]["out_0"]
```

```python
from contextlib import ExitStack

import numpy as np

import concourse.bass as bass
from concourse import mybir

F32 = mybir.dt.float32
F16 = mybir.dt.float16
BF16 = mybir.dt.bfloat16
I32 = mybir.dt.int32
U32 = mybir.dt.uint32
ALU = mybir.AluOpType
ACT = mybir.ActivationFunctionType
AX = mybir.AxisListType

P = 128
NB, T, C = 16, 128, 256
H, L, DH = 16, 64, 16
DE = DH // 2
CIN, TAPS, DS, CMID = 2, 7, 16, 32
WIN = DS + TAPS - 1
KWIN = CIN * WIN
KX = KWIN + 2
E, FF, CAP = 8, 1024, 512
FT, CT, ST = FF // P, C // P, CAP // P
SLOT, HP = 64, H // 2
GROUP = 3
CANDS = 2 ** GROUP - 1
FIRST = 10
ROUNDS = 10
ROW = C + E
EPS = 1e-5
SEED, NEWTON = float(0x5F3759DF), 3
ROOT_OPS = 2 + 4 * NEWTON
LATE = 2
QUARTERS = 4
DSCALE = 64.0
QKSCALE = 64.0
VSCALE = 64.0
LIFT = 7.0
WSCALE = 64.0
MASKED = -1e30


def at(base, n):
    return max(base + n, 0) if isinstance(base, int) else base + n if n else base


def build(nc, a, out, table):
    with ExitStack() as ctx:
        def sb(name, shape, dt=F32):
            return ctx.enter_context(nc.sbuf_tensor(name, shape, dt))

        def sem(name):
            return ctx.enter_context(nc.semaphore(name))

        front = ctx.enter_context(nc.psum_tensor("front", [P, 512], F32))
        qk_ps = ctx.enter_context(nc.psum_tensor("qk_ps", [P, 512], F32))
        v_ps = ctx.enter_context(nc.psum_tensor("v_ps", [P, 512], F32))
        ring = [ctx.enter_context(nc.psum_tensor(f"ring{i}", [P, 1024], F32)) for i in range(2)]
        tail = ctx.enter_context(nc.psum_tensor("tail", [P, 512], F32))
        out_bank = [front, qk_ps, ring[1][:, 512:1024], ring[1][:, 0:512]]
        mT_ps = front[:, 256:320].bitcast(BF16)

        ident = sb("ident", [P, P])
        ident_bf = sb("ident_bf", [P, P], BF16)
        ident_h = sb("ident_h", [P, P], F16)
        mask_qk = sb("mask_qk", [P, P], BF16)
        mask_kq = sb("mask_kq", [P, P], BF16)
        pick = sb("pick", [P, H, P], BF16)
        raw = sb("raw", [P, 3, P])
        cos_t = sb("cos_t", [P, 2 * H, DE])
        sin_t = sb("sin_t", [P, 2 * H, DE])
        lower = sb("lower", [P, P], BF16)
        ones_bf = sb("ones_bf", [P, P], BF16)
        iota_lo = sb("iota_lo", [P, P], F16)
        iota_hi = sb("iota_hi", [P, ST], F16)
        tok_id = sb("tok_id", [P, NB])
        seg = sb("seg", [P, 2 * E, NB])
        bits = sb("bits", [P, ROUNDS + 1, CANDS, E], I32)
        xwin = sb("xwin", [P, NB * C])
        band = sb("band", [P, 4, KWIN + 1])
        wpT = sb("wpT", [P, 4, P])
        weffT = sb("weffT", [64, P])
        stage = sb("stage", [P, 24 * C])
        wdT = stage[:, :].rearrange("p (j c) -> p j c", c=C)
        wqkv = sb("wqkv", [P, 2, CT, 3 * C], F16)
        wc = sb("wc", [P, CT, C])
        wr = sb("wr", [P, CT, E])
        rb = sb("rb", [P, E])
        b1 = sb("b1", [P, E, FT])
        b2 = sb("b2", [P, E, C])

        resid = sb("resid", [P, NB, C])
        scores = sb("scores", [P, E, NB])
        st6 = sb("st6", [P, NB, 6])
        mv = sb("mv", [P, NB, 2])
        var = sb("var", [P, NB])
        rstd = sb("rstd", [P, NB])
        newton = sb("newton", [P, NB])
        xhat = sb("xhat", [P, C])
        xT = sb("xT", [P, 2, CT, P], F16)
        qk = sb("qk", [P, 2 * H, DH])
        parts = sb("parts", [P, 2 * H, SLOT], F16)
        rot1 = sb("rot1", [P, 2 * H, DE])
        rot2 = sb("rot2", [P, 2 * H, DE])
        qT = [sb(f"qT{i}", [P, HP, P], F16) for i in range(2)]
        kT = [sb(f"kT{i}", [P, HP, 2, P], F16) for i in range(2)]
        vv = [sb(f"vv{i}", [P, 2, H, DH + 1], F16) for i in range(2)]
        negmax = sb("negmax", [P, H])
        mst = sb("mst", [P, P], BF16)
        mT = sb("mT", [P, P], BF16)
        pT = sb("pT", [P, H, P])
        ph = sb("ph", [P, 2, H, P], F16)
        lift = sb("lift", [P, 1])
        rden = sb("rden", [P, H])
        yn = sb("yn", [P, H, DH])
        ynT = sb("ynT", [P, CT, P])
        x2 = [sb(f"x2_{i}", [P, 2, C]) for i in range(2)]
        x2T = [sb(f"x2T{i}", [P, 2, 2, CT, P], F16) for i in range(2)]
        wr_parts = sb("wr_parts", [P, 2, CT, E], F16)
        rows = sb("rows", [P, NB, ROW])
        lg = sb("lg", [P, NB, E])
        lmax = sb("lmax", [P, NB])
        lsum = sb("lsum", [P, NB])

        thr = sb("thr", [P, E], I32)
        cand = sb("cand", [P, CANDS, E], I32)
        reach = sb("reach", [P, NB, CANDS, E], BF16)
        base = sb("base", [P, CANDS, E], I32)
        gain = sb("gain", [P, CANDS, E])
        take = sb("take", [P, E], I32)
        cls = sb("cls", [P, 2 * E, NB], BF16)
        cnt = sb("cnt", [P, E])
        need = sb("need", [P, E])
        tot_sb = sb("tot_sb", [P, 2 * E, NB])
        before = sb("before", [P, 2 * E, NB])
        tie_ok = sb("tie_ok", [P, E, NB])
        rank = sb("rank", [P, E, NB])
        off = sb("off", [P, E, NB])
        sel = sb("sel", [P, E, NB], BF16)
        slot = sb("slot", [P, E, NB], I32)
        slot_lo_i = sb("slot_lo_i", [P, E, NB], I32)
        slot_hi_i = sb("slot_hi_i", [P, E, NB], I32)
        slot_lo = sb("slot_lo", [P, E, NB], F16)
        slot_hi = sb("slot_hi", [P, E, NB])
        hot_hi = [sb(f"hot_hi{i}", [P, NB, ST], F16) for i in range(2)]
        hot_lo = [ph[:, i] for i in range(2)]
        token_of = sb("token_of", [P, E, ST], U32)

        w1s = stage[:, 0:2048].rearrange("p (k f) -> p k f", k=CT)
        w2s = stage[:, 2048:4096].rearrange("p (f c) -> p f c", f=FT)
        wh = [sb(f"wh{i}", [P, 4, 2048], F16) for i in range(2)]
        W = [[wh[i][:, j, :] for j in range(4)] for i in range(2)]
        W1 = [[w.rearrange("p (k f) -> p k f", k=CT) for w in W[i][0:2]] for i in range(2)]
        W2 = [[w.rearrange("p (f c) -> p f c", f=FT) for w in W[i][2:4]] for i in range(2)]
        hid_all = xwin[:, :].bitcast(F16).rearrange("p (i f s) -> p i f s", i=2, f=FT)
        hid = [hid_all[:, i] for i in range(2)]
        relu = pT[:, :, :].rearrange("p h q -> p (h q)").rearrange("p (i s) -> p i s", i=4)
        got = [sb(f"got{i}", [P, ST, ROW]) for i in range(2)]
        gT = [kT[0][:, 4 * i:4 * i + 4, :, :].rearrange("p i j k -> p (i j k)").rearrange("p (k s) -> p k s", k=CT)
              for i in range(2)]
        tmp = qT[0][:, :, :].rearrange("p i k -> p (i k)").bitcast(F32).rearrange("p (i c) -> p i c", i=2)
        contrib = parts[:, :, :].rearrange("p h s -> p (h s)").bitcast(F32).rearrange("p (t c) -> p t c", t=ST)
        spare_ve = sb("spare_ve", [1, 1])
        b1e = [sb(f"b1e{i}", [P, FT]) for i in range(2)]

        up = pT[:, 0, 0:3 * 2 * DH].rearrange("p (j m) -> p j m", j=3)
        up_parts = pT[:, 1:3, :].rearrange("p i m -> p (i m)").bitcast(F16)[:, 0:3 * 4 * DH]\
            .rearrange("p (i j m) -> p i j m", i=2, j=3)
        wd_parts = [wh[i][:, :, :].rearrange("p i w -> p (i w)")[:, 0:24 * C].rearrange("p (j c) -> p j c", c=C)
                    for i in range(2)]
        eff_scale = [x / DSCALE ** 2 for x in (QKSCALE * DH ** -0.5, QKSCALE, VSCALE)]
        eff_bank = [v_ps, tail, ring[1][:, 512:1024]]

        bias_ready = sem("bias_ready")
        ld_const = sem("ld_const")
        ld_w = sem("ld_w")
        ld_x = sem("ld_x")
        ld_bias = sem("ld_bias")
        ld_up = sem("ld_up")
        ld_down = [sem(f"ld_down_{i}") for i in "qkv"]
        zeroed = sem("zeroed")
        weff_ready = sem("weff_ready")
        weff_saved = sem("weff_saved")
        bp_in = sem("bp_in")
        up_hi = sem("up_hi")
        up_lo = sem("up_lo")
        wd_hi = sem("wd_hi")
        wd_lo = sem("wd_lo")
        eff_ready = sem("eff_ready")
        eff_hi = sem("eff_hi")
        eff_saved = sem("eff_saved")
        bf_ready = sem("bf_ready")
        conv_ready = sem("conv_ready")
        h_saved = sem("h_saved")
        s_stats = sem("s_stats")
        s_stats2 = sem("s_stats2")
        s_root = sem("s_root")
        first_stats = sem("first_stats")
        first_root = sem("first_root")
        late_stats = sem("late_stats")
        late_root = sem("late_root")
        xhat_ready = sem("xhat_ready")
        xhatT_ready = sem("xhatT_ready")
        xT_hi = sem("xT_hi")
        xT_lo = sem("xT_lo")
        qk_ready = sem("qk_ready")
        v_ready = sem("v_ready")
        qkc_saved = sem("qkc_saved")
        v_hi = sem("v_hi")
        v_lo = sem("v_lo")
        s_rot1 = sem("s_rot1")
        s_rot2 = sem("s_rot2")
        rope_done = sem("rope_done")
        q_hi = sem("q_hi")
        k_hi = sem("k_hi")
        q_lo = sem("q_lo")
        parts_ready = sem("parts_ready")
        qkT_ready = sem("qkT_ready")
        kT_even_saved = sem("kT_even_saved")
        kT_odd_saved = sem("kT_odd_saved")
        qT_saved = sem("qT_saved")
        s_mhi = sem("s_mhi")
        mst_ready = sem("mst_ready")
        mT_ready = sem("mT_ready")
        mT_saved = sem("mT_saved")
        s_rden = sem("s_rden")
        yn_ready = sem("yn_ready")
        ynT_ready = sem("ynT_ready")
        ynT_saved = sem("ynT_saved")
        attn_ready = sem("attn_ready")
        h2_ready = sem("h2_ready")
        x2_ready = sem("x2_ready")
        x2T_ready = sem("x2T_ready")
        rows_ready = sem("rows_ready")
        wr_hi = sem("wr_hi")
        wr_lo = sem("wr_lo")
        x2T_hi = sem("x2T_hi")
        x2T_lo = sem("x2T_lo")
        logits_ready = sem("logits_ready")
        logits_shifted = sem("logits_shifted")
        exp_logits_done = sem("exp_logits_done")
        scores_ready = sem("scores_ready")
        table_in = sem("table_in")
        resid_out = sem("resid_out")
        s_cmp = sem("s_cmp")
        s_count = sem("s_count")
        s_base = sem("s_base")
        s_gain = sem("s_gain")
        s_take = sem("s_take")
        s_cand = sem("s_cand")
        s_thr = sem("s_thr")
        s_tie = sem("s_tie")
        s_tied = sem("s_tied")
        s_chain = sem("s_chain")
        hot_hi_ready = sem("hot_hi_ready")
        hot_ready = sem("hot_ready")
        list_ready = sem("list_ready")
        list_saved = sem("list_saved")
        w1_in = sem("w1_in")
        w2_in = sem("w2_in")
        wsplit_hi = sem("wsplit_hi")
        wsplit_lo = sem("wsplit_lo")
        got_in = sem("got_in")
        gT_ready = sem("gT_ready")
        gT_hi = sem("gT_hi")
        gT_lo = sem("gT_lo")
        h1_ready = sem("h1_ready")
        relu_done = sem("relu_done")
        hid_hi = sem("hid_hi")
        hid_lo = sem("hid_lo")
        eo_ready = sem("eo_ready")
        s_eo = sem("s_eo")
        contrib_ready = sem("contrib_ready")
        added = sem("added")
        S_ready = [sem("S_ready_lo"), sem("S_ready_hi")]
        T_ready = [sem("T_ready_lo"), sem("T_ready_hi")]
        row_maxed = [sem("row_maxed_lo"), sem("row_maxed_hi")]
        pv_done = [sem("pv_done_lo"), sem("pv_done_hi")]
        p_hi = [sem("p_hi_lo"), sem("p_hi_hi")]
        p_lo = [sem("p_lo_lo"), sem("p_lo_hi")]
        exp_done = [sem("exp_done_lo"), sem("exp_done_hi")]

        def take_wait(e, spare):
            e.tensor_tensor(spare, spare, spare, ALU.mult)

        def quarter(p, i):
            part, side = divmod(i, 2)
            cols = slice(1024 * side, 1024 * (side + 1))
            return stage[:, 2048 * part:2048 * (part + 1)][:, cols], W[p][2 * part][:, cols], W[p][2 * part + 1][:, cols]

        def inverse_roots(e, done, first, cols):
            v, y, t = var[:, cols], rstd[:, cols], newton[:, cols]
            e.tensor_scalar(v, mv[:, cols, 1], EPS, None, ALU.add).then_inc(done, 1)
            e.wait_ge(done, first + 1)
            e.tensor_scalar(y.bitcast(I32), v.bitcast(I32), -0.5, SEED, ALU.mult, ALU.add).then_inc(done, 1)
            e.wait_ge(done, first + 2)
            for n in range(NEWTON):
                e.tensor_tensor(t, y, y, ALU.mult).then_inc(done, 1)
                e.wait_ge(done, first + 4 * n + 3)
                e.tensor_tensor(t, t, v, ALU.mult).then_inc(done, 1)
                e.wait_ge(done, first + 4 * n + 4)
                e.tensor_scalar(t, t, -0.5, 1.5, ALU.mult, ALU.add).then_inc(done, 1)
                e.wait_ge(done, first + 4 * n + 5)
                e.tensor_tensor(y, y, t, ALU.mult).then_inc(done, 1)
                e.wait_ge(done, first + 4 * n + 6)

        def low_p(e, b, half):
            e.wait_ge(p_hi[half], at(b, 1))
            e.wait_ge(exp_done[half], at(b, 1))
            h = slice(8 * half, 8 * half + 8)
            e.tensor_tensor(ph[:, 1, h, :], pT[:, h, :], ph[:, 0, h, :], ALU.subtract).then_inc(p_lo[half], 1)

        out_rows = out.rearrange("b t c -> (b t) c")

        def flat(t):
            return t.rearrange("p a b -> p (a b)")

        blk = ctx.enter_context(nc.Block())

        @blk.sync
        def _(sp):
            def ld(dst, src, done):
                sp.dma_start(dst, src).then_inc(done, 16)

            ld(band[:, :, :], a["band"].rearrange("(s p) j -> p s j", p=P), ld_w)
            ld(wpT[:, :, :], a["wpT"].rearrange("(s p) o -> p s o", p=P), ld_w)
            ld(weffT[KX - 1:KX, :], a["bp"].rearrange("(a o) -> a o", a=1), bp_in)
            ld(xwin[0:KX, :], a["xwin"], ld_x)
            ld(pT[:, 0, 0:3 * 2 * DH], a["up"], ld_up)
            for j in range(3):
                ld(wdT[:, 8 * j:8 * j + 8, :], a["wdT"][j * 8 * P:(j + 1) * 8 * P].rearrange("(j p) c -> p j c", p=P),
                   ld_down[j])
            for dst, n in [(ident[:, :], "ident"), (raw[:, 0, :], "mask_qk"), (raw[:, 1, :], "mask_kq"),
                           (raw[:, 2, :], "lower"),
                           (flat(cos_t[:, :, :]), "cos"), (flat(sin_t[:, :, :]), "sin"),
                           (iota_lo[:, :], "iota_lo"), (iota_hi[:, :], "iota_hi"), (tok_id[:, :], "tok_id"),
                           (flat(seg[:, :, :]), "seg"), (bits[:, :, :, :].rearrange("p r j e -> p (r j e)"), "bits")]:
                ld(dst, a[n], ld_const)
            ld(wc[:, :, :], a["wc"].rearrange("(k p) c -> p k c", p=P), ld_const)
            ld(wr[:, :, :], a["wr"].rearrange("(k p) e -> p k e", p=P), ld_const)
            ld(rb[:, :], a["rb"].partition_broadcast(P), ld_const)
            ld(flat(b1[:, :, :]), a["b1"], ld_bias)
            ld(b2[:, :, :], a["b2"].partition_broadcast(P), ld_bias)
            sp.wait_ge(wd_lo, 12)
            sp.dma_start(w1s, a["w1"][0].rearrange("(k p) f -> p k f", p=P)).then_inc(w1_in, 16)
            sp.dma_start(w2s, a["w2"][0].rearrange("(f p) c -> p f c", p=P)).then_inc(w2_in, 16)
            with sp.Fori(0, NB) as b:
                sp.wait_ge(h2_ready, at(b, 1))
                sp.dma_start(out_rows[bass.ds(b * P, P), :], resid[:, bass.ds(b, 1), :]).then_inc(resid_out, 16)
            sp.wait_ge(rows_ready, 1)
            sp.wait_ge(scores_ready, 1)
            sp.dma_start(table.rearrange("(b p) r -> p b r", p=P), rows[:, :, :]).then_inc(table_in, 16)

            def weights(e):
                sp.wait_ge(wsplit_lo, e * QUARTERS)
                sp.dma_start(w1s, a["w1"][bass.ds(e, 1)].rearrange("a (k p) f -> p (a k) f", p=P)).then_inc(w1_in, 16)
                sp.dma_start(w2s, a["w2"][bass.ds(e, 1)].rearrange("a (f p) c -> p (a f) c", p=P)).then_inc(w2_in, 16)

            with sp.Fori(1, E) as e:
                weights(e)
            sp.wait_ge(resid_out, 16 * NB)
            sp.wait_ge(table_in, 16)
            sp.wait_ge(added, 16 * ST * E)

        @blk.tensor
        def _(pe):
            mm, tr = pe.matmul, pe.transpose

            pe.wait_ge(ld_w, 32)
            for i in range(4):
                x = mm(front[0:KWIN + 1, 0:P], band[:, i, :], wpT[:, i, :], start=i == 0, stop=i == 3)
            x.then_inc(weff_ready, 1)
            pe.wait_ge(weff_saved, 1)
            pe.wait_ge(ld_x, 16)
            pe.wait_ge(bp_in, 16)
            for b in range(NB):
                pe.wait_ge(h_saved, at(b, -1))
                mm((front, qk_ps)[b % 2][:, 0:C], weffT[0:KX, :], xwin[0:KX, b * C:(b + 1) * C],
                   start=True, stop=True).then_inc(conv_ready, 1)
            pe.wait_ge(up_lo, 1)
            for j in range(3):
                pe.wait_ge(wd_lo, 4 * (j + 1))
                for k in range(CT):
                    for i in range(8):
                        o = eff_bank[j][:, k * C + 2 * DH * i:k * C + 2 * DH * (i + 1)]
                        w = [part[:, 8 * j + i, k * P:(k + 1) * P] for part in wd_parts]
                        mm(o, w[0], up_parts[:, 0, j, :], start=True, stop=False)
                        mm(o, w[0], up_parts[:, 1, j, :], start=False, stop=False)
                        x = mm(o, w[1], up_parts[:, 0, j, :], start=False, stop=True)
                x.then_inc(eff_ready, 1)
            pe.wait_ge(eff_saved, 3)
            pe.wait_ge(ld_const, 16 * 14)
            pe.wait_ge(h_saved, NB)

            def xhat_t(b):
                pe.wait_ge(xhat_ready, at(b, 1))
                pe.wait_ge(qT_saved, 2 * b)
                for k in range(CT):
                    x = tr(front[:, k * P:(k + 1) * P], xhat[:, k * P:(k + 1) * P], ident[:, :])
                x.then_inc(xhatT_ready, 1)

            split_terms = [(i, j, k) for i, j in ((0, 0), (0, 1), (1, 0)) for k in range(CT)]

            def project(o, b, cols):
                for n, (i, j, k) in enumerate(split_terms):
                    if n == 2 * CT:
                        pe.wait_ge(xT_lo, at(b, 1))
                    x = mm(o, xT[:, i, k, :], wqkv[:, j, k, cols], start=n == 0, stop=n == len(split_terms) - 1)
                return x

            def qk(b):
                pe.wait_ge(xT_hi, at(b, 1))
                pe.wait_ge(kT_even_saved, 2 * b)
                pe.wait_ge(kT_odd_saved, 2 * b)
                project(qk_ps[:, :], b, slice(0, 2 * C)).then_inc(qk_ready, 1)

            def v(b):
                pe.wait_ge(v_lo, b)
                project(v_ps[:, 0:C], b, slice(2 * C, 3 * C)).then_inc(v_ready, 1)

            def qk_t(b):
                pe.wait_ge(parts_ready, at(b, 1))
                pe.wait_ge(q_lo, at(b, 1))
                split = flat(parts[:, :, :])
                for bank, first in ((front, 0), (qk_ps, HP)):
                    o = bank[:, :].bitcast(F16)
                    for i in range(HP):
                        x = tr(o[:, i * P:(i + 1) * P], split[:, (first + i) * P:(first + i + 1) * P], ident_h[:, :])
                x.then_inc(qkT_ready, 1)

            def scores_for_max(b, p, half):
                pe.wait_ge(exp_done[half], b)
                pe.wait_ge(kT_even_saved, at(2 * b, half + 1))
                pe.wait_ge(kT_odd_saved, at(2 * b, half + 1))
                pe.wait_ge(qT_saved, at(2 * b, half + 1))
                for c in range(2):
                    o = ring[half][:, c * 512:(c + 1) * 512]
                    for j in range(2):
                        i = 4 * half + 2 * c + j
                        mm(o[:, j * 2 * P:(j + 1) * 2 * P], qT[p][:, i, :], flat(kT[p][:, i, :, :]),
                           start=j == 0, stop=False, skip_group_check=True)
                    x = mm(o.rearrange("q (h k) -> q h k", h=4), ident_bf[:, :],
                           mask_qk[:, :].unsqueeze(1).to_broadcast([P, 4, P]), start=False, stop=True,
                           skip_group_check=True)
                x.then_inc(S_ready[half], 1)

            def max_t(b):
                pe.wait_ge(mst_ready, at(b, 1))
                tr(mT_ps, mst[:, :], ident_bf[:, :]).then_inc(mT_ready, 1)

            def scores_t(b, p, half):
                if not half:
                    pe.wait_ge(mT_saved, at(b, 1))
                pe.wait_ge(row_maxed[half], at(b, 1))
                for c in range(2):
                    o = ring[half][:, c * 512:(c + 1) * 512]
                    for j in range(4):
                        i = 4 * half + 2 * c + j // 2
                        mm(o[:, j * P:(j + 1) * P], kT[p][:, i, j % 2, :], qT[p][:, i, :],
                           start=j == 0, stop=False, skip_group_check=True)
                    for j in range(4):
                        mm(o[:, j * P:(j + 1) * P], pick[:, 8 * half + 4 * c + j, :], mT[:, :],
                           start=False, stop=False, skip_group_check=True)
                    x = mm(o.rearrange("q (h k) -> q h k", h=4), ident_bf[:, :],
                           mask_kq[:, :].unsqueeze(1).to_broadcast([P, 4, P]), start=False, stop=True,
                           skip_group_check=True)
                x.then_inc(T_ready[half], 1)

            def values(b, p, half):
                pe.wait_ge(p_lo[half], at(b, 1))
                pe.wait_ge(v_lo, at(b, 1))
                pe.wait_ge(h2_ready, b)
                for h in range(8 * half, 8 * half + 8):
                    o = tail[:, 32 * h:32 * h + DH + 1]
                    mm(o, ph[:, 0, h, :], vv[p][:, 0, h, :], start=True, stop=False)
                    mm(o, ph[:, 0, h, :], vv[p][:, 1, h, :], start=False, stop=False)
                    x = mm(o, ph[:, 1, h, :], vv[p][:, 0, h, :], start=False, stop=True)
                x.then_inc(pv_done[half], 1)

            def yn_t(b):
                pe.wait_ge(yn_ready, at(b, 1))
                ynf = flat(yn[:, :, :])
                for k in range(CT):
                    x = tr(tail[:, k * P:(k + 1) * P], ynf[:, k * P:(k + 1) * P], ident[:, :])
                x.then_inc(ynT_ready, 1)

            def out_proj(b):
                pe.wait_ge(ynT_saved, at(b, 1))
                for k in range(CT):
                    x = mm(tail[:, C:2 * C], ynT[:, k, :], wc[:, k, :], start=k == 0, stop=k == CT - 1)
                x.then_inc(attn_ready, 1)

            def x2_t(g, p):
                pe.wait_ge(x2_ready, at(g, 1))
                pe.wait_ge(x2T_lo, at(g, -1))
                for i in range(2 * CT):
                    x = tr((front, qk_ps)[p][:, i * P:(i + 1) * P], flat(x2[p][:, :, :])[:, i * P:(i + 1) * P], ident[:, :])
                x.then_inc(x2T_ready, 1)

            def router(g, p):
                pe.wait_ge(x2T_hi, at(g, 1))
                pe.wait_ge(x2T_lo, at(g, 1))
                for b in range(2):
                    for n, (i, j, k) in enumerate(split_terms):
                        x = mm(v_ps[:, bass.ds((2 * g + b) * E, E)], x2T[p][:, i, b, k, :], wr_parts[:, j, k, :],
                               start=n == 0, stop=n == len(split_terms) - 1)
                x.then_inc(logits_ready, 1)

            def step(b, p, has_front=True, has_tail=True):
                n, o = at(b, 1), at(b, -1)
                scores_for_max(b, p, 0)
                if has_front:
                    xhat_t(n)
                scores_for_max(b, p, 1)
                if has_tail:
                    values(o, 1 - p, 0)
                if has_front:
                    qk(n)
                if has_front:
                    v(n)
                max_t(b)
                if has_tail:
                    values(o, 1 - p, 1)
                scores_t(b, p, 0)
                scores_t(b, p, 1)
                if has_tail:
                    yn_t(o)
                if has_front:
                    qk_t(n)
                if has_tail:
                    out_proj(o)

            xhat_t(0)
            qk(0)
            v(0)
            pe.wait_ge(bf_ready, 1)
            qk_t(0)
            step(0, 0, has_tail=False)
            step(1, 1)
            with pe.Fori(2, NB - 3, 2) as b:
                step(b, 0)
                step(b + 1, 1)
            step(NB - 2, 0)
            step(NB - 1, 1, has_front=False)
            values(NB - 1, 1, 0)
            values(NB - 1, 1, 1)
            yn_t(NB - 1)
            x2_t(0, 0)
            out_proj(NB - 1)

            pe.wait_ge(wr_lo, 1)
            x2_t(1, 1)
            router(0, 0)
            with pe.Fori(2, NB // 2 - 1, 2) as g:
                x2_t(g, 0)
                router(g - 1, 1)
                x2_t(g + 1, 1)
                router(g, 0)
            router(NB // 2 - 1, 1)

            for i in range(ROUNDS):
                for b in range(NB):
                    if b in (0, FIRST):
                        pe.wait_ge(s_cmp, 2 * i + (1 if b == 0 else 2))
                    x = mm(front[:, 0:CANDS * E], ones_bf[:, :], flat(reach[:, b, :, :]), start=b == 0, stop=b == NB - 1)
                x.then_inc(s_count, 1)
            pe.wait_ge(s_tie, 1)
            mm(front[:, 0:2 * P], ones_bf[:, :], flat(cls[:, :, :]), start=True, stop=True)
            mm(front[:, 2 * P:4 * P], lower[:, :], flat(cls[:, :, :]), start=True, stop=True).then_inc(s_tied, 1)

            def token_list(e, p):
                pe.wait_ge(hot_ready, at(e, 1))
                for b in range(NB):
                    x = mm((front, qk_ps)[p][:, 0:ST], hot_lo[p][:, b, :], hot_hi[p][:, b, :], start=b == 0, stop=b == NB - 1)
                x.then_inc(list_ready, 1)

            token_list(0, 0)
            token_list(1, 1)

            def transpose_rows(e, p):
                pe.wait_ge(got_in, at(e * 64, 64))
                for k in range(CT):
                    pe.wait_ge(gT_lo, at(e * CT, k - 1) if k else e * CT)
                    for t in range(ST):
                        x = tr((tail if k else v_ps)[:, t * P:(t + 1) * P], got[p][:, t, k * P:(k + 1) * P], ident[:, :])
                    x.then_inc(gT_ready, 1)

            def hidden(e, p, f):
                if f == 0:
                    pe.wait_ge(gT_lo, at(e * CT, CT))
                    pe.wait_ge(wsplit_lo, at(e * QUARTERS, QUARTERS // 2))
                pe.wait_ge(relu_done, at(e * FT, f - 3))
                if f in (2, 3):
                    pe.wait_ge(s_eo, e * ST)
                o = ring[f % 4 // 2][:, (f % 2) * 512:(f % 2 + 1) * 512]
                for n, (i, j, k) in enumerate(split_terms):
                    x = mm(o, W1[p][i][:, k, f * P:(f + 1) * P], gT[j][:, k, :], start=n == 0,
                           stop=n == len(split_terms) - 1)
                x.then_inc(h1_ready, 1)

            def expert_out(e, p, t, lists):
                if t == 0:
                    pe.wait_ge(wsplit_lo, at(e * QUARTERS, QUARTERS))
                    pe.wait_ge(hid_hi, at(e * FT, FT - 1))
                    pe.wait_ge(list_saved, at(e, 3) if lists else E)
                    pe.wait_ge(s_eo, e * ST)
                if t == 2:
                    pe.wait_ge(relu_done, at(e * FT, FT))
                o = out_bank[t][:, 0:C]
                terms = [(i, j, f) for i, j in ((0, 0), (0, 1), (1, 0)) for f in range(FT)]
                for n, (i, j, f) in enumerate(terms):
                    if t == 0 and n == FT - 1:
                        pe.wait_ge(hid_hi, at(e * FT, FT))
                    if t == 0 and n == 2 * FT:
                        pe.wait_ge(hid_lo, at(e * FT, FT))
                    x = mm(o, hid[i][:, f, t * P:(t + 1) * P], W2[p][j][:, f, :], start=n == 0, stop=n == len(terms) - 1)
                x.then_inc(eo_ready, 1)

            def expert(e, p, last=False, lists=True):
                for f in range(FT):
                    hidden(e, p, f)
                    if f == 4 and lists:
                        pe.wait_ge(s_eo, e * ST)
                        token_list(at(e, 2), p)
                if not last:
                    transpose_rows(at(e, 1), 1 - p)
                for t in range(ST):
                    expert_out(e, p, t, lists)

            transpose_rows(0, 0)
            expert(0, 0)
            expert(1, 1)
            with pe.Fori(2, E - 3, 2) as e:
                expert(e, 0)
                expert(e + 1, 1)
            expert(E - 2, 0, lists=False)
            expert(E - 1, 1, last=True, lists=False)

        @blk.vector
        def _(ve):
            tt, ts, cp = ve.tensor_tensor, ve.tensor_scalar, ve.tensor_copy
            ve.wait_ge(weff_ready, 1)
            cp(weffT[0:KWIN + 1, :], front[0:KWIN + 1, 0:P]).then_inc(weff_saved, 1)

            def feat(b):
                return resid[:, bass.ds(b, 1), :].rearrange("p a c -> p (a c)")

            def stats(b, done):
                ve.wait_ge(h2_ready, at(b, 1))
                ve.wait_ge(done, b)
                take_wait(ve, spare_ve[:, :])
                ve.bn_stats(st6[:, bass.ds(b, 1), :].rearrange("p a s -> p (a s)"), feat(b)).then_inc(done, 1)

            def aggregate(batches, done, count):
                for b in batches:
                    x = ve.bn_aggr(mv[:, b, :], st6[:, b, :])
                x.then_inc(done, 1)
                ve.wait_ge(done, count)

            def low_eff(j):
                ve.wait_ge(eff_hi, j + 1)
                cols = slice(j * C, (j + 1) * C)
                ve.scalar_tensor_tensor(wqkv[:, 1, :, cols], eff_bank[j][:, :].rearrange("p (k c) -> p k c", k=CT),
                                        eff_scale[j], wqkv[:, 0, :, cols], ALU.mult, ALU.subtract).then_inc(eff_saved, 1)

            def low_xT(b):
                ve.wait_ge(xT_hi, at(b, 1))
                tt(flat(xT[:, 1, :, :]), front[:, 0:C], flat(xT[:, 0, :, :]), ALU.subtract).then_inc(xT_lo, 1)

            def normalise(b, dst):
                return ts(dst, feat(b), mv[:, bass.ds(b, 1), 0:1].rearrange("p a s -> p (a s)"),
                          rstd[:, bass.ds(b, 1)], ALU.subtract, ALU.mult)

            def norm1(b):
                ve.wait_ge(xhatT_ready, b)
                normalise(b, xhat[:, :]).then_inc(xhat_ready, 1)

            def rope(b):
                ve.wait_ge(qkc_saved, at(b, 1))
                rot = qk_ps[:, :].rearrange("p (h d) -> p h d", d=DH)[:, :, DE:]
                tt(rot1[:, :, :], rot, cos_t[:, :, :], ALU.mult).then_inc(s_rot1, 1)
                for i in range(2):
                    x = tt(rot2[:, :, i::2], rot[:, :, 1 - i::2], sin_t[:, :, i::2], ALU.mult)
                x.then_inc(s_rot2, 1)
                ve.wait_ge(s_rot1, at(b, 1))
                ve.wait_ge(s_rot2, at(b, 1))
                tt(qk[:, :, DE:], rot1[:, :, :], rot2[:, :, :], ALU.add).then_inc(rope_done, 1)

            def split_qk(b):
                ve.wait_ge(rope_done, at(b, 1))
                ve.wait_ge(qkT_ready, b)
                k = qk[:, H:, :]
                cp(parts[:, H:, 0:2 * DH].rearrange("p h (i d) -> p h i d", i=2),
                   k.unsqueeze(2).to_broadcast([P, H, 2, DH])).then_inc(k_hi, 1)
                ve.wait_ge(q_hi, at(b, 1))
                tt(parts[:, 0:H, DH:2 * DH], qk[:, 0:H, :], parts[:, 0:H, 0:DH], ALU.subtract).then_inc(q_lo, 1)
                ve.wait_ge(k_hi, at(b, 1))
                tt(parts[:, H:, 2 * DH:3 * DH], k, parts[:, H:, 0:DH], ALU.subtract).then_inc(parts_ready, 1)

            def low_v(b, p):
                ve.wait_ge(v_hi, at(b, 1))
                tt(vv[p][:, 1, :, 0:DH], v_ps[:, 0:C].rearrange("p (h d) -> p h d", d=DH), vv[p][:, 0, :, 0:DH],
                   ALU.subtract).then_inc(v_lo, 1)

            def save_qkT(b, p):
                ve.wait_ge(qkT_ready, at(b, 1))
                ve.wait_ge(T_ready[1], at(b, -1))
                for i in range(0, HP, HP // 2):
                    pairs, cols = slice(i, i + HP // 2), slice(i * P // 2, (i + HP // 2) * P // 2)
                    cp(kT[p][64:P, pairs, 1, :], qk_ps[64:P, cols].bitcast(F16).rearrange("p (i k) -> p i k", k=P))\
                        .then_inc(kT_odd_saved, 1)
                    cp(flat(qT[p][:, pairs, :]), front[:, cols].bitcast(F16)).then_inc(qT_saved, 1)

            def high_p(b):
                ve.wait_ge(exp_done[1], at(b, 1))
                ve.wait_ge(pv_done[1], b)
                cp(ph[:, 0, H // 2:, :], pT[:, H // 2:, :]).then_inc(p_hi[1], 1)

            def row_max(b, half):
                ve.wait_ge(S_ready[half], at(b, 1))
                if not half:
                    ve.wait_ge(mst_ready, b)
                ve.tensor_reduce(negmax[:, 8 * half:8 * half + 8],
                                 ring[half][:, :].rearrange("q (h k) -> q h k", h=8), AX.X, ALU.max,
                                 negate=True).then_inc(row_maxed[half], 1)

            def split_max(b):
                ve.wait_ge(row_maxed[0], at(b, 1))
                ve.wait_ge(row_maxed[1], at(b, 1))
                ve.wait_ge(mT_ready, b)
                cp(mst[:, 0:H], negmax[:, :]).then_inc(s_mhi, 1)
                ve.wait_ge(s_mhi, at(b, 1))
                tt(mst[:, H:2 * H], negmax[:, :], mst[:, 0:H], ALU.subtract).then_inc(mst_ready, 1)

            def divide(b):
                ve.wait_ge(pv_done[1], at(b, 1))
                y = tail[:, :].rearrange("q (h d) -> q h d", h=H)
                ve.reciprocal(rden[:, :], y[:, :, DH]).then_inc(s_rden, 1)
                ve.wait_ge(s_rden, at(b, 1))
                ve.wait_ge(ynT_ready, b)
                tt(yn[:, :, :], y[:, :, 0:DH], rden[:, :].unsqueeze(2).to_broadcast([P, H, DH]),
                   ALU.mult).then_inc(yn_ready, 1)

            def add_attention(b):
                ve.wait_ge(attn_ready, at(b, 1))
                tt(feat(b), tail[:, C:2 * C], feat(b), ALU.add).then_inc(h2_ready, 1)

            def early_roots():
                ve.wait_ge(s_stats2, NB - LATE)
                aggregate(range(NB - LATE), s_root, 1)
                inverse_roots(ve, s_root, 1, slice(0, NB - LATE))

            def step(b, p, has_front=True, has_tail=True, has_next=True, has_stats=True):
                n, o = at(b, 1), at(b, -1)
                row_max(b, 0)
                if has_tail:
                    high_p(o)
                if has_front:
                    low_xT(n)
                row_max(b, 1)
                split_max(b)
                if has_front:
                    rope(n)
                if has_tail:
                    divide(o)
                if has_front:
                    split_qk(n)
                    low_v(n, 1 - p)
                if has_next:
                    norm1(at(b, 2))
                if has_stats:
                    stats(at(b, -2), s_stats2)
                if not has_front:
                    early_roots()
                if has_front:
                    save_qkT(n, 1 - p)
                if has_tail:
                    add_attention(o)

            def low_quarter(e, p, i):
                src, hi, lo = quarter(p, i)
                ve.wait_ge(wsplit_hi, at(e * QUARTERS, i + 1))
                x = ve.scalar_tensor_tensor(lo, src, WSCALE, hi, ALU.mult, ALU.subtract)
                x.then_inc(wsplit_lo, 1)
                if i == QUARTERS - 1:
                    ts(b1e[p][:, :], b1[:, bass.ds(e, 1), :].rearrange("p a f -> p (a f)"), 1.0, None,
                       ALU.mult).then_inc(bias_ready, 1)

            ve.wait_ge(up_hi, 1)
            ve.scalar_tensor_tensor(up_parts[:, 1, :, :], up, DSCALE, up_parts[:, 0, :, :], ALU.mult, ALU.subtract)\
                .then_inc(up_lo, 1)
            for b in range(NB):
                ve.wait_ge(h_saved, b + 1)
                ve.bn_stats(st6[:, b, :], resid[:, b, :]).then_inc(s_stats, 1)
                if b >= 4:
                    c = slice(2 * (b - 4), 2 * (b - 3))
                    ve.wait_ge(wd_hi, b - 3)
                    ve.scalar_tensor_tensor(wd_parts[1][:, c, :], wdT[:, c, :], DSCALE, wd_parts[0][:, c, :],
                                            ALU.mult, ALU.subtract).then_inc(wd_lo, 1)
            ve.wait_ge(s_stats, NB)
            aggregate(range(NB), first_stats, 1)
            for j in range(3):
                low_eff(j)
            ve.wait_ge(first_root, ROOT_OPS)
            norm1(0)
            low_xT(0)
            ve.wait_ge(ld_const, 16 * 14)
            ve.wait_ge(zeroed, 2)
            rope(0)
            split_qk(0)
            low_v(0, 0)
            save_qkT(0, 0)
            norm1(1)
            ve.wait_ge(wr_hi, 1)
            ve.scalar_tensor_tensor(wr_parts[:, 1, :, :], wr[:, :, :], WSCALE, wr_parts[:, 0, :, :],
                                    ALU.mult, ALU.subtract).then_inc(wr_lo, 1)
            step(0, 0, has_tail=False, has_stats=False)
            step(1, 1, has_stats=False)
            step(2, 0)
            step(3, 1)
            with ve.Fori(4, NB - 3, 2) as b:
                step(b, 0)
                step(b + 1, 1)
            step(NB - 2, 0, has_next=False)
            step(NB - 1, 1, has_front=False, has_next=False)
            def norm2(g, p):
                ve.wait_ge(x2T_ready, at(g, -1))
                normalise(2 * g, x2[p][:, 0, :])
                normalise(at(2 * g, 1), x2[p][:, 1, :]).then_inc(x2_ready, 1)

            def low_x2T(g, p):
                ve.wait_ge(x2T_hi, at(g, 1))
                tt(x2T[p][:, 1, :, :, :].rearrange("p b k t -> p (b k t)"), (front, qk_ps)[p][:, :],
                   x2T[p][:, 0, :, :, :].rearrange("p b k t -> p (b k t)"), ALU.subtract).then_inc(x2T_lo, 1)

            stats(NB - 2, s_stats2)
            high_p(NB - 1)
            low_p(ve, NB - 1, 1)
            divide(NB - 1)
            norm2(0, 0)
            norm2(1, 1)
            add_attention(NB - 1)
            stats(NB - 1, s_stats2)

            ve.wait_ge(s_stats2, NB)
            aggregate(range(NB - LATE, NB), late_stats, 1)
            with ve.Fori(2, NB // 2 - 3, 2) as g:
                low_x2T(g - 2, 0)
                norm2(g, 0)
                low_x2T(g - 1, 1)
                norm2(g + 1, 1)
            low_x2T(NB // 2 - 4, 0)
            norm2(NB // 2 - 2, 0)
            low_x2T(NB // 2 - 3, 1)
            ve.wait_ge(late_root, ROOT_OPS)
            norm2(NB // 2 - 1, 1)
            low_x2T(NB // 2 - 2, 0)
            low_x2T(NB // 2 - 1, 1)
            order = [0]

            def chain(x):
                order[0] += 1
                x.then_inc(s_chain, 1)
                ve.wait_ge(s_chain, order[0])

            ve.wait_ge(logits_ready, NB // 2)
            lgs = v_ps[:, 0:NB * E].rearrange("p (b e) -> p b e", e=E)
            chain(ve.scalar_tensor_tensor(lg[:, :, :], lgs, 1.0 / WSCALE, rb[:, :].unsqueeze(1).to_broadcast([P, NB, E]),
                                          ALU.mult, ALU.add))
            chain(ve.tensor_reduce(lmax[:, :], lg[:, :, :], AX.X, ALU.max))
            tt(lg[:, :, :], lg[:, :, :], lmax[:, :].unsqueeze(2).to_broadcast([P, NB, E]),
               ALU.subtract).then_inc(logits_shifted, 1)
            ve.wait_ge(exp_logits_done, 1)
            chain(ve.tensor_reduce(lsum[:, :], lg[:, :, :], AX.X, ALU.add))
            chain(ve.reciprocal(lsum[:, :], lsum[:, :]))
            chain(tt(scores[:, :, :].rearrange("p e b -> p b e"), lg[:, :, :],
                     lsum[:, :].unsqueeze(2).to_broadcast([P, NB, E]), ALU.mult))
            cp(rows[:, :, C:], scores[:, :, :].rearrange("p e b -> p b e")).then_inc(scores_ready, 1)

            ve.memset(thr[:, :], 0).then_inc(s_thr, 1)
            cp(cand[:, :, :], bits[:, 0, :, :]).then_inc(s_cand, 1)
            all_scores = scores[:, :, :].rearrange("p e b -> p b e").unsqueeze(2).to_broadcast([P, NB, CANDS, E])

            for i in range(ROUNDS):
                ve.wait_ge(s_cand, i + 1)
                for lo, hi in (0, FIRST), (FIRST, NB):
                    tt(reach[:, lo:hi, :, :], all_scores[:, lo:hi, :, :],
                       cand[:, :, :].bitcast(F32).unsqueeze(1).to_broadcast([P, hi - lo, CANDS, E]),
                       ALU.is_ge).then_inc(s_cmp, 1)
                ve.wait_ge(s_thr, i + 1)
                tt(base[:, :, :], thr[:, :].unsqueeze(1).to_broadcast([P, CANDS, E]), bits[:, i + 1, :, :],
                   ALU.bitwise_or).then_inc(s_base, 1)
                ve.wait_ge(s_count, i + 1)
                ve.scalar_tensor_tensor(gain[:, :, :], front[:, 0:CANDS * E].rearrange("p (j e) -> p j e", e=E),
                                        float(CAP), bits[:, i, 0:1, :].to_broadcast([P, CANDS, E]),
                                        ALU.is_ge, ALU.mult).then_inc(s_gain, 1)
                ve.wait_ge(s_gain, i + 1)
                with nc.allow_low_precision(reason="GROUP bits of an integer, which float32 holds"):
                    ve.tensor_reduce(take[:, :], gain[:, :, :].rearrange("p j e -> p e j"), AX.X,
                                     ALU.add).then_inc(s_take, 1)
                ve.wait_ge(s_take, i + 1)
                ve.wait_ge(s_base, i + 1)
                tt(cand[:, :, :], base[:, :, :], take[:, :].unsqueeze(1).to_broadcast([P, CANDS, E]),
                   ALU.bitwise_or).then_inc(s_cand, 1)
                tt(thr[:, :], thr[:, :], take[:, :], ALU.bitwise_or).then_inc(s_thr, 1)
            ve.wait_ge(s_thr, ROUNDS + 1)

            def against(i, op):
                return tt(cls[:, i * E:(i + 1) * E, :], scores[:, :, :],
                          thr[:, :].bitcast(F32).unsqueeze(2).to_broadcast([P, E, NB]), op)

            against(0, ALU.is_gt)
            against(1, ALU.is_equal).then_inc(s_tie, 1)
            ve.wait_ge(s_tied, 1)
            chain(cp(flat(tot_sb[:, :, :]), front[:, 0:2 * P]))
            ve.tensor_reduce(cnt[:, :], tot_sb[:, 0:E, :], AX.X, ALU.add)
            chain(ve.tensor_tensor_scan(flat(before[:, :, :]), flat(seg[:, :, :]), flat(tot_sb[:, :, :]), 0.0,
                                        ALU.mult, ALU.add))
            ts(need[:, :], cnt[:, :], -1.0, float(CAP), ALU.mult, ALU.add)
            chain(tt(before[:, :, :], before[:, :, :], tot_sb[:, :, :], ALU.subtract))
            chain(tt(flat(before[:, :, :]), flat(before[:, :, :]), front[:, 2 * P:4 * P], ALU.add))
            needed = need[:, :].unsqueeze(2).to_broadcast([P, E, NB])
            tt(rank[:, :, :], before[:, E:, :], needed, ALU.min)
            chain(tt(tie_ok[:, :, :], before[:, E:, :], needed, ALU.is_lt))
            tt(rank[:, :, :], rank[:, :, :], before[:, 0:E, :], ALU.add)
            chain(tt(tie_ok[:, :, :], tie_ok[:, :, :], cls[:, E:, :], ALU.mult))
            chain(tt(sel[:, :, :], tie_ok[:, :, :], cls[:, 0:E, :], ALU.add))
            chain(ts(off[:, :, :], sel[:, :, :], -float(CAP), float(CAP), ALU.mult, ALU.add))
            chain(tt(slot[:, :, :], rank[:, :, :], off[:, :, :], ALU.add))
            ts(slot_lo_i[:, :, :], slot[:, :, :], P - 1, None, ALU.bitwise_and)
            chain(ts(slot_hi_i[:, :, :], slot[:, :, :], 7, None, ALU.logical_shift_right))
            cp(slot_lo[:, :, :], slot_lo_i[:, :, :])
            chain(cp(slot_hi[:, :, :], slot_hi_i[:, :, :]))

            def one_hot(e, p):
                ve.wait_ge(list_ready, at(e, -1))
                lo, hi = (t[:, bass.ds(e, 1), :].rearrange("p a b -> p (a b)") for t in (slot_lo, slot_hi))
                tt(hot_hi[p][:, :, :], hi.unsqueeze(2).to_broadcast([P, NB, ST]),
                   iota_hi[:, :].unsqueeze(1).to_broadcast([P, NB, ST]), ALU.is_equal).then_inc(hot_hi_ready, 1)
                tt(hot_lo[p][:, :, :], lo.unsqueeze(2).to_broadcast([P, NB, P]),
                   iota_lo[:, :].unsqueeze(1).to_broadcast([P, NB, P]), ALU.is_equal)
                ve.wait_ge(hot_hi_ready, at(e, 1))
                tt(hot_hi[p][:, :, :], hot_hi[p][:, :, :], tok_id[:, :].unsqueeze(2).to_broadcast([P, NB, ST]),
                   ALU.mult).then_inc(hot_ready, 1)

            def save_list(e, p):
                ve.wait_ge(list_ready, at(e, 1))
                cp(token_of[:, bass.ds(e, 1), :].rearrange("p a s -> p (a s)"), (front, qk_ps)[p][:, 0:ST])\
                    .then_inc(list_saved, 1)

            for e in (0, 1):
                one_hot(e, e)
                save_list(e, e)
            ve.wait_ge(ld_bias, 32)
            for i in range(QUARTERS):
                low_quarter(0, 0, i)

            def low_rows(e):
                for k in range(CT):
                    src = (tail if k else v_ps)[:, :]
                    ve.wait_ge(gT_hi, at(e * CT, k + 1))
                    tt(gT[1][:, k, :], src, gT[0][:, k, :], ALU.subtract).then_inc(gT_lo, 1)

            def split_hidden(e, f):
                ve.wait_ge(hid_hi, at(e * FT, f + 1))
                ve.wait_ge(relu_done, at(e * FT, f + 1))
                tt(hid[1][:, f, :], relu[:, f % 4, :], hid[0][:, f, :], ALU.subtract).then_inc(hid_lo, 1)

            def combine(e, p, t):
                ve.wait_ge(eo_ready, at(e * ST, t + 1))
                b2e = b2[:, bass.ds(e, 1), :].rearrange("p a c -> p (a c)")
                ve.wait_ge(contrib_ready, at(e * ST, t))
                ve.scalar_tensor_tensor(tmp[:, t % 2, :], out_bank[t][:, 0:C], 1.0 / WSCALE, b2e,
                                        ALU.mult, ALU.add).then_inc(s_eo, 1)
                ve.wait_ge(s_eo, at(e * ST, t + 1))
                ve.wait_ge(added, at(e * 64, 0))
                gate = got[p][:, t, C:].rearrange("p (a e) -> p a e", a=1)[:, 0, bass.ds(e, 1)]
                ts(contrib[:, t, :], tmp[:, t % 2, :], gate, None, ALU.mult).then_inc(contrib_ready, 1)

            def expert(e, p, last=False, lists=True):
                if lists:
                    one_hot(at(e, 2), p)
                for f in range(FT):
                    split_hidden(e, f)
                    if f == 6 and lists:
                        save_list(at(e, 2), p)
                if not last:
                    low_rows(at(e, 1))
                    low_quarter(at(e, 1), 1 - p, 0)
                for t in range(ST):
                    combine(e, p, t)
                    if t < ST - 1 and not last:
                        low_quarter(at(e, 1), 1 - p, t + 1)

            low_rows(0)
            expert(0, 0)
            expert(1, 1)
            with ve.Fori(2, E - 3, 2) as e:
                expert(e, 0)
                expert(e + 1, 1)
            expert(E - 2, 0, lists=False)
            expert(E - 1, 1, last=True, lists=False)

        @blk.scalar
        def _(sc):
            def copy(dst, src):
                return sc.activation(dst, src, ACT.Copy)

            def high_xT(b):
                sc.wait_ge(xhatT_ready, at(b, 1))
                sc.wait_ge(v_ready, b)
                copy(flat(xT[:, 0, :, :]), front[:, 0:C]).then_inc(xT_hi, 1)

            def save_qk(b):
                sc.wait_ge(qk_ready, at(b, 1))
                sc.wait_ge(parts_ready, b)
                sc.wait_ge(q_lo, b)
                sc.activation(qk[:, :, 0:DE], qk_ps[:, :].rearrange("p (h d) -> p h d", d=DH)[:, :, 0:DE], ACT.Copy,
                              scale=1.0 / QKSCALE).then_inc(qkc_saved, 1)

            def high_v(b, p):
                sc.wait_ge(v_ready, at(b, 1))
                sc.wait_ge(pv_done[1], at(b, -1))
                copy(vv[p][:, 0, :, 0:DH], v_ps[:, 0:C].rearrange("p (h d) -> p h d", d=DH)).then_inc(v_hi, 1)

            def high_q(b):
                sc.wait_ge(rope_done, at(b, 1))
                sc.wait_ge(qkT_ready, b)
                copy(parts[:, 0:H, :].rearrange("p h (i d) -> p h i d", d=DH)[:, :, 0:3:2, :],
                     qk[:, 0:H, :].unsqueeze(2).to_broadcast([P, H, 2, DH])).then_inc(q_hi, 1)

            def save_kT(b, p):
                sc.wait_ge(qkT_ready, at(b, 1))
                sc.wait_ge(T_ready[1], at(b, -1))
                for i in range(0, HP, HP // 2):
                    pairs, cols = slice(i, i + HP // 2), slice(i * P // 2, (i + HP // 2) * P // 2)
                    copy(kT[p][0:64, pairs, 0, :], qk_ps[0:64, cols].bitcast(F16).rearrange("p (i k) -> p i k", k=P))\
                        .then_inc(kT_even_saved, 1)

            def save_mT(b):
                sc.wait_ge(mT_ready, at(b, 1))
                sc.wait_ge(T_ready[1], b)
                copy(mT[:, :], mT_ps).then_inc(mT_saved, 1)

            def exp_high(b):
                sc.wait_ge(T_ready[0], at(b, 1))
                sc.wait_ge(pv_done[0], b)
                sc.activation(flat(ph[:, 0, 0:H // 2, :]), ring[0][:, :], ACT.Exp,
                              bias=lift[:, :]).then_inc(p_hi[0], 1)

            def exp(b, half):
                sc.wait_ge(T_ready[half], at(b, 1))
                sc.wait_ge(p_lo[half], b)
                sc.activation(flat(pT[:, 8 * half:8 * half + 8, :]), ring[half][:, :], ACT.Exp,
                              bias=lift[:, :]).then_inc(exp_done[half], 1)

            def save_ynT(b):
                sc.wait_ge(ynT_ready, at(b, 1))
                sc.wait_ge(attn_ready, b)
                copy(flat(ynT[:, :, :]), tail[:, 0:C]).then_inc(ynT_saved, 1)

            def high_x2T(g, p):
                sc.wait_ge(x2T_ready, at(g, 1))
                sc.wait_ge(logits_ready, at(g, -1))
                copy(x2T[p][:, 0, :, :, :].rearrange("p b k t -> p (b k t)"), (front, qk_ps)[p][:, :]).then_inc(x2T_hi, 1)

            def high_quarter(e, p, i):
                src, hi, lo = quarter(p, i)
                if i == 0:
                    sc.wait_ge(w1_in, at(e * 16, 16))
                    sc.wait_ge(w2_in, at(e * 16, 16))
                    sc.wait_ge(eo_ready, at(e * ST, -ST))
                sc.activation(hi, src, ACT.Copy, scale=WSCALE).then_inc(wsplit_hi, 1)

            def high_rows(e):
                for k in range(CT):
                    sc.wait_ge(gT_ready, at(e * CT, k + 1))
                    sc.wait_ge(h1_ready, e * FT)
                    copy(gT[0][:, k, :], (tail if k else v_ps)[:, :]).then_inc(gT_hi, 1)

            def step(b, p, has_front=True, has_tail=True):
                n, o = at(b, 1), at(b, -1)
                if has_front:
                    high_xT(n)
                if has_front:
                    save_qk(n)
                save_mT(b)
                if has_front:
                    high_v(n, 1 - p)
                    high_q(n)
                exp_high(b)
                exp(b, 0)
                if has_tail:
                    save_ynT(o)
                if has_front:
                    save_kT(n, 1 - p)
                exp(b, 1)

            sc.wait_ge(ld_up, 16)
            sc.activation(up_parts[:, 0, :, :], up, ACT.Copy, scale=DSCALE).then_inc(up_hi, 1)
            for b in range(NB):
                sc.wait_ge(conv_ready, b + 1)
                copy(resid[:, b, :], (front, qk_ps)[b % 2][:, 0:C]).then_inc(h_saved, 1)
                if b >= 4:
                    c = slice(2 * (b - 4), 2 * (b - 3))
                    sc.wait_ge(ld_down[(b - 4) // 4], 16)
                    sc.activation(wd_parts[0][:, c, :], wdT[:, c, :], ACT.Copy, scale=DSCALE).then_inc(wd_hi, 1)
            for j in range(3):
                sc.wait_ge(eff_ready, j + 1)
                sc.activation(wqkv[:, 0, :, j * C:(j + 1) * C], eff_bank[j][:, :].rearrange("p (k c) -> p k c", k=CT),
                              ACT.Copy, scale=eff_scale[j]).then_inc(eff_hi, 1)
            high_xT(0)
            sc.wait_ge(zeroed, 2)
            save_qk(0)
            high_v(0, 0)
            high_q(0)
            save_kT(0, 0)
            sc.activation(wr_parts[:, 0, :, :], wr[:, :, :], ACT.Copy, scale=WSCALE).then_inc(wr_hi, 1)
            step(0, 0, has_tail=False)
            step(1, 1)
            with sc.Fori(2, NB - 3, 2) as b:
                step(b, 0)
                step(b + 1, 1)
            step(NB - 2, 0)
            step(NB - 1, 1, has_front=False)
            save_ynT(NB - 1)
            high_x2T(0, 0)
            high_x2T(1, 1)
            with sc.Fori(2, NB // 2 - 1, 2) as g:
                high_x2T(g, 0)
                high_x2T(g + 1, 1)
            sc.wait_ge(logits_shifted, 1)
            sc.activation(flat(lg[:, :, :]), flat(lg[:, :, :]), ACT.Exp).then_inc(exp_logits_done, 1)

            def rectify(e, p, f):
                if f == 0:
                    sc.wait_ge(bias_ready, at(e, 1))
                sc.wait_ge(h1_ready, at(e * FT, f + 1))
                h1, bias = ring[f % 4 // 2][:, (f % 2) * 512:(f % 2 + 1) * 512], b1e[p][:, f:f + 1]
                sc.wait_ge(eo_ready, at(e * ST, 0))
                sc.activation(hid[0][:, f, :], h1, ACT.Relu, bias=bias, scale=1.0 / WSCALE).then_inc(hid_hi, 1)
                if f >= 4:
                    sc.wait_ge(hid_lo, at(e * FT, f - 3))
                else:
                    sc.wait_ge(hid_lo, e * FT)
                sc.activation(relu[:, f % 4, :], h1, ACT.Relu, bias=bias, scale=1.0 / WSCALE).then_inc(relu_done, 1)

            def expert(e, p, last=False):
                for f in range(FT):
                    rectify(e, p, f)
                if not last:
                    high_rows(at(e, 1))
                    for i in range(QUARTERS):
                        high_quarter(at(e, 1), 1 - p, i)

            for i in range(QUARTERS):
                high_quarter(0, 0, i)
            high_rows(0)
            expert(0, 0)
            expert(1, 1)
            with sc.Fori(2, E - 3, 2) as e:
                expert(e, 0)
                expert(e + 1, 1)
            expert(E - 2, 0)
            expert(E - 1, 1, last=True)

        @blk.gpsimd
        def _(gp):
            def gather(e, p):
                gp.wait_ge(list_saved, e + 1)
                gp.wait_ge(got_in, e * 64)
                gp.wait_ge(contrib_ready, at(e * ST, -ST))
                gp.wait_ge(gT_ready, at(e * CT, -CT))
                for t in range(ST):
                    gp.indirect_dma_start(got[p][:, t, :], None, table,
                                          bass.IndirectOffsetOnAxis(ap=token_of[:, e, t:t + 1], axis=0)).then_inc(got_in, 16)

            def add(e, p, t):
                gp.wait_ge(contrib_ready, at(e * ST, t + 1))
                if t == 0:
                    gp.wait_ge(added, e * 64)
                gp.indirect_dma_start(out_rows, bass.IndirectOffsetOnAxis(ap=token_of[:, e, t:t + 1], axis=0),
                                      contrib[:, t, :], None, compute_op=ALU.add).then_inc(added, 16)

            def expert(e, p, last=False):
                if not last:
                    gather(at(e, 1), 1 - p)
                for t in range(ST):
                    add(e, p, t)

            for i in range(2):
                gp.memset(vv[i][:, :, :, :], 0.0)
            gp.memset(flat(parts[:, :, :]).bitcast(F32), 0.0)
            for i in range(2):
                gp.memset(kT[i][:, :, :, :].rearrange("p i j k -> p (i j k)").bitcast(F32), 0.0)
            gp.memset(mst[:, :], 0.0)
            gp.memset(spare_ve[:, :], 0.0)
            gp.memset(lift[:, :], LIFT)
            gp.memset(ones_bf[:, :], 1.0).then_inc(zeroed, 1)
            gp.wait_ge(zeroed, 1)
            for i in range(2):
                x = gp.memset(vv[i][:, 0, :, DH], VSCALE)
            x.then_inc(zeroed, 1)
            gp.wait_ge(first_stats, 1)
            inverse_roots(gp, first_root, 0, slice(0, NB))
            gp.wait_ge(ld_const, 16 * 14)
            gp.tensor_copy(ident_h[:, :], ident[:, :])
            gp.tensor_copy(ident_bf[:, :], ident[:, :])
            for i, dst in enumerate((mask_qk, mask_kq, lower)):
                gp.tensor_copy(dst[:, :], raw[:, i, :])
            gp.tensor_tensor(pick[:, :, :], ident[:, 0:H].unsqueeze(2).to_broadcast([P, H, P]),
                             ident[:, H:2 * H].unsqueeze(2).to_broadcast([P, H, P]), ALU.add).then_inc(bf_ready, 1)

            with gp.Fori(0, NB - 1) as b:
                low_p(gp, b, 0)
                low_p(gp, b, 1)
            low_p(gp, NB - 1, 0)
            gp.wait_ge(late_stats, 1)
            inverse_roots(gp, late_root, 0, slice(NB - LATE, NB))
            gp.wait_ge(s_root, ROOT_OPS + 1)
            for b in range(NB):
                x = gp.tensor_scalar(rows[:, b, 0:C], resid[:, b, :], mv[:, b, 0:1], rstd[:, b:b + 1],
                                     ALU.subtract, ALU.mult)
            x.then_inc(rows_ready, 1)
            gp.wait_ge(table_in, 16)
            gather(0, 0)
            gp.wait_ge(resid_out, 16 * NB)
            for e in range(E):
                expert(e, e % 2, last=e == E - 1)


def constants():
    i = np.arange(P)
    eye = np.eye(P, dtype=np.float32)
    later = i[None, :] > i[:, None]
    inv = (np.float32(1.0) / np.float32(10000.0) ** (np.arange(0, DE, 2, dtype=np.float32) / np.float32(DE))).astype(np.float32)
    ang = np.arange(T, dtype=np.float32)[:, None] * np.concatenate([inv, inv])[None, :]
    cos, sin = np.cos(ang).astype(np.float32), np.sin(ang).astype(np.float32)
    sin[:, 0::2] *= -1.0
    seg = np.ones((P, 2 * E, NB), np.float32)
    seg[:, :, 0] = 0.0
    bits = np.zeros((P, ROUNDS + 1, CANDS, E), np.int32)
    for r in range(ROUNDS):
        for j in range(CANDS):
            bits[:, r, j, :] = (j + 1) << (GROUP * (ROUNDS - 1 - r))
    return {
        "ident": eye,
        "mask_qk": np.where(later, np.float32(MASKED), np.float32(0)),
        "mask_kq": np.where(later.T, np.float32(MASKED), np.float32(0)),
        "cos": np.tile(cos, (1, 2 * H)) * np.float32(1 / QKSCALE), "sin": np.tile(sin, (1, 2 * H)) * np.float32(1 / QKSCALE),
        "lower": later.astype(np.float32),
        "iota_lo": np.tile(i.astype(np.float16), (P, 1)),
        "iota_hi": np.tile(np.arange(ST, dtype=np.float16), (P, 1)),
        "tok_id": (np.arange(NB)[None, :] * P + i[:, None]).astype(np.float32),
        "seg": seg.reshape(P, -1), "bits": bits.reshape(P, -1),
    }


def kernel(**inputs):
    import concourse.bacc as _bacc
    from concourse.bass_utils import run_bass_kernel_spmd as _run

    g = {k: np.ascontiguousarray(v) for k, v in inputs.items()}
    x, we, be = g["x"], g["L0_tok_W_embed"], g["L0_tok_b_embed"]
    xp = np.zeros((NB, CIN, x.shape[2] + TAPS - 1), x.dtype)
    xp[:, :, TAPS // 2:TAPS // 2 + x.shape[2]] = x
    xwin = np.stack([xp[:, c, j:j + DS * C:DS] for c in range(CIN) for j in range(WIN)]
                    + [np.ones((NB, C), x.dtype)] * 2)
    band = np.zeros((DS * CMID, KWIN + 1), we.dtype)
    for i in range(DS):
        for c in range(CIN):
            band[i * CMID:(i + 1) * CMID, c * WIN + i:c * WIN + i + TAPS] = we[:, c, :]
        band[i * CMID:(i + 1) * CMID, KWIN] = be
    up = np.zeros((P, 3, 2 * DH), np.float32)
    ups = [np.concatenate([g["L0_attn_Wq_up_c"], g["L0_attn_Wq_up_e"]], 1),
           np.concatenate([g["L0_attn_Wk_up_c"], g["L0_attn_Wk_up_e"]], 1), g["L0_attn_Wv_up"]]
    for j in range(3):
        for i in range(2):
            up[i * L:(i + 1) * L, j, i * DH:(i + 1) * DH] = ups[j]
    arrays = {
        "xwin": xwin.reshape(KX, NB * C), "band": band,
        "wpT": np.ascontiguousarray(g["L0_tok_W_proj"][:, :, 0].T), "bp": g["L0_tok_b_proj"],
        "wdT": np.concatenate([g["L0_attn_Wq_down"].T, g["L0_attn_Wk_down"].T, g["L0_attn_Wv_down"].T]),
        "up": up.reshape(P, -1), "wc": g["L0_attn_Wc"], "wr": g["L0_ffn_router_w"], "rb": g["L0_ffn_router_b"],
        "w1": g["L0_ffn_w1"], "b1": g["L0_ffn_b1"].reshape(E, FT, P).transpose(2, 0, 1).reshape(P, E * FT), "w2": g["L0_ffn_w2"], "b2": g["L0_ffn_b2"],
        **constants(),
    }
    arrays = {k: np.ascontiguousarray(v) for k, v in arrays.items()}
    nc = _bacc.Bacc("TRN2", target_bir_lowering=False, num_devices=1)
    a = {k: nc.dram_tensor(f"in_{k}", v.shape, mybir.dt.from_np(v.dtype), kind="ExternalInput").ap()
         for k, v in arrays.items()}
    out = nc.dram_tensor("out_0", (NB, T, C), F32, kind="ExternalOutput").ap()
    table = nc.dram_tensor("token_rows", (NB * T, ROW), F32, kind="Internal").ap()
    build(nc, a, out, table)
    r = _run(nc, [{f"in_{k}": v for k, v in arrays.items()}], core_ids=[0])
    return r.results[0]["out_0"]
```
